# Optimizing a Trainium2 kernel written in Bass

```python
import numpy as np
import jax
import jax.numpy as jnp

def _softmax(x, axis=-1):
    return jax.nn.softmax(x, axis=axis)

def _gelu(x):
    return jax.nn.gelu(x, approximate=True)

def _silu(x):
    return jax.nn.silu(x)

def _sigmoid(x):
    return jax.nn.sigmoid(x)

def _layernorm(x, axis=-1, eps=1e-05):
    m = jnp.mean(x, axis=axis, keepdims=True)
    v = jnp.var(x, axis=axis, keepdims=True)
    return (x - m) / jnp.sqrt(v + eps)

def _scatter_add(tgt, idx, src, axis=0):
    return tgt.at[idx].add(src)

def _segment_sum(src, seg, n):
    return jax.ops.segment_sum(src, seg, n)
kernel_name = 'mk_sandwich_d1_jaxref_r8_4d51bd'

def setup_inputs(seed: int=0):
    np.random.seed(seed)
    _w = jnp.asarray

    def _L0_attn_setup():
        import jax, jax.numpy as jnp
        import numpy as np
        EMBED_DIM = 128
        NUM_HEADS = 16
        HEAD_DIM = EMBED_DIM // NUM_HEADS
        ROPE_BASE = 10000.0

        def _rope(t):
            hd = t.shape[-1]
            half = hd // 2
            S = t.shape[2]
            inv_freq = 1.0 / ROPE_BASE ** (jnp.arange(half, dtype=jnp.float32) / half)
            ang = jnp.arange(S, dtype=jnp.float32)[:, None] * inv_freq[None, :]
            cos, sin = (jnp.cos(ang), jnp.sin(ang))
            t1, t2 = (t[..., :half], t[..., half:])
            return jnp.concatenate([t1 * cos - t2 * sin, t1 * sin + t2 * cos], axis=-1)

        def _attention_mc(x, Wq, Wk, Wv, Wo):
            B, S, D = x.shape
            H, hd = (NUM_HEADS, HEAD_DIM)
            q = (x @ Wq.T).reshape(B, S, H, hd).transpose(0, 2, 1, 3)
            k = (x @ Wk.T).reshape(B, S, H, hd).transpose(0, 2, 1, 3)
            v = (x @ Wv.T).reshape(B, S, H, hd).transpose(0, 2, 1, 3)
            q = _rope(q)
            k = _rope(k)
            scale = 1.0 / jnp.sqrt(jnp.float32(hd))
            scores = jnp.einsum('bhqd,bhkd->bhqk', q, k) * scale
            causal = jnp.tril(jnp.ones((S, S), dtype=bool))
            scores = jnp.where(causal, scores, jnp.finfo(scores.dtype).min)
            attn = jax.nn.softmax(scores, axis=-1)
            out = jnp.einsum('bhqk,bhkd->bhqd', attn, v)
            out = out.transpose(0, 2, 1, 3).reshape(B, S, D)
            return out @ Wo.T
        key = jax.random.key(seed)
        ks = jax.random.split(key, 5)
        B, S, D = (2, 256, EMBED_DIM)
        bound = 1.0 / np.sqrt(D)
        x = jax.random.normal(ks[0], (B, S, D), dtype=jnp.float32)
        Wq = jax.random.uniform(ks[1], (D, D), dtype=jnp.float32, minval=-bound, maxval=bound)
        Wk = jax.random.uniform(ks[2], (D, D), dtype=jnp.float32, minval=-bound, maxval=bound)
        Wv = jax.random.uniform(ks[3], (D, D), dtype=jnp.float32, minval=-bound, maxval=bound)
        Wo = jax.random.uniform(ks[4], (D, D), dtype=jnp.float32, minval=-bound, maxval=bound)
        return {'x': x, 'Wq': Wq, 'Wk': Wk, 'Wv': Wv, 'Wo': Wo}
    _L0_attn_in = _L0_attn_setup()

    def _L0_ffn_setup():
        import jax, jax.numpy as jnp
        import numpy as np
        B, T, C = (2, 256, 128)
        H, D = (16, 64)
        CR = 8
        R = C // CR
        ROPE = D // 2
        NOPE = D - ROPE
        E, K, I, S = (8, 2, 64, 1)
        THETA = 100000.0
        EPS = 1e-05

        def _rmsnorm(x, w):
            rms = jnp.sqrt(jnp.mean(x * x, axis=-1, keepdims=True) + EPS)
            return w * (x / rms)

        def _rope(xh):
            d = xh.shape[-1]
            t = jnp.arange(xh.shape[2], dtype=jnp.float32)
            freqs = 1.0 / THETA ** (jnp.arange(0, d, 2, dtype=jnp.float32) / d)
            ang = jnp.outer(t, freqs)
            cos, sin = (jnp.cos(ang), jnp.sin(ang))
            xr = xh.reshape(xh.shape[:-1] + (d // 2, 2))
            x0, x1 = (xr[..., 0], xr[..., 1])
            rot = jnp.stack([x0 * cos - x1 * sin, x0 * sin + x1 * cos], axis=-1)
            return rot.reshape(xh.shape)

        def _attention(x, Wq, Wkva, Wkvb, Wo):
            b, t, _ = x.shape
            q = (x @ Wq).reshape(b, t, H, D).transpose(0, 2, 1, 3)
            ckv = x @ Wkva
            kv_latent, k_rope = (ckv[:, :, :R], ckv[:, :, R:])
            kv = (kv_latent @ Wkvb).reshape(b, t, H, NOPE).transpose(0, 2, 1, 3)
            k_rope = jnp.broadcast_to(k_rope[:, None, :, :], (b, H, t, ROPE))
            q_nope, q_rope = (q[..., :NOPE], q[..., NOPE:])
            q = jnp.concatenate([q_nope, _rope(q_rope)], axis=-1)
            k = jnp.concatenate([kv, _rope(k_rope)], axis=-1)
            v = jnp.concatenate([kv, jnp.zeros_like(k_rope)], axis=-1)
            att = jnp.einsum('bhqd,bhkd->bhqk', q, k) / jnp.sqrt(jnp.float32(D))
            mask = jnp.tril(jnp.ones((t, t), dtype=bool))
            att = jnp.where(mask, att, jnp.float32(-jnp.inf))
            att = jax.nn.softmax(att, axis=-1)
            y = jnp.einsum('bhqk,bhkd->bhqd', att, v)
            y = y.transpose(0, 2, 1, 3).reshape(b, t, H * D)
            return y @ Wo

        def _experts(x_flat, Wg, Wu, Wd):
            g = jax.nn.silu(jnp.einsum('nc,eci->nei', x_flat, Wg))
            u = jnp.einsum('nc,eci->nei', x_flat, Wu)
            return jnp.einsum('nei,eic->nec', g * u, Wd)

        def _moe(x, Wgate, expert_bias, Wg, Wu, Wd, sWg, sWu, sWd):
            b, t, c = x.shape
            xf = x.reshape(-1, c)
            shared = jnp.mean(_experts(xf, sWg, sWu, sWd), axis=1)
            logits = xf @ Wgate + expert_bias
            probs = jax.nn.softmax(logits, axis=-1)
            topk_p, topk_i = jax.lax.top_k(probs, K)
            topk_p = topk_p / jnp.sum(topk_p, axis=-1, keepdims=True)
            comb = jnp.sum(jax.nn.one_hot(topk_i, E, dtype=xf.dtype) * topk_p[..., None], axis=1)
            routed = jnp.einsum('ne,nec->nc', comb, _experts(xf, Wg, Wu, Wd))
            return (shared + routed).reshape(b, t, c)
        key = jax.random.key(seed)
        ks = jax.random.split(key, 16)
        w = lambda k, shp: jax.random.normal(k, shp, dtype=jnp.float32) * 0.02
        return {'x': jax.random.normal(ks[0], (B, T, C), dtype=jnp.float32), 'w_ln1': jnp.ones((C,), jnp.float32), 'Wq': w(ks[1], (C, H * D)), 'Wkva': w(ks[2], (C, R + ROPE)), 'Wkvb': w(ks[3], (R, H * NOPE)), 'Wo': w(ks[4], (H * D, C)), 'w_ln2': jnp.ones((C,), jnp.float32), 'Wgate': w(ks[5], (C, E)), 'expert_bias': jnp.zeros((E,), jnp.float32), 'Wg': w(ks[6], (E, C, I)), 'Wu': w(ks[7], (E, C, I)), 'Wd': w(ks[8], (E, I, C)), 'sWg': w(ks[9], (S, C, I)), 'sWu': w(ks[10], (S, C, I)), 'sWd': w(ks[11], (S, I, C))}
    _L0_ffn_in = _L0_ffn_setup()
    _d = {'L0_attn_x': _L0_attn_in['x'], 'L0_attn_Wq': _L0_attn_in['Wq'], 'L0_attn_Wk': _L0_attn_in['Wk'], 'L0_attn_Wv': _L0_attn_in['Wv'], 'L0_attn_Wo': _L0_attn_in['Wo'], 'L0_ffn_w_ln1': _L0_ffn_in['w_ln1'], 'L0_ffn_Wq': _L0_ffn_in['Wq'], 'L0_ffn_Wkva': _L0_ffn_in['Wkva'], 'L0_ffn_Wkvb': _L0_ffn_in['Wkvb'], 'L0_ffn_Wo': _L0_ffn_in['Wo'], 'L0_ffn_w_ln2': _L0_ffn_in['w_ln2'], 'L0_ffn_Wgate': _L0_ffn_in['Wgate'], 'L0_ffn_expert_bias': _L0_ffn_in['expert_bias'], 'L0_ffn_Wg': _L0_ffn_in['Wg'], 'L0_ffn_Wu': _L0_ffn_in['Wu'], 'L0_ffn_Wd': _L0_ffn_in['Wd'], 'L0_ffn_sWg': _L0_ffn_in['sWg'], 'L0_ffn_sWu': _L0_ffn_in['sWu'], 'L0_ffn_sWd': _L0_ffn_in['sWd']}
    _x0 = _d['L0_attn_x']
    _d['L0_attn_x'] = jax.random.normal(jax.random.fold_in(jax.random.key(seed), 1), (4, 512, 128), dtype=_x0.dtype)
    del _x0
    return _d

def reference(L0_attn_x, L0_attn_Wq, L0_attn_Wk, L0_attn_Wv, L0_attn_Wo, L0_ffn_w_ln1, L0_ffn_Wq, L0_ffn_Wkva, L0_ffn_Wkvb, L0_ffn_Wo, L0_ffn_w_ln2, L0_ffn_Wgate, L0_ffn_expert_bias, L0_ffn_Wg, L0_ffn_Wu, L0_ffn_Wd, L0_ffn_sWg, L0_ffn_sWu, L0_ffn_sWd):

    def _L0_attn_ref(x, Wq, Wk, Wv, Wo):
        import jax, jax.numpy as jnp
        import numpy as np
        EMBED_DIM = 128
        NUM_HEADS = 16
        HEAD_DIM = EMBED_DIM // NUM_HEADS
        ROPE_BASE = 10000.0

        def _rope(t):
            hd = t.shape[-1]
            half = hd // 2
            S = t.shape[2]
            inv_freq = 1.0 / ROPE_BASE ** (jnp.arange(half, dtype=jnp.float32) / half)
            ang = jnp.arange(S, dtype=jnp.float32)[:, None] * inv_freq[None, :]
            cos, sin = (jnp.cos(ang), jnp.sin(ang))
            t1, t2 = (t[..., :half], t[..., half:])
            return jnp.concatenate([t1 * cos - t2 * sin, t1 * sin + t2 * cos], axis=-1)

        def _attention_mc(x, Wq, Wk, Wv, Wo):
            B, S, D = x.shape
            H, hd = (NUM_HEADS, HEAD_DIM)
            q = (x @ Wq.T).reshape(B, S, H, hd).transpose(0, 2, 1, 3)
            k = (x @ Wk.T).reshape(B, S, H, hd).transpose(0, 2, 1, 3)
            v = (x @ Wv.T).reshape(B, S, H, hd).transpose(0, 2, 1, 3)
            q = _rope(q)
            k = _rope(k)
            scale = 1.0 / jnp.sqrt(jnp.float32(hd))
            scores = jnp.einsum('bhqd,bhkd->bhqk', q, k) * scale
            causal = jnp.tril(jnp.ones((S, S), dtype=bool))
            scores = jnp.where(causal, scores, jnp.finfo(scores.dtype).min)
            attn = jax.nn.softmax(scores, axis=-1)
            out = jnp.einsum('bhqk,bhkd->bhqd', attn, v)
            out = out.transpose(0, 2, 1, 3).reshape(B, S, D)
            return out @ Wo.T
        return _attention_mc(x, Wq, Wk, Wv, Wo)

    def _L0_ffn_ref(x, w_ln1, Wq, Wkva, Wkvb, Wo, w_ln2, Wgate, expert_bias, Wg, Wu, Wd, sWg, sWu, sWd):
        import jax, jax.numpy as jnp
        import numpy as np
        B, T, C = (2, 256, 128)
        H, D = (16, 64)
        CR = 8
        R = C // CR
        ROPE = D // 2
        NOPE = D - ROPE
        E, K, I, S = (8, 2, 64, 1)
        THETA = 100000.0
        EPS = 1e-05

        def _rmsnorm(x, w):
            rms = jnp.sqrt(jnp.mean(x * x, axis=-1, keepdims=True) + EPS)
            return w * (x / rms)

        def _rope(xh):
            d = xh.shape[-1]
            t = jnp.arange(xh.shape[2], dtype=jnp.float32)
            freqs = 1.0 / THETA ** (jnp.arange(0, d, 2, dtype=jnp.float32) / d)
            ang = jnp.outer(t, freqs)
            cos, sin = (jnp.cos(ang), jnp.sin(ang))
            xr = xh.reshape(xh.shape[:-1] + (d // 2, 2))
            x0, x1 = (xr[..., 0], xr[..., 1])
            rot = jnp.stack([x0 * cos - x1 * sin, x0 * sin + x1 * cos], axis=-1)
            return rot.reshape(xh.shape)

        def _attention(x, Wq, Wkva, Wkvb, Wo):
            b, t, _ = x.shape
            q = (x @ Wq).reshape(b, t, H, D).transpose(0, 2, 1, 3)
            ckv = x @ Wkva
            kv_latent, k_rope = (ckv[:, :, :R], ckv[:, :, R:])
            kv = (kv_latent @ Wkvb).reshape(b, t, H, NOPE).transpose(0, 2, 1, 3)
            k_rope = jnp.broadcast_to(k_rope[:, None, :, :], (b, H, t, ROPE))
            q_nope, q_rope = (q[..., :NOPE], q[..., NOPE:])
            q = jnp.concatenate([q_nope, _rope(q_rope)], axis=-1)
            k = jnp.concatenate([kv, _rope(k_rope)], axis=-1)
            v = jnp.concatenate([kv, jnp.zeros_like(k_rope)], axis=-1)
            att = jnp.einsum('bhqd,bhkd->bhqk', q, k) / jnp.sqrt(jnp.float32(D))
            mask = jnp.tril(jnp.ones((t, t), dtype=bool))
            att = jnp.where(mask, att, jnp.float32(-jnp.inf))
            att = jax.nn.softmax(att, axis=-1)
            y = jnp.einsum('bhqk,bhkd->bhqd', att, v)
            y = y.transpose(0, 2, 1, 3).reshape(b, t, H * D)
            return y @ Wo

        def _experts(x_flat, Wg, Wu, Wd):
            g = jax.nn.silu(jnp.einsum('nc,eci->nei', x_flat, Wg))
            u = jnp.einsum('nc,eci->nei', x_flat, Wu)
            return jnp.einsum('nei,eic->nec', g * u, Wd)

        def _moe(x, Wgate, expert_bias, Wg, Wu, Wd, sWg, sWu, sWd):
            b, t, c = x.shape
            xf = x.reshape(-1, c)
            shared = jnp.mean(_experts(xf, sWg, sWu, sWd), axis=1)
            logits = xf @ Wgate + expert_bias
            probs = jax.nn.softmax(logits, axis=-1)
            topk_p, topk_i = jax.lax.top_k(probs, K)
            topk_p = topk_p / jnp.sum(topk_p, axis=-1, keepdims=True)
            comb = jnp.sum(jax.nn.one_hot(topk_i, E, dtype=xf.dtype) * topk_p[..., None], axis=1)
            routed = jnp.einsum('ne,nec->nc', comb, _experts(xf, Wg, Wu, Wd))
            return (shared + routed).reshape(b, t, c)
        x = x + _attention(_rmsnorm(x, w_ln1), Wq, Wkva, Wkvb, Wo)
        residual = x
        xn = _rmsnorm(x, w_ln2)
        x_out = _moe(xn, Wgate, expert_bias, Wg, Wu, Wd, sWg, sWu, sWd)
        return residual + x_out
    x = L0_attn_x
    x = x + _layernorm(_L0_attn_ref(_layernorm(x, axis=-1), L0_attn_Wq, L0_attn_Wk, L0_attn_Wv, L0_attn_Wo), axis=-1)
    x = x + _layernorm(_L0_ffn_ref(_layernorm(x, axis=-1), L0_ffn_w_ln1, L0_ffn_Wq, L0_ffn_Wkva, L0_ffn_Wkvb, L0_ffn_Wo, L0_ffn_w_ln2, L0_ffn_Wgate, L0_ffn_expert_bias, L0_ffn_Wg, L0_ffn_Wu, L0_ffn_Wd, L0_ffn_sWg, L0_ffn_sWu, L0_ffn_sWd), axis=-1)
    return x

_drawn_inputs = setup_inputs


def setup_inputs(seed=0):
    import zlib

    import numpy as np

    out = dict(_drawn_inputs(seed))
    spreads = {'L0_ffn_w_ln1': (1.0, 0.6), 'L0_ffn_w_ln2': (1.0, 0.6), 'L0_ffn_expert_bias': (0.0, 0.8)}
    factors = {'L0_ffn_Wq': 8.0,
     'L0_ffn_Wkva': 8.0,
     'L0_ffn_Wkvb': 8.0,
     'L0_ffn_Wo': 8.0,
     'L0_ffn_Wgate': 8.0,
     'L0_ffn_Wg': 8.0,
     'L0_ffn_Wu': 8.0,
     'L0_ffn_Wd': 8.0,
     'L0_ffn_sWg': 8.0,
     'L0_ffn_sWu': 8.0,
     'L0_ffn_sWd': 8.0}
    for name, (base, spread) in spreads.items():
        noise = np.random.default_rng([zlib.crc32(name.encode()), seed]).standard_normal(out[name].shape)
        drawn = base * np.exp(spread * noise) if base else spread * noise
        out[name] = jnp.asarray(drawn.astype(out[name].dtype))
    for name, factor in factors.items():
        out[name] = (out[name] * factor).astype(out[name].dtype)
    return out
```

```python
from contextlib import ExitStack

import concourse.bass as bass
from concourse import mybir

F32 = mybir.dt.float32
F32R = mybir.dt.float32r
BF16 = mybir.dt.bfloat16
ALU = mybir.AluOpType
ACT = mybir.ActivationFunctionType
AX = mybir.AxisListType

P = 128
B, T, C = 4, 512, 128
NT = T // P
H = 16
G, HG = 4, 4
D1 = C // H
NOPE, ROPE, LAT = 32, 32, 16
D2 = NOPE + ROPE
DK2 = LAT + ROPE
E, I = 8, 64
EPS = 1e-5
MROW = 96
NEG = -1e30
FILLS = 12


class Signal:

    def __init__(self, sem, per, base=0):
        self.sem, self.per, self.base = sem, per, base

    def __call__(self, it, n):
        return self.sem, it * self.per + (self.base + n)


def block_program(nc, x, x_ahead, wqkv, wo1, wkva, wq_nope, wq_rope, wkvb, wo2, ln1w, ln2w, wgate, gbias, wgu, wgu_s, wd,
                  wd_s, ident, masks, rope1, ropek, ropeq, rank, expert_rows, out):
    with ExitStack() as ctx:
        def sb(name, shape, dt=F32):
            return ctx.enter_context(nc.sbuf_tensor(name, shape, dt))

        def signal(name, per=1, base=0):
            return Signal(ctx.enter_context(nc.semaphore(name)), per, base)

        wqkv_sb = sb("wqkv_sb", [P, 5, C])
        wo1_sb = sb("wo1_sb", [P, C])
        wkva_sb = sb("wkva_sb", [P, 2, P])
        wkvb_sb = sb("wkvb_sb", [NOPE, H, LAT])
        wqr_sb = sb("wqr_sb", [P, 2, 4, P])
        wabs_sb = sb("wabs_sb", [P, 2, P])
        wco_t = sb("wco_t", [P, 2, P])
        wco_sb = sb("wco_sb", [P, 2, C])
        ln1w_sb = sb("ln1w_sb", [P, 1])
        ln2w_sb = sb("ln2w_sb", [P, 1])
        wgate_sb = sb("wgate_sb", [P, E])
        gbias_sb = sb("gbias_sb", [P, E])
        wgu_sb = sb("wgu_sb", [P, 4, 2, P])
        wgus_sb = sb("wgus_sb", [P, 2, I])
        wd_sb = sb("wd_sb", [P, 4, C])
        wds_sb = sb("wds_sb", [I, C])
        ident_sb = sb("ident_sb", [P, P])
        identb = sb("identb", [P, P], BF16)
        maskb = sb("maskb", [P, 2, P], BF16)
        rope1_sb = sb("rope1_sb", [P, 2, T])
        ropek_sb = sb("ropek_sb", [P, 2, T])
        ropeq_sb = sb("ropeq_sb", [P, 4, 2, T])
        rank_sb = sb("rank_sb", [P, NT, E])
        erow = sb("erow", [P, 4, P], F32R)
        half = sb("half", [P, NT])

        x_in = sb("x_in", [P, NT, C])
        x_cur = sb("x_cur", [P, NT, C])
        xn = sb("xn", [P, NT, C])
        hres = sb("hres", [P, NT, C])
        y_sb = sb("y_sb", [P, NT, C])
        stats = sb("stats", [P, NT, 6])
        mv = sb("mv", [P, NT, 2])
        ve = sb("ve", [P, NT])
        sq = sb("sq", [P, NT])
        rstd = sb("rstd", [P, NT])
        xT = sb("xT", [P, T])
        tq = sb("tq", [P, 2, T])
        tk = sb("tk", [P, 2, T])
        qf = sb("qf", [P, T])
        kf = sb("kf", [P, T])
        qp = sb("qp", [P, 3, T], BF16)
        kp = sb("kp", [P, 3, T], BF16)
        qr_, kr_ = tq[:, 0, :], tk[:, 0, :]
        QS1 = sb("QS1", [P, H, T], BF16)
        KS1 = sb("KS1", [P, H, T], BF16)
        V1 = sb("V1", [P, NT, H, 32])
        QS2 = sb("QS2", [P, H, T], F32R)
        K1 = sb("K1", [P, T], F32R)
        K2 = sb("K2", [P, T], F32R)
        V2 = sb("V2", [P, NT, 32])
        NM = sb("NM", [P, NT, H])
        MB = sb("MB", [P, NT, 3, HG], BF16)
        MRest = sb("MRest", [P, NT, HG])
        MF = sb("MF", [P, NT, 2, HG], F32R)
        MPb = sb("MPb", [3 * HG, 2, T], BF16)
        MPr = sb("MPr", [2 * HG, 2, T], F32R)
        PA = sb("PA", [P, 8, 2 * T])
        PC = sb("PC", [P, 4, 2, 256])
        pa_flat = PA[:].rearrange("p a t -> p (a t)")
        wqn_sb = pa_flat[0:NOPE, 0:H * C].rearrange("d (h c) -> d h c", h=H)
        wo2_sb = pa_flat[0:NOPE, H * C:2 * H * C].rearrange("d (h c) -> d h c", h=H)
        erow_sb = pa_flat[:, 4096:4608].rearrange("p (a b) -> p a b", a=4)
        masks_sb = pa_flat[:, 4608:4864].rearrange("p (a b) -> p a b", a=2)
        QC2 = pa_flat[:, 0:12 * T].bitcast(F32R).rearrange("p (a n t) -> p a n t", a=2, n=6)
        HH = pa_flat[:, 0:5 * T].rearrange("p (n t) -> p n t", t=T)
        sg = pa_flat[:, 5 * T:7 * T].rearrange("p (n t) -> p n t", t=T)
        hu = pa_flat[:, 7 * T:9 * T].rearrange("p (n t) -> p n t", t=T)
        OT = qf
        rec = sb("rec", [P, NT, HG])
        ON = sb("ON", [P, NT, H * LAT])
        ONT = tk
        lg = sb("lg", [P, NT, E])
        mx = sb("mx", [P, NT])
        pe_ = sb("pe_", [P, NT, E])
        eq = sb("eq", [P, NT, E])
        key = sb("key", [P, NT, E])
        s1 = sb("s1", [P, NT, E])
        s2 = sb("s2", [P, NT, E])
        comb = sb("comb", [P, NT, E])
        CT = sb("CT", [P, T], F32R)

        scr_q = nc.dram_tensor("scr_q", [3, P, T], BF16, kind="Internal")
        scr_k = nc.dram_tensor("scr_k", [5, P, T], BF16, kind="Internal")
        scr_2 = nc.dram_tensor("scr_2", [2, 6, P, T], F32, kind="Internal")

        ps = ctx.enter_context(nc.psum_tensor("ps", [P, 8, T], F32))
        BK_C, BK_O = 6, 7

        loaded_first = signal("loaded_first")
        loaded = signal("loaded")
        consts_on_dve = signal("consts_on_dve")
        wprod = signal("wprod")
        wprod_read = signal("wprod_read")
        zeroed = signal("zeroed")
        x_copied = signal("x_copied")
        dve_past, sp_past = signal("dve_past", 6), signal("sp_past", 3)
        x_fetched = signal("x_fetched", 16, base=16)
        stat_step = signal("stat_step", 6 * 2)
        square_step = signal("square_step", 2)
        var_ready = signal("var_ready", 6)
        rstd_ready = signal("rstd_ready", 6)
        y_normed = signal("y_normed", 2)
        x1_ready = signal("x1_ready")
        h_res_ready = signal("h_res_ready")
        xn_ready = signal("xn_ready", 3)
        xT_ps = signal("xT_ps", 3)
        xT_ready = signal("xT_ready", 3)
        proj = signal("proj", 3)
        rot_terms = signal("rot_terms", 2)
        rotated = signal("rotated", 2)
        part_a = signal("part_a", 4)
        part_p = signal("part_p", 4)
        v1_ready = signal("v1_ready")
        stored = signal("stored", 3 * 16)
        stack_in = signal("stack_in", 6 * 16)
        score_fill = signal("score_fill", 2 * G * FILLS)
        fill_read = signal("fill_read", 2 * G * (FILLS - 1))
        m_step = signal("m_step", G * (4 + 2))
        m_copied = signal("m_copied", 2 * G)
        m_stacked = [signal(f"m_stacked{g}", 2 * 16) for g in range(G)]
        st_a = signal("st_a", 2 * H)
        st_c = signal("st_c", H)
        exp_a = signal("exp_a", 2 * H)
        exp_c = signal("exp_c", H)
        pv = signal("pv", 2 * G)
        ot_ready = signal("ot_ready", 2 * G)
        o_turned = signal("o_turned", 2 * G)
        rec_ready = signal("rec_ready", 2 * G)
        on_ready = signal("on_ready", 2 * G)
        ont_ps = signal("ont_ps", 2)
        ont_ready = signal("ont_ready", 2)
        y_ps = signal("y_ps", 3)
        y_ready = signal("y_ready", 3)
        kproj = signal("kproj", 2)
        k_step = signal("k_step", 4)
        v2_ready = signal("v2_ready")
        qabs_ps = signal("qabs_ps", 2)
        qabs_hi = signal("qabs_hi", 2)
        q_lo = signal("q_lo", 2)
        qrope_ps = signal("qrope_ps", 4)
        qrope_terms = signal("qrope_terms", 4)
        qrope_sum = signal("qrope_sum", 4)
        qrope_hi = signal("qrope_hi", 4)
        qrope_lo = signal("qrope_lo", 4)
        stored2 = signal("stored2", 2 * 16)
        stack2_in = [signal(f"stack2_in{g}", 16) for g in range(G)]
        logits_ps = signal("logits_ps")
        gate_step = signal("gate_step", 19)
        gate_exp = signal("gate_exp")
        comb_ps = signal("comb_ps")
        ct_hi = signal("ct_hi")
        ct_lo = signal("ct_lo")
        gu_ps = signal("gu_ps", 5)
        cb_ps = signal("cb_ps", 4)
        silu = signal("silu", 5)
        hu_ready = signal("hu_ready", 4)
        h_ready = signal("h_ready", 5)
        out_ready = signal("out_ready")
        out_sent = signal("out_sent", 16)

        x_next = x_ahead.rearrange("(n p) c -> p n c", p=P)
        x_seq = x.rearrange("(n p) c -> p n c", p=P)
        FIRST_LOADS = ((x_in[:], x_seq[:, 0:NT, :]), (ident_sb[:], ident[:]), (wqkv_sb[:], wqkv[:]),
                       (rope1_sb[:], rope1[:]), (masks_sb, masks[:]))
        LOADS = ((wo1_sb[:], wo1[:]), (wkva_sb[:], wkva[:]), (wqn_sb, wq_nope[:]), (wkvb_sb[:], wkvb[:]),
                 (wqr_sb[:], wq_rope[:]), (wo2_sb, wo2[:]), (ln1w_sb[:], ln1w[:]), (ln2w_sb[:], ln2w[:]),
                 (wgate_sb[:], wgate[:]), (gbias_sb[:], gbias[:]), (ropek_sb[:], ropek[:]), (ropeq_sb[:], ropeq[:]),
                 (wgu_sb[:], wgu[:]), (wgus_sb[:], wgu_s[:]), (wd_sb[:], wd[:]), (wds_sb[:], wd_s[:]),
                 (rank_sb[:], rank[:]), (erow_sb, expert_rows[:]))
        ALL_FIRST, ALL_LOADED = 16 * (len(FIRST_LOADS) - 1), 16 * len(LOADS)

        block = ctx.enter_context(nc.Block())

        @block.sync
        def _(sp):
            for dst, src in FIRST_LOADS[:1]:
                sp.dma_start(dst, src).then_inc(x_fetched.sem, 16)
            for dst, src in FIRST_LOADS[1:]:
                sp.dma_start(dst, src).then_inc(loaded_first.sem, 16)
            for dst, src in LOADS:
                sp.dma_start(dst, src).then_inc(loaded.sem, 16)

            def send_max(it, att, g):
                sp.wait_ge(*m_copied(it, att * G + g + 1))
                if att == 0:
                    sp.dma_start(QS1[MROW:MROW + 3, HG * g:HG * g + HG, :], MPb[:, g % 2, :]).then_inc(m_stacked[g].sem, 16)
                else:
                    sp.dma_start(QS2[MROW:MROW + 2, HG * g:HG * g + HG, :].bitcast(F32), MPr[:, g % 2, :].bitcast(F32))\
                      .then_inc(m_stacked[g].sem, 16)

            with sp.Fori(0, B) as it:
                sp.wait_ge(*x_copied(it, 1))
                sp.sem_inc(sp_past.sem, 1)
                sp.dma_start(x_in[:], x_next[:, bass.ds(it * NT, NT), :]).then_inc(x_fetched.sem, 16)
                sp.wait_ge(*part_p(it, 4))
                sp.dma_start(scr_q[:].rearrange("a p t -> p a t"), qp[:]).then_inc(stored.sem, 16)
                sp.dma_start(scr_k[0:3].rearrange("a p t -> p a t"), kp[:]).then_inc(stored.sem, 16)
                sp.dma_start(scr_k[3:5].rearrange("a p t -> p a t"), kp[:, 0:2, :]).then_inc(stored.sem, 16)
                sp.wait_ge(*stored(it, 48))
                sp.wait_ge(consts_on_dve.sem, 3)
                for b in range(3):
                    sp.dma_start(QS1[24 * b:24 * b + 24, :, :],
                                 scr_q[:].rearrange("a (d h) t -> (a d) h t", h=H)).then_inc(stack_in.sem, 16)
                    sp.dma_start(KS1[24 * b:24 * b + 24, :, :],
                                 scr_k[b:b + 3].rearrange("a (d h) t -> (a d) h t", h=H)).then_inc(stack_in.sem, 16)
                for g in range(G):
                    send_max(it, 0, g)
                sp.wait_ge(*qrope_lo(it, 4))
                for a in range(2):
                    sp.dma_start(scr_2[a].rearrange("n p t -> p n t"), QC2[:, a, :, :].bitcast(F32)).then_inc(stored2.sem, 16)
                sp.wait_ge(*stored2(it, 32))
                sp.wait_ge(zeroed.sem, 2)
                for g in range(G):
                    sp.dma_start(QS2[0:2 * DK2, HG * g:HG * g + HG, :].bitcast(F32),
                                 scr_2[:].rearrange("a n (d h) t -> (a n d) h t", h=H)[:, HG * g:HG * g + HG, :])\
                      .then_inc(stack2_in[g].sem, 16)
                for g in range(G):
                    send_max(it, 1, g)
                sp.wait_ge(*out_ready(it, 1))
                sp.sem_inc(sp_past.sem, 1)
                sp.dma_start(out.rearrange("(n p) c -> p n c", p=P)[:, bass.ds(it * NT, NT), :], y_sb[:])\
                  .then_inc(out_sent.sem, 16)
                sp.wait_ge(*out_sent(it, 16))
                sp.sem_inc(sp_past.sem, 1)

        @block.tensor
        def _(pe):
            def fill(it, att, g, n, hh):
                f = (att * G + g) * FILLS + n
                if n == 1 and att * G + g:
                    pe.wait_ge(*m_copied(it, att * G + g))
                elif n >= 2 or (n == 0 and att * G + g):
                    pe.wait_ge(*fill_read(it, (att * G + g) * (FILLS - 1) + n - 1))
                return ps[:, f % 2, :]

            def products(dst, att, h, i, n):
                if att == 0:
                    pe.matmul(dst, QS1[0:MROW, h, P * i:P * i + P], KS1[0:MROW, h, 0:P * n], start=True, stop=False)
                else:
                    pe.matmul(dst, QS2[0:MROW, h, P * i:P * i + P], K1[0:MROW, 0:P * n], start=True, stop=False)
                return pe.matmul(dst[:, P * (n - 1):P * n], identb[:], maskb[:, 0, :], start=False, stop=True)

            def scores_for_max(it, att, g, hh):
                h = HG * g + hh
                n = 2 * hh + hh // 2
                bank = fill(it, att, g, n, hh)
                products(bank, att, h, 3, 4).then_inc(score_fill.sem, 1)
                bank = fill(it, att, g, n + 1, hh)
                products(bank[:, 0:3 * P], att, h, 2, 3).then_inc(score_fill.sem, 1)
                if hh % 2:
                    bank = fill(it, att, g, n + 2, hh)
                    for k in range(2):
                        mm = products(bank[:, 256 * k:256 * k + 256], att, h - 1 + k, 1, 2)
                    mm.then_inc(score_fill.sem, 1)
                if hh == HG - 1:
                    bank = fill(it, att, g, n + 3, hh)
                    for k in range(HG):
                        mm = products(bank[:, P * k:P * k + P], att, HG * g + k, 0, 1)
                    mm.then_inc(score_fill.sem, 1)

            def turn_max(it, att, g):
                f = (att * G + g) * FILLS + FILLS - 1
                pe.wait_ge(*m_step(it, 4 * (g + 1) if att == 0 else 4 * G + 2 * (g + 1)))
                for t in range(NT):
                    if att == 0:
                        mm = pe.transpose(ps[0:3 * HG, f % 2, :].bitcast(BF16)[:, P * t:P * t + P],
                                          MB[:, t, :, :].rearrange("p a h -> p (a h)"), identb[:])
                    else:
                        mm = pe.transpose(ps[0:2 * HG, f % 2, P * t:P * t + P],
                                          MF[:, t, :, :].bitcast(F32).rearrange("p a h -> p (a h)"), ident_sb[:])
                mm.then_inc(score_fill.sem, 1)

            def scores_t(dst, att, h, j, n):
                q0 = P * j
                if att == 0:
                    pe.matmul(dst, KS1[:, h, q0:q0 + P], QS1[:, h, q0:T], start=True, stop=False)
                else:
                    pe.matmul(dst, K1[:, q0:q0 + P], QS2[:, h, q0:T], start=True, stop=False)
                    pe.matmul(dst, K2[:, q0:q0 + P], QS2[:, h, q0:T], start=False, stop=False)
                return pe.matmul(dst[:, 0:P], identb[:], maskb[:, 1, :], start=False, stop=True)

            def scores_for_exp(it, att, g, hh):
                h = HG * g + hh
                n = att * H + h
                if hh == 0:
                    pe.wait_ge(*m_stacked[g](it, 16 * (att + 1)))
                if n >= 2:
                    pe.wait_ge(*exp_a(it, n - 1))
                a = 2 + 2 * (h % 2)
                scores_t(ps[:, a, :], att, h, 0, 4)
                scores_t(ps[:, a + 1, 0:3 * P], att, h, 1, 3)
                scores_t(ps[:, a + 1, 3 * P:T], att, h, 3, 1).then_inc(st_a.sem, 1)
                if hh % 2 == 0 and n >= 2:
                    pe.wait_ge(*exp_c(it, n // 2))
                mm = scores_t(ps[:, BK_C, 256 * (h % 2):256 * (h % 2) + 256], att, h, 2, 2)
                if hh % 2:
                    mm.then_inc(st_c.sem, 1)

            def values(it, att, g):
                pe.wait_ge(*exp_a(it, att * H + HG * (g + 1)))
                pe.wait_ge(*exp_c(it, (att * H + HG * (g + 1)) // 2))
                if att or g:
                    pe.wait_ge(*on_ready(it, att * G + g))
                for j in range(NT):
                    for hh in range(HG):
                        h = HG * g + hh
                        slot = h % 8
                        p = (PA[:, slot, 0:T], PA[:, slot, T:T + 3 * P], PC[:, slot // 2, hh % 2, :],
                             PA[:, slot, T + 3 * P:2 * T])[j]
                        v = V1[:, j, h, :] if att == 0 else V2[:, j, :]
                        mm = pe.matmul(ps[32 * hh:32 * hh + 32, BK_O, P * j:T], v, p, start=(j == 0), stop=(j == NT - 1),
                                       skip_group_check=True)
                mm.then_inc(pv.sem, 1)

            def turn_out(it, att, g):
                pe.wait_ge(*ot_ready(it, att * G + g + 1))
                for t in range(NT):
                    mm = pe.transpose(ps[:, BK_O, P * t:P * t + P], OT[:, P * t:P * t + P], ident_sb[:])
                mm.then_inc(o_turned.sem, 1)

            def attention(it, att):
                for g in range(2):
                    if att and g < 2:
                        pe.wait_ge(*stack2_in[g](it, 16))
                    for hh in range(HG):
                        scores_for_max(it, att, g, hh)
                    turn_max(it, att, g)
                for g in range(G):
                    if att and g + 2 < G:
                        pe.wait_ge(*stack2_in[g + 2](it, 16))
                    for hh in range(HG):
                        scores_for_exp(it, att, g, hh)
                        if g + 2 < G:
                            scores_for_max(it, att, g + 2, hh)
                        if hh == 1 and g:
                            values(it, att, g - 1)
                    if g + 2 < G:
                        turn_max(it, att, g + 2)
                    if g:
                        turn_out(it, att, g - 1)
                values(it, att, G - 1)
                turn_out(it, att, G - 1)

            def turn_tokens(it, n, src):
                for t in range(NT):
                    mm = pe.transpose(ps[:, 0, P * t:P * t + P], src[:, t, :], ident_sb[:])
                mm.then_inc(xT_ps.sem, 1)
                pe.wait_ge(*xT_ready(it, n))

            pe.wait_ge(loaded_first.sem, ALL_FIRST)
            pe.wait_ge(loaded.sem, ALL_LOADED)
            pe.wait_ge(consts_on_dve.sem, 3)
            for h in range(H):
                pe.matmul(ps[:, 0, LAT * h:LAT * h + LAT], wqn_sb[:, h, :], wkvb_sb[:, h, :], start=True, stop=True)
                mm = pe.matmul(ps[:, 1, LAT * h:LAT * h + LAT], wo2_sb[:, h, :], wkvb_sb[:, h, :], start=True, stop=True)
            mm.then_inc(wprod.sem, 1)
            pe.wait_ge(wprod_read.sem, 2)
            for a in range(2):
                mm = pe.transpose(ps[:, 2, P * a:P * a + P], wco_t[:, a, :], ident_sb[:])
            mm.then_inc(wprod.sem, 1)

            with pe.Fori(0, B) as it:
                pe.wait_ge(*xn_ready(it, 1))
                turn_tokens(it, 1, xn)
                for n in range(4):
                    mm = pe.matmul(ps[:, 2 + n, :], wqkv_sb[:, n, :], xT[:], start=True, stop=True)
                    if n % 2:
                        mm.then_inc(proj.sem, 1)
                for t in range(NT):
                    mm = pe.matmul(ps[:, BK_C, P * t:P * t + P], xT[:, P * t:P * t + P], wqkv_sb[:, 4, :],
                                   start=True, stop=True)
                mm.then_inc(proj.sem, 1)
                pe.wait_ge(*stack_in(it, 96))
                pe.wait_ge(*v1_ready(it, 1))
                attention(it, 0)
                pe.wait_ge(*on_ready(it, G))
                for t in range(NT):
                    mm = pe.transpose(ps[:, 0, P * t:P * t + P], ON[:, t, 0:P], ident_sb[:])
                mm.then_inc(ont_ps.sem, 1)
                pe.wait_ge(*ont_ready(it, 1))
                for t in range(NT):
                    mm = pe.matmul(ps[:, 1, P * t:P * t + P], ONT[:, 0, P * t:P * t + P], wo1_sb[:], start=True, stop=True)
                mm.then_inc(y_ps.sem, 1)

                pe.wait_ge(*xn_ready(it, 2))
                turn_tokens(it, 2, xn)
                for n in range(2):
                    mm = pe.matmul(ps[:, 2 + n, :], wkva_sb[:, n, :], xT[:], start=True, stop=True)
                mm.then_inc(kproj.sem, 1)
                for t in range(NT):
                    mm = pe.matmul(ps[:, BK_C, LAT * t:LAT * t + LAT], xT[:, P * t:P * t + P], wkva_sb[:, 0, 0:LAT],
                                   start=True, stop=True)
                mm.then_inc(kproj.sem, 1)
                for n in range(2):
                    pe.matmul(ps[:, 4 + n, :], wabs_sb[:, n, :], xT[:], start=True, stop=True).then_inc(qabs_ps.sem, 1)
                for n in range(4):
                    a = (0, 2, 4, 0)[n]
                    if n == 1:
                        pe.wait_ge(*k_step(it, 1))
                    if n == 2:
                        pe.wait_ge(*q_lo(it, 2))
                    if n == 3:
                        pe.wait_ge(*qrope_terms(it, 1))
                    for m in range(2):
                        mm = pe.matmul(ps[:, a + m, :], wqr_sb[:, m, n, :], xT[:], start=True, stop=True)
                    mm.then_inc(qrope_ps.sem, 1)
                pe.wait_ge(*qrope_terms(it, 4))
                pe.wait_ge(*k_step(it, 4))
                pe.wait_ge(*v2_ready(it, 1))
                attention(it, 1)
                pe.wait_ge(*on_ready(it, 2 * G))
                for a in range(2):
                    for t in range(NT):
                        mm = pe.transpose(ps[:, 2 + a, P * t:P * t + P], ON[:, t, P * a:P * a + P], ident_sb[:])
                mm.then_inc(ont_ps.sem, 1)
                pe.wait_ge(*ont_ready(it, 2))
                for t in range(NT):
                    for a in range(2):
                        mm = pe.matmul(ps[:, 1, P * t:P * t + P], ONT[:, a, P * t:P * t + P], wco_sb[:, a, :],
                                       start=(a == 0), stop=(a == 1))
                mm.then_inc(y_ps.sem, 1)

                pe.wait_ge(*xn_ready(it, 3))
                turn_tokens(it, 3, xn)
                for t in range(NT):
                    mm = pe.matmul(ps[:, 1, E * t:E * t + E], xT[:, P * t:P * t + P], wgate_sb[:], start=True, stop=True)
                mm.then_inc(logits_ps.sem, 1)
                for n in range(5):
                    a = 2 + 2 * (n % 2)
                    if n >= 2:
                        pe.wait_ge(*silu(it, n - 1))
                        pe.wait_ge(*(h_ready(it, 1) if n == 2 else hu_ready(it, n - 2)))
                    for m in range(2):
                        if n == 0:
                            mm = pe.matmul(ps[0:I, a + m, :], wgus_sb[:, m, :], xT[:], start=True, stop=True)
                        else:
                            mm = pe.matmul(ps[:, a + m, :], wgu_sb[:, n - 1, m, :], xT[:], start=True, stop=True)
                    mm.then_inc(gu_ps.sem, 1)
                    if n == 1:
                        pe.wait_ge(*gate_step(it, 19))
                        for t in range(NT):
                            mm = pe.transpose(ps[0:E, BK_C, P * t:P * t + P], comb[:, t, :], ident_sb[:])
                        mm.then_inc(comb_ps.sem, 1)
                        pe.wait_ge(*ct_hi(it, 1))
                        pe.wait_ge(*ct_lo(it, 1))
                    if n >= 1:
                        if n >= 3:
                            pe.wait_ge(*h_ready(it, n - 1))
                        pe.matmul(ps[:, (n - 1) % 2, :], erow[:, n - 1, :], CT[:], start=True, stop=True)\
                          .then_inc(cb_ps.sem, 1)
                pe.wait_ge(*h_ready(it, 5))
                for t in range(NT):
                    pe.matmul(ps[:, BK_O, P * t:P * t + P], HH[0:I, 4, P * t:P * t + P], wds_sb[:], start=True, stop=False)
                    for n in range(4):
                        mm = pe.matmul(ps[:, BK_O, P * t:P * t + P], HH[:, n, P * t:P * t + P], wd_sb[:, n, :],
                                       start=False, stop=(n == 3))
                mm.then_inc(y_ps.sem, 1)

        @block.scalar
        def _(act):
            def exps(it, att, g, hh, scale):
                h = HG * g + hh
                n = att * H + h
                if hh == 0 and att * G + g >= 2:
                    act.wait_ge(*pv(it, att * G + g - 1))
                act.wait_ge(*st_a(it, n + 1))
                a = 2 + 2 * (h % 2)
                act.activation(PA[:, h % 8, :].rearrange("p (a t) -> p a t", a=2), ps[:, a:a + 2, :], ACT.Exp,
                               scale=scale).then_inc(exp_a.sem, 1)
                if hh % 2:
                    act.wait_ge(*st_c(it, (n + 1) // 2))
                    act.activation(PC[:, (h % 8) // 2, :, :], ps[:, BK_C, :].rearrange("p (a t) -> p a t", a=2), ACT.Exp,
                                   scale=scale).then_inc(exp_c.sem, 1)

            def copy_out(it, att, g):
                act.wait_ge(*pv(it, att * G + g + 1))
                act.activation(OT[:], ps[:, BK_O, :], ACT.Copy).then_inc(ot_ready.sem, 1)

            def attention(it, att, scale):
                for g in range(G):
                    for hh in range(HG):
                        exps(it, att, g, hh, scale)
                        if hh == 2 and g:
                            copy_out(it, att, g - 1)
                copy_out(it, att, G - 1)

            act.wait_ge(loaded.sem, ALL_LOADED)
            with act.Fori(0, B) as it:
                act.wait_ge(*xT_ps(it, 1))
                act.activation(xT[:], ps[:, 0, :], ACT.Copy).then_inc(xT_ready.sem, 1)
                act.wait_ge(*rotated(it, 1))
                act.activation(qp[:, 0, :], qf[:], ACT.Copy).then_inc(part_a.sem, 1)
                act.wait_ge(*rotated(it, 2))
                act.activation(kp[:, 0, :], kf[:], ACT.Copy).then_inc(part_a.sem, 1)
                act.wait_ge(*part_p(it, 1))
                act.activation(qp[:, 1, :], qr_, ACT.Copy).then_inc(part_a.sem, 1)
                act.wait_ge(*part_p(it, 2))
                act.activation(kp[:, 1, :], kr_, ACT.Copy).then_inc(part_a.sem, 1)
                act.wait_ge(*proj(it, 3))
                act.wait_ge(zeroed.sem, 2)
                act.activation(V1[:, :, :, 0:D1], ps[:, BK_C, :].rearrange("p (t h d) -> p t h d", t=NT, h=H),
                               ACT.Copy).then_inc(v1_ready.sem, 1)
                attention(it, 0, D1 ** -0.5)
                act.wait_ge(*ont_ps(it, 1))
                act.activation(ONT[:, 0, :], ps[:, 0, :], ACT.Copy).then_inc(ont_ready.sem, 1)

                act.wait_ge(*xT_ps(it, 2))
                act.activation(xT[:], ps[:, 0, :], ACT.Copy, scale=ln1w_sb[:]).then_inc(xT_ready.sem, 1)
                act.wait_ge(*kproj(it, 2))
                act.activation(V2[:, :, 0:LAT], ps[:, BK_C, 0:NT * LAT].rearrange("p (t r) -> p t r", t=NT),
                               ACT.Copy).then_inc(v2_ready.sem, 1)
                for n in range(2):
                    act.wait_ge(*qabs_ps(it, n + 1))
                    act.activation(QC2[:, 0, n, :], ps[:, 4 + n, :], ACT.Copy).then_inc(qabs_hi.sem, 1)
                for n in range(4):
                    act.wait_ge(*qrope_sum(it, n + 1))
                    act.activation(QC2[:, 0, 2 + n, :], (qf, kf)[n % 2][:], ACT.Copy).then_inc(qrope_hi.sem, 1)
                attention(it, 1, D2 ** -0.5)
                act.wait_ge(*ont_ps(it, 2))
                act.activation(ONT[:], ps[:, 2:4, :], ACT.Copy).then_inc(ont_ready.sem, 1)

                act.wait_ge(*xT_ps(it, 3))
                act.activation(xT[:], ps[:, 0, :], ACT.Copy, scale=ln2w_sb[:]).then_inc(xT_ready.sem, 1)
                act.wait_ge(*gate_step(it, 3))
                act.activation(pe_[:], key[:], ACT.Exp).then_inc(gate_exp.sem, 1)
                act.wait_ge(*comb_ps(it, 1))
                act.activation(CT[0:E, :], ps[0:E, BK_C, :], ACT.Copy).then_inc(ct_hi.sem, 1)
                for n in range(5):
                    a = 2 + 2 * (n % 2)
                    rows = I if n == 0 else P
                    act.wait_ge(*gu_ps(it, n + 1))
                    if n >= 2:
                        act.wait_ge(*(h_ready(it, 1) if n == 2 else hu_ready(it, n - 2)))
                    act.activation(sg[0:rows, n % 2, :], ps[0:rows, a, :], ACT.Silu).then_inc(silu.sem, 1)

        @block.gpsimd
        def _(pool):
            def power(it, n):
                pool.wait_ge(*var_ready(it, n))
                pool.tensor_tensor(rstd[:], ve[:], half[:], ALU.pow).then_inc(rstd_ready.sem, 1)

            pool.memset(QS2[64:P].bitcast(F32), 0.0).then_inc(zeroed.sem, 1)
            pool.wait_ge(zeroed.sem, 1)
            pool.memset(V1[:], 1.0)
            pool.memset(V2[:], 1.0)
            pool.memset(half[:], -0.5).then_inc(zeroed.sem, 1)
            pool.wait_ge(zeroed.sem, 2)
            with pool.Fori(0, B) as it:
                power(it, 1)
                for n, (terms, whole) in enumerate(((tq, qf), (tk, kf))):
                    pool.wait_ge(*rot_terms(it, n + 1))
                    pool.tensor_tensor(whole[:], terms[:, 0, :], terms[:, 1, :], ALU.add).then_inc(rotated.sem, 1)
                for n, (whole, high, rest) in enumerate(((qf, qp, qr_), (kf, kp, kr_))):
                    pool.wait_ge(*part_a(it, n + 1))
                    pool.tensor_tensor(rest, whole[:], high[:, 0, :], ALU.subtract).then_inc(part_p.sem, 1)
                for n, (rest, parts) in enumerate(((qr_, qp), (kr_, kp))):
                    pool.wait_ge(*part_a(it, n + 3))
                    pool.tensor_tensor(parts[:, 2, :], rest, parts[:, 1, :], ALU.subtract).then_inc(part_p.sem, 1)
                for n in range(2, 5):
                    power(it, n)
                for n in range(4):
                    whole, terms = (qf, kf)[n % 2], (tq, tk)[n % 2]
                    pool.wait_ge(*qrope_terms(it, n + 1))
                    if n >= 2:
                        pool.wait_ge(*qrope_hi(it, n - 1))
                    pool.tensor_tensor(whole[:], terms[:, 0, :], terms[:, 1, :], ALU.add).then_inc(qrope_sum.sem, 1)
                    pool.wait_ge(*qrope_hi(it, n + 1))
                    pool.tensor_tensor(QC2[:, 1, 2 + n, :], whole[:], QC2[:, 0, 2 + n, :].bitcast(F32), ALU.subtract)\
                        .then_inc(qrope_lo.sem, 1)
                for n in range(5, 7):
                    power(it, n)

        @block.vector
        def _(dve):
            def moments(it, n, src):
                for t in range(NT):
                    last = dve.bn_stats(stats[:, t, :], src[:, t, :])
                last.then_inc(stat_step.sem, 1)
                dve.wait_ge(*stat_step(it, 2 * n + 1))
                dve.sem_inc(dve_past.sem, 1)
                for t in range(NT):
                    last = dve.bn_aggr(mv[:, t, :], stats[:, t, :])
                last.then_inc(stat_step.sem, 1)
                dve.wait_ge(*stat_step(it, 2 * n + 2))

            def layer_var(it, n):
                dve.tensor_scalar(ve[:], mv[:, :, 1], EPS, None, ALU.add).then_inc(var_ready.sem, 1)
                dve.wait_ge(*rstd_ready(it, n + 1))

            def mean_square(it, n):
                dve.tensor_tensor(sq[:], mv[:, :, 0], mv[:, :, 0], ALU.mult).then_inc(square_step.sem, 1)
                dve.wait_ge(*square_step(it, n - 2))
                dve.scalar_tensor_tensor(out=ve[:], in0=sq[:], scalar=EPS, in1=mv[:, :, 1], op0=ALU.add, op1=ALU.add)\
                    .then_inc(var_ready.sem, 1)
                dve.wait_ge(*rstd_ready(it, n + 1))

            def normalise(dst, src):
                for t in range(NT):
                    last = dve.tensor_scalar(dst[:, t, :], src[:, t, :], mv[:, t, 0:1], rstd[:, t:t + 1], ALU.subtract,
                                             ALU.mult)
                return last

            def rescale(dst, src):
                for t in range(NT):
                    last = dve.tensor_scalar(dst[:, t, :], src[:, t, :], rstd[:, t:t + 1], None, ALU.mult)
                return last

            def reduce_fill(it, att, g, n, src, dst):
                dve.wait_ge(*score_fill(it, (att * G + g) * FILLS + n + 1))
                dve.tensor_reduce(dst, src, AX.X, ALU.max, negate=True).then_inc(fill_read.sem, 1)

            def maxima(it, att, g, hh):
                h = HG * g + hh
                n = 2 * hh + hh // 2
                f = (att * G + g) * FILLS + n
                reduce_fill(it, att, g, n, ps[:, f % 2, :], NM[:, 3, h:h + 1])
                reduce_fill(it, att, g, n + 1, ps[:, (f + 1) % 2, 0:3 * P], NM[:, 2, h:h + 1])
                if hh % 2:
                    reduce_fill(it, att, g, n + 2, ps[:, (f + 2) % 2, :].rearrange("p (a k) -> p a k", a=2),
                                NM[:, 1, h - 1:h + 1])
                if hh == HG - 1:
                    reduce_fill(it, att, g, n + 3, ps[:, (f + 3) % 2, :].rearrange("p (a k) -> p a k", a=4),
                                NM[:, 0, HG * g:HG * g + HG])

            def split_max(it, att, g):
                m, f = NM[:, :, HG * g:HG * g + HG], (att * G + g + 1) * FILLS
                k = 4 * g if att == 0 else 4 * G + 2 * g
                dve.wait_ge(*fill_read(it, (att * G + g + 1) * (FILLS - 1)))
                if att * G + g:
                    dve.wait_ge(*m_copied(it, att * G + g))
                if att == 0:
                    dve.tensor_copy(MB[:, :, 0, :], m).then_inc(m_step.sem, 1)
                    dve.wait_ge(*m_step(it, k + 1))
                    dve.tensor_tensor(MRest[:], m, MB[:, :, 0, :], ALU.subtract).then_inc(m_step.sem, 1)
                    dve.wait_ge(*m_step(it, k + 2))
                    dve.tensor_copy(MB[:, :, 1, :], MRest[:]).then_inc(m_step.sem, 1)
                    dve.wait_ge(*m_step(it, k + 3))
                    dve.tensor_tensor(MB[:, :, 2, :], MRest[:], MB[:, :, 1, :], ALU.subtract).then_inc(m_step.sem, 1)
                else:
                    dve.tensor_copy(MF[:, :, 0, :], m).then_inc(m_step.sem, 1)
                    dve.wait_ge(*m_step(it, k + 1))
                    dve.tensor_tensor(MF[:, :, 1, :], m, MF[:, :, 0, :].bitcast(F32), ALU.subtract)\
                        .then_inc(m_step.sem, 1)
                dve.wait_ge(*score_fill(it, f))
                if g >= 2:
                    dve.wait_ge(*m_stacked[g - 2](it, 16 * (att + 1)))
                if att == 0:
                    dve.tensor_copy(MPb[:, g % 2, :], ps[0:3 * HG, (f - 1) % 2, :].bitcast(BF16)[:, 0:T])\
                        .then_inc(m_copied.sem, 1)
                else:
                    dve.tensor_copy(MPr[:, g % 2, :], ps[0:2 * HG, (f - 1) % 2, :]).then_inc(m_copied.sem, 1)

            def divide(it, att, g):
                w, n = (D1, att * G + g) if att == 0 else (LAT, att * G + g)
                bank = ps[:, BK_O, :].rearrange("p (t h d) -> p t h d", t=NT, h=HG)
                dve.wait_ge(*o_turned(it, n + 1))
                dve.reciprocal(rec[:], bank[:, :, :, w]).then_inc(rec_ready.sem, 1)
                dve.wait_ge(*rec_ready(it, n + 1))
                on = ON[:, :, 0:H * w].rearrange("p t (h d) -> p t h d", h=H)
                dve.tensor_tensor(on[:, :, HG * g:HG * g + HG, :], bank[:, :, :, 0:w],
                                  rec[:].unsqueeze(3).to_broadcast([P, NT, HG, w]), ALU.mult).then_inc(on_ready.sem, 1)

            def attention(it, att):
                for g in range(2):
                    for hh in range(HG):
                        maxima(it, att, g, hh)
                    split_max(it, att, g)
                for g in range(G):
                    if g + 2 < G:
                        for hh in range(HG):
                            maxima(it, att, g + 2, hh)
                        split_max(it, att, g + 2)
                    if g:
                        divide(it, att, g - 1)
                divide(it, att, G - 1)

            dve.memset(QS1[64:P].bitcast(F32), 0.0)
            dve.memset(KS1[64:P].bitcast(F32), 0.0)
            dve.memset(K1[:].bitcast(F32), 0.0)
            dve.memset(K2[:].bitcast(F32), 0.0)
            dve.memset(CT[:].bitcast(F32), 0.0).then_inc(consts_on_dve.sem, 1)
            dve.wait_ge(consts_on_dve.sem, 1)
            dve.memset(KS1[MROW:P], 1.0)
            dve.memset(K1[MROW:P].bitcast(F32), 1.0)
            dve.wait_ge(loaded_first.sem, ALL_FIRST)
            dve.wait_ge(loaded.sem, ALL_LOADED)
            dve.tensor_copy(identb[:], ident_sb[:])
            dve.tensor_copy(maskb[:], masks_sb)
            dve.tensor_copy(erow[:], erow_sb).then_inc(consts_on_dve.sem, 2)
            dve.wait_ge(wprod.sem, 1)
            dve.tensor_copy(wabs_sb[:].rearrange("p a b -> p (a b)").rearrange("p (r h) -> p r h", h=H),
                            ps[:, 0, 0:H * LAT].rearrange("p (h r) -> p r h", h=H)).then_inc(wprod_read.sem, 1)
            dve.tensor_copy(wco_t[:].rearrange("p a b -> p (a b)"), ps[:, 1, 0:H * LAT]).then_inc(wprod_read.sem, 1)
            dve.wait_ge(wprod.sem, 2)
            dve.tensor_copy(wco_sb[:].rearrange("p a b -> p (a b)"), ps[:, 2, 0:2 * P]).then_inc(wprod_read.sem, 1)

            with dve.Fori(0, B) as it:
                dve.wait_ge(*x_fetched(it, 0))
                dve.tensor_copy(x_cur[:], x_in[:]).then_inc(x_copied.sem, 1)
                dve.wait_ge(*x_copied(it, 1))
                moments(it, 0, x_cur)
                layer_var(it, 0)
                normalise(xn, x_cur).then_inc(xn_ready.sem, 1)
                for n, terms in enumerate((tq, tk)):
                    dve.wait_ge(*proj(it, n + 1))
                    dve.tensor_tensor(terms[:, 0, :], ps[:, 2 + 2 * n, :], rope1_sb[:, 0, :], ALU.mult)
                    dve.tensor_tensor(terms[:, 1, :], ps[:, 3 + 2 * n, :], rope1_sb[:, 1, :], ALU.mult)\
                        .then_inc(rot_terms.sem, 1)
                attention(it, 0)
                dve.wait_ge(*y_ps(it, 1))
                dve.tensor_copy(y_sb[:], ps[:, 1, :].rearrange("p (t c) -> p t c", t=NT)).then_inc(y_ready.sem, 1)
                dve.wait_ge(*y_ready(it, 1))
                moments(it, 1, y_sb)
                layer_var(it, 1)
                normalise(y_sb, y_sb).then_inc(y_normed.sem, 1)
                dve.wait_ge(*y_normed(it, 1))
                dve.tensor_tensor(x_cur[:], x_cur[:], y_sb[:], ALU.add).then_inc(x1_ready.sem, 1)
                dve.wait_ge(*x1_ready(it, 1))
                moments(it, 2, x_cur)
                layer_var(it, 2)
                normalise(hres, x_cur).then_inc(h_res_ready.sem, 1)
                dve.wait_ge(*h_res_ready(it, 1))
                moments(it, 3, hres)
                mean_square(it, 3)
                rescale(xn, hres).then_inc(xn_ready.sem, 1)

                dve.wait_ge(*kproj(it, 1))
                dve.tensor_tensor(tq[:, 0, :], ps[:, 2, :], ropek_sb[:, 0, :], ALU.mult)
                dve.tensor_tensor(tq[:, 1, :], ps[:, 3, :], ropek_sb[:, 1, :], ALU.mult).then_inc(k_step.sem, 1)
                dve.wait_ge(*k_step(it, 1))
                dve.tensor_tensor(tk[:, 0, :], tq[:, 0, :], tq[:, 1, :], ALU.add).then_inc(k_step.sem, 1)
                dve.wait_ge(*k_step(it, 2))
                dve.tensor_copy(K1[0:2 * DK2, :], tk[0:2 * DK2, 0, :]).then_inc(k_step.sem, 1)
                dve.wait_ge(*k_step(it, 3))
                dve.tensor_tensor(K2[0:2 * DK2, :], tk[0:2 * DK2, 0, :], K1[0:2 * DK2, :].bitcast(F32), ALU.subtract)\
                    .then_inc(k_step.sem, 1)
                dve.wait_ge(*k_step(it, 4))
                for n in range(2):
                    dve.wait_ge(*qabs_hi(it, n + 1))
                    dve.tensor_tensor(QC2[:, 1, n, :], ps[:, 4 + n, :], QC2[:, 0, n, :].bitcast(F32), ALU.subtract)\
                        .then_inc(q_lo.sem, 1)
                for n in range(4):
                    terms, a = (tq, tk)[n % 2], (0, 2, 4, 0)[n]
                    dve.wait_ge(*qrope_ps(it, n + 1))
                    if n >= 2:
                        dve.wait_ge(*qrope_sum(it, n - 1))
                    dve.tensor_tensor(terms[:, 0, :], ps[:, a, :], ropeq_sb[:, n, 0, :], ALU.mult)
                    dve.tensor_tensor(terms[:, 1, :], ps[:, a + 1, :], ropeq_sb[:, n, 1, :], ALU.mult)\
                        .then_inc(qrope_terms.sem, 1)
                attention(it, 1)
                dve.wait_ge(*y_ps(it, 2))
                dve.tensor_tensor(hres[:], hres[:], ps[:, 1, :].rearrange("p (t c) -> p t c", t=NT), ALU.add)\
                    .then_inc(y_ready.sem, 1)
                dve.wait_ge(*y_ready(it, 2))
                moments(it, 4, hres)
                mean_square(it, 4)
                rescale(xn, hres).then_inc(xn_ready.sem, 1)

                def gate(n, ins):
                    ins.then_inc(gate_step.sem, 1)
                    dve.wait_ge(*gate_step(it, n))

                def wide(v):
                    return v[:].unsqueeze(2).to_broadcast([P, NT, E])

                dve.wait_ge(*logits_ps(it, 1))
                gate(1, dve.tensor_tensor(lg[:], ps[:, 1, 0:NT * E].rearrange("p (t e) -> p t e", t=NT),
                                          gbias_sb[:].unsqueeze(1).to_broadcast([P, NT, E]), ALU.add))
                gate(2, dve.tensor_reduce(mx[:], lg[:], AX.X, ALU.max))
                gate(3, dve.tensor_tensor(key[:], lg[:], wide(mx), ALU.subtract))
                dve.wait_ge(*gate_exp(it, 1))
                step = 3
                for probs, chosen in ((pe_, s1), (lg, s2)):
                    gate(step + 1, dve.tensor_reduce(mx[:], probs[:], AX.X, ALU.max))
                    gate(step + 2, dve.tensor_tensor(eq[:], probs[:], wide(mx), ALU.is_ge))
                    gate(step + 3, dve.tensor_tensor(key[:], eq[:], rank_sb[:], ALU.mult))
                    gate(step + 4, dve.tensor_reduce(mx[:], key[:], AX.X, ALU.max))
                    gate(step + 5, dve.tensor_tensor(chosen[:], key[:], wide(mx), ALU.is_equal))
                    step += 5
                    if chosen is s1:
                        gate(9, dve.scalar_tensor_tensor(out=lg[:], in0=s1[:], scalar=-2.0, in1=pe_[:], op0=ALU.mult,
                                                         op1=ALU.add))
                        step = 9
                gate(15, dve.tensor_tensor(s1[:], s1[:], s2[:], ALU.add))
                gate(16, dve.tensor_tensor(comb[:], pe_[:], s1[:], ALU.mult))
                gate(17, dve.tensor_reduce(mx[:], comb[:], AX.X, ALU.add))
                gate(18, dve.reciprocal(sq[:], mx[:]))
                gate(19, dve.tensor_tensor(comb[:], comb[:], wide(sq), ALU.mult))

                dve.wait_ge(*silu(it, 1))
                dve.tensor_tensor(HH[0:I, 4, :], sg[0:I, 0, :], ps[0:I, 3, :], ALU.mult).then_inc(h_ready.sem, 1)
                dve.wait_ge(*ct_hi(it, 1))
                dve.tensor_tensor(CT[32:32 + E, :], ps[0:E, BK_C, :], CT[0:E, :].bitcast(F32), ALU.subtract)\
                    .then_inc(ct_lo.sem, 1)
                for n in range(1, 5):
                    a = 2 + 2 * (n % 2)
                    dve.wait_ge(*silu(it, n + 1))
                    dve.tensor_tensor(hu[:, n % 2, :], sg[:, n % 2, :], ps[:, a + 1, :], ALU.mult).then_inc(hu_ready.sem, 1)
                    dve.wait_ge(*hu_ready(it, n))
                    dve.wait_ge(*cb_ps(it, n))
                    dve.tensor_tensor(HH[:, n - 1, :], hu[:, n % 2, :], ps[:, (n - 1) % 2, :], ALU.mult)\
                        .then_inc(h_ready.sem, 1)
                dve.wait_ge(*y_ps(it, 3))
                dve.tensor_tensor(y_sb[:], hres[:], ps[:, BK_O, :].rearrange("p (t c) -> p t c", t=NT), ALU.add)\
                    .then_inc(y_ready.sem, 1)
                dve.wait_ge(*y_ready(it, 3))
                moments(it, 5, y_sb)
                layer_var(it, 5)
                normalise(y_sb, y_sb).then_inc(y_normed.sem, 1)
                dve.wait_ge(*y_normed(it, 2))
                dve.tensor_tensor(y_sb[:], x_cur[:], y_sb[:], ALU.add).then_inc(out_ready.sem, 1)
                dve.wait_ge(*out_ready(it, 1))


def _constants(np):
    ident = np.eye(P, dtype=np.float32)
    k_above_q = np.triu(np.full((P, P), NEG, np.float32), 1)
    masks = np.stack([k_above_q, k_above_q.T], axis=1)
    t = np.arange(T, dtype=np.float32)[:, None]

    def table(freqs):
        ang = (t * freqs[None, :].astype(np.float32)).astype(np.float32).astype(np.float64)
        return np.cos(ang).astype(np.float32).T, np.sin(ang).astype(np.float32).T

    half1 = D1 // 2
    cos1, sin1 = table(1.0 / np.float32(10000.0) ** (np.arange(half1, dtype=np.float32) / np.float32(half1)))
    d = np.arange(D1)
    rope1 = np.stack([cos1[d % half1], np.where(d < half1, -1, 1)[:, None].astype(np.float32) * sin1[d % half1]], axis=1)
    rope1 = np.repeat(rope1, H, axis=0)
    cos2, sin2 = table(1.0 / np.float32(100000.0) ** (np.arange(0, ROPE, 2, dtype=np.float32) / np.float32(ROPE)))
    d = np.arange(ROPE)
    rope2 = np.stack([cos2[d // 2], np.where(d % 2 == 0, -1, 1)[:, None].astype(np.float32) * sin2[d // 2]], axis=1)
    ropeq = np.repeat(rope2, H, axis=0).reshape(4, P, 2, T).transpose(1, 0, 2, 3)
    plain = np.zeros((LAT, 2, T), np.float32)
    plain[:, 0] = 1
    ropek = np.concatenate([plain, rope2, plain, rope2, np.zeros((P - 2 * DK2, 2, T), np.float32)])
    rank = np.broadcast_to(np.arange(E, 0, -1, dtype=np.float32), (P, NT, E))
    rows = np.zeros((P, E // 2, P), np.float32)
    for e in range(E):
        for r in (e, 32 + e):
            rows[r, e // 2, I * (e % 2):I * (e % 2) + I] = 1
    return dict(ident=ident, masks=masks, rope1=rope1, ropek=ropek, ropeq=ropeq, rank=rank, expert_rows=rows)


def _layouts(np, w):
    a = {k: np.asarray(v) for k, v in w.items()}
    d, h = np.meshgrid(np.arange(D1), np.arange(H), indexing="ij")
    plain1, turned1 = (h * D1 + d).ravel(), (h * D1 + (d + D1 // 2) % D1).ravel()
    wq, wk = a["L0_attn_Wq"], a["L0_attn_Wk"]
    wqkv = np.stack([wq[plain1].T, wq[turned1].T, wk[plain1].T, wk[turned1].T, a["L0_attn_Wv"].T], axis=1)
    kva = a["L0_ffn_Wkva"]
    zeros = np.zeros((C, P - 2 * DK2), kva.dtype)
    turned = np.arange(ROPE) ^ 1
    kturned = np.concatenate([np.zeros((C, LAT), kva.dtype), kva[:, LAT:][:, turned]], axis=1)
    wkva = np.stack([np.concatenate([kva, kva, zeros], axis=1), np.concatenate([kturned, kturned, zeros], axis=1)], axis=1)
    wq2 = a["L0_ffn_Wq"].reshape(C, H, D2)
    rope = wq2[:, :, NOPE:].transpose(0, 2, 1)
    wq_rope = np.stack([rope.reshape(C, 4, P), rope[:, turned].reshape(C, 4, P)], axis=1)
    wkvb = a["L0_ffn_Wkvb"].reshape(LAT, H, NOPE).transpose(2, 1, 0)
    wo2 = a["L0_ffn_Wo"].reshape(H, D2, C)[:, :NOPE].transpose(1, 0, 2)
    wg, wu = (a[k].reshape(E // 2, 2, C, I).transpose(2, 0, 1, 3).reshape(C, E // 2, P) for k in ("L0_ffn_Wg", "L0_ffn_Wu"))
    return dict(
        x=a["L0_attn_x"].reshape(B * T, C), x_ahead=np.roll(a["L0_attn_x"], -1, axis=0).reshape(B * T, C), wqkv=wqkv, wo1=a["L0_attn_Wo"].T, wkva=wkva,
        wq_nope=wq2[:, :, :NOPE].transpose(2, 1, 0), wq_rope=wq_rope, wkvb=wkvb, wo2=wo2,
        ln1w=a["L0_ffn_w_ln1"].reshape(C, 1), ln2w=a["L0_ffn_w_ln2"].reshape(C, 1), wgate=a["L0_ffn_Wgate"],
        gbias=np.broadcast_to(a["L0_ffn_expert_bias"], (P, E)), wgu=np.stack([wg, wu], axis=2),
        wgu_s=np.stack([a["L0_ffn_sWg"][0], a["L0_ffn_sWu"][0]], axis=1),
        wd=a["L0_ffn_Wd"].reshape(E // 2, P, C).transpose(1, 0, 2), wd_s=a["L0_ffn_sWd"][0])


def kernel(**inputs):
    import numpy as np
    from concourse import bacc
    from concourse.bass_utils import run_bass_kernel_spmd

    nc = bacc.Bacc("TRN2", target_bir_lowering=False, num_devices=1)
    arrays = {k: np.ascontiguousarray(v) for k, v in {**_layouts(np, inputs), **_constants(np)}.items()}
    aps = {k: nc.dram_tensor(f"in_{k}", v.shape, F32, kind="ExternalInput").ap() for k, v in arrays.items()}
    out = nc.dram_tensor("out_x", (B * T, C), F32, kind="ExternalOutput").ap()
    block_program(nc, out=out, **aps)
    r = run_bass_kernel_spmd(nc, [{f"in_{k}": v for k, v in arrays.items()}], core_ids=[0])
    return r.results[0]["out_x"].reshape(B, T, C)
```

```python
from contextlib import ExitStack

import concourse.bass as bass
from concourse import mybir

F32 = mybir.dt.float32
F32R = mybir.dt.float32r
BF16 = mybir.dt.bfloat16
ALU = mybir.AluOpType
ACT = mybir.ActivationFunctionType
AX = mybir.AxisListType

P = 128
B, T, C = 4, 512, 128
NT = T // P
H = 16
G, HG = 4, 4
D1 = C // H
NOPE, ROPE, LAT = 32, 32, 16
D2 = NOPE + ROPE
DK2 = LAT + ROPE
E, I = 8, 64
EPS = 1e-5
MROW = 96
NEG = -1e30
FILLS = 12
UNITS = 10

PHASES = ((1, 0), (1, 1), (1, 2), (2, 0), (1, 3), (2, 1), (2, 2), (2, 3))
NG = G * len(PHASES)
LAYER = [PHASES[n // G][0] for n in range(NG)]
SEQ = [PHASES[n // G][1] for n in range(NG)]
MSTEPS = [sum(4 if LAYER[m] == 1 else 2 for m in range(n)) for n in range(NG + 1)]


def first_group(layer, b):
    return G * PHASES.index((layer, b))


def beside():
    def prep1(b, at):
        names = (("ln1", 0), ("ln1n", 0), ("x1T", 0), ("q1", 0), ("k1", 0), ("parts1", 0), ("store1", 0))
        return [(*slot, name, b, part) for slot, (name, part) in zip(at, names)]

    def row(b, *stages):
        return [(n, h, name, b, part) for (n, h), name, part in stages]

    def experts(b, n, tight):
        k = 4 * n
        order = [("o2T", 0), ("o2y", 0), ("rms2", 0), ("x3T", 0), ("logit", 0), ("shared", 0), ("pairA", 0), ("route", 0),
                 ("combT", 0), ("pairB", 0), ("pairA", 1), ("pairB", 1), ("pairA", 2), ("pairB", 2), ("pairA", 3),
                 ("pairB", 3), ("y3", 0), ("fin", 0)]
        slots = ((1, 2, 3, 4, 5, 5, 6, 6, 7, 8, 8, 9, 9, 10, 10, 11, 12, 13) if tight else
                 (1, 2, 3, 4, 5, 6, 7, 7, 8, 9, 10, 11, 12, 13, 14, 15, 16, 17))
        return [((k + s) // 4, (k + s) % 4, name, b, part) for s, (name, part) in zip(slots, order)]

    plan = []
    pre = -3
    plan += [(pre, 0, name, 0, 0) for name in ("ln1", "ln1n", "x1T", "q1", "k1", "parts1", "v1", "v1c", "store1")]
    plan += [(pre, 0, "load1", 0, g) for g in range(G)]
    plan += prep1(1, ((-2, 0), (-2, 1), (-2, 2), (-2, 3), (-1, 0), (-1, 2), (-1, 3)))
    plan += row(1, ((-1, 1), "v1", 0), ((4, 2), "v1c", 0))
    plan += [(1 + g, 0, "load1", 1, g) for g in range(G)]
    plan += row(0, ((0, 2), "wprod", 0), ((0, 3), "wturn", 0))
    plan += prep1(2, ((1, 1), (1, 2), (1, 3), (2, 1), (2, 2), (2, 3), (3, 1)))
    plan += row(2, ((4, 3), "v1", 0), ((8, 2), "v1c", 0))
    plan += [(5 + g, 0, "load1", 2, g) for g in range(G)]
    plan += row(0, ((5, 1), "o1T", 0), ((5, 2), "o1y", 0), ((5, 3), "lna", 0), ((6, 0), "lnb", 0), ((6, 1), "rms", 0),
                ((6, 2), "x2T", 0), ((6, 3), "kst", 0), ((7, 0), "latv", 0), ((7, 0), "qabs", 0), ((7, 1), "qabs", 1),
                ((7, 1), "kst2", 0), ((7, 2), "ropeA", 0), ((7, 3), "ropeB", 0), ((7, 3), "ropeA", 1),
                ((8, 0), "ropeB", 1), ((8, 0), "ropeA", 2), ((8, 1), "ropeB", 2), ((8, 1), "ropeA", 3),
                ((8, 2), "ropeB", 3), ((8, 3), "load2", 0), ((9, 0), "load2", 1), ((9, 1), "load2", 2),
                ((9, 2), "load2", 3))
    plan += prep1(3, ((8, 3), (9, 0), (9, 1), (9, 2), (9, 3), (10, 1), (10, 2)))
    plan += row(3, ((10, 0), "v1", 0), ((12, 2), "v1c", 0))
    plan += [(12, g, "load1", 3, g) for g in range(G)]
    plan += row(1, ((9, 2), "o1T", 0), ((10, 3), "o1y", 0), ((11, 0), "lna", 0), ((11, 1), "lnb", 0), ((11, 2), "rms", 0),
                ((11, 3), "x2T", 0), ((12, 0), "kst", 0), ((12, 1), "latv", 0), ((12, 1), "qabs", 0),
                ((12, 3), "qabs", 1), ((12, 3), "kst2", 0), ((13, 0), "ropeA", 0), ((13, 1), "ropeB", 0),
                ((13, 1), "ropeA", 1), ((13, 2), "ropeB", 1), ((13, 2), "ropeA", 2), ((13, 3), "ropeB", 2),
                ((13, 3), "ropeA", 3), ((14, 0), "ropeB", 3), ((16, 3), "load2", 0), ((17, 0), "load2", 1),
                ((17, 1), "load2", 2), ((17, 2), "load2", 3))
    plan += row(2, ((14, 1), "o1T", 0), ((14, 2), "o1y", 0), ((14, 3), "lna", 0), ((15, 0), "lnb", 0), ((15, 1), "rms", 0),
                ((15, 2), "x2T", 0), ((15, 3), "qabs", 0), ((16, 0), "qabs", 1), ((16, 1), "kst", 0),
                ((16, 2), "latv", 0), ((16, 2), "kst2", 0), ((17, 0), "ropeA", 0), ((17, 1), "ropeB", 0),
                ((17, 1), "ropeA", 1), ((17, 2), "ropeB", 1), ((17, 2), "ropeA", 2), ((17, 3), "ropeB", 2),
                ((17, 3), "ropeA", 3), ((18, 0), "ropeB", 3), ((21, 0), "load2", 0), ((22, 0), "load2", 1),
                ((23, 0), "load2", 2), ((24, 0), "load2", 3))
    plan += row(0, ((20, 0), "experts_in", 0))
    plan += row(0, ((18, 1), "o2T", 0), ((18, 2), "o2y", 0), ((18, 3), "rms2", 0), ((20, 1), "x3T", 0), ((20, 2), "logit", 0),
                ((20, 3), "shared", 0), ((21, 0), "pairA", 0), ((21, 0), "route", 0), ((21, 1), "combT", 0),
                ((21, 2), "pairB", 0), ((22, 2), "pairA", 1), ((22, 3), "pairB", 1), ((23, 1), "pairA", 2),
                ((23, 2), "pairB", 2), ((23, 3), "pairA", 3), ((24, 0), "pairB", 3), ((24, 3), "y3", 0), ((25, 0), "fin", 0))
    plan += row(3, ((21, 1), "o1T", 0), ((21, 2), "o1y", 0), ((21, 3), "lna", 0), ((22, 0), "lnb", 0), ((22, 1), "rms", 0),
                ((22, 2), "x2T", 0), ((22, 3), "qabs", 0), ((23, 0), "qabs", 1), ((23, 1), "ropeA", 0),
                ((23, 2), "ropeB", 0), ((23, 2), "ropeA", 1), ((23, 3), "ropeB", 1), ((23, 3), "ropeA", 2),
                ((24, 0), "ropeB", 2), ((24, 1), "kst", 0), ((24, 2), "latv", 0), ((24, 2), "kst2", 0),
                ((24, 2), "ropeA", 3), ((24, 3), "ropeB", 3), ((25, 0), "load2", 0), ((26, 0), "load2", 1),
                ((27, 0), "load2", 2), ((28, 0), "load2", 3))
    plan += experts(1, 25, False)
    plan += experts(2, 29, True)
    plan += experts(3, 33, True)
    return sorted(plan, key=lambda e: (e[0], e[1]))


BESIDE = beside()
LAST = max(e[0] for e in BESIDE)

TAKES = {"x1T": (1, 0, 0, 0), "q1": (2, 0, 1, 0), "k1": (2, 0, 1, 0), "v1": (1, 0, 0, 0), "wprod": (2, 0, 0, 0),
         "wturn": (1, 0, 0, 0), "ln1": (0, 1, 0, 0), "ln1n": (0, 0, 0, 1), "o1T": (1, 0, 0, 0), "o1y": (1, 1, 0, 0),
         "lna": (0, 1, 0, 0), "lnb": (0, 1, 0, 0), "rms": (0, 0, 0, 1), "x2T": (1, 0, 0, 0), "kst": (2, 0, 1, 0),
         "latv": (1, 0, 0, 0), "qabs": (1, 0, 0, 0), "ropeA": (2, 0, 1, 0), "o2T": (2, 0, 0, 0), "o2y": (1, 1, 0, 0),
         "rms2": (0, 0, 0, 1), "x3T": (1, 0, 0, 0), "logit": (1, 0, 0, 0), "combT": (1, 0, 0, 0), "shared": (2, 0, 0, 0),
         "pairA": (2, 0, 0, 0), "pairB": (1, 0, 0, 0), "y3": (1, 1, 0, 0)}
BANK0, NORM0, JOB0, TILE0, TURN_OF = {}, {}, {}, {}, []
_n = [0, 0, 0, 0]
for _, _, _stage, _b, _part in BESIDE:
    BANK0[_stage, _b, _part], NORM0[_stage, _b], JOB0[_stage, _b, _part], TILE0[_stage, _b] = _n
    if _stage in ("x1T", "x2T", "x3T"):
        TURN_OF.append(_n[0])
    _n = [a + t for a, t in zip(_n, TAKES.get(_stage, (0, 0, 0, 0)))]
QTILE = {}
for _, _, _stage, _b, _part in BESIDE:
    if _stage in ("qabs", "ropeB"):
        QTILE[_stage, _b, _part] = len(QTILE)


ONT_AFTER, _k = {}, 0
for _, _, _stage, _b, _ in BESIDE:
    if _stage in ("o1T", "o2T"):
        _k += TAKES[_stage][0]
        ONT_AFTER[_stage, _b] = _k


def block_program(nc, x, wqkv, wo1, wkva, wq_nope, wq_rope, wkvb, wo2, ln1w, ln2w, wgate, gbias, wgu, wgu_s, wd,
                  wd_s, ident, masks, rope1, ropek, ropeq, rank, expert_rows, out):
    with ExitStack() as ctx:
        def sb(name, shape, dt=F32):
            return ctx.enter_context(nc.sbuf_tensor(name, shape, dt))

        def sem(name):
            return ctx.enter_context(nc.semaphore(name))

        wqkv_sb = sb("wqkv_sb", [P, 5, C])
        wo1_sb = sb("wo1_sb", [P, C])
        wkva_sb = sb("wkva_sb", [P, 2, P])
        wqr_sb = sb("wqr_sb", [P, 2, 4, P])
        wabs_sb = sb("wabs_sb", [P, 2, P])
        wco_sb = sb("wco_sb", [P, 2, C])
        ln1w_sb = sb("ln1w_sb", [P, 1])
        ln2w_sb = sb("ln2w_sb", [P, 1])
        wgate_sb = sb("wgate_sb", [P, E])
        gbias_sb = sb("gbias_sb", [P, E])
        ident_sb = sb("ident_sb", [P, P])
        identb = sb("identb", [P, P], BF16)
        maskb = sb("maskb", [P, 2, P], BF16)
        rope1_sb = sb("rope1_sb", [P, 2, T])
        ropek_sb = sb("ropek_sb", [P, 2, T])
        ropeq_sb = sb("ropeq_sb", [P, 2, T])
        rank_sb = sb("rank_sb", [P, NT, E])
        erow = sb("erow", [P, 4, P], F32R)
        half = sb("half", [P, NT])

        xs = [sb(f"x{b}", [P, NT, C]) for b in range(B)]
        xn = sb("xn", [P, NT, C])
        y_b = sb("y_b", [P, NT, C])
        stats = [sb(f"stats{k}", [P, NT, 6]) for k in range(3)]
        mv = [sb(f"mv{k}", [P, NT, 2]) for k in range(3)]
        ve = [sb(f"ve{k}", [P, NT]) for k in range(3)]
        sq = [sb(f"sq{k}", [P, NT]) for k in range(3)]
        rstd = [sb(f"rstd{k}", [P, NT]) for k in range(3)]
        xT2 = sb("xT2", [P, T])
        terms = sb("terms", [P, 2, 2, T])
        whole = sb("whole", [P, 2, T])
        vc = sb("vc", [P, NT, C])
        QS1 = sb("QS1", [P, H, T], BF16)
        KS1 = sb("KS1", [P, H, T], BF16)
        V1 = sb("V1", [P, NT, H, 32])
        QC = sb("QC", [P, 2, 2, T], F32R)
        QS2 = sb("QS2", [P, H, T], F32R)
        K1 = sb("K1", [P, 2, T], F32R)
        K2 = sb("K2", [P, 2, T], F32R)
        V2 = sb("V2", [P, 2, NT, 32])
        NM = sb("NM", [P, NT, H])
        MB = sb("MB", [P, NT, 3, HG], BF16)
        MRest = sb("MRest", [P, NT, HG])
        MF = sb("MF", [P, NT, 2, HG], F32R)
        MP = sb("MP", [3 * HG, 2, T])
        PA = sb("PA", [P, 8, 2 * T])
        PC = sb("PC", [P, 4, 2, 256])
        OT = sb("OT", [P, T])
        rec = sb("rec", [P, NT, HG])
        ON1 = sb("ON1", [P, NT, H * D1])
        ONT = sb("ONT", [P, 2, T])
        mx = sb("mx", [P, NT])
        CT = sb("CT", [P, T], F32R)[:]

        pa_flat = PA[:].rearrange("p a t -> p (a t)")[:, 8 * T:16 * T]
        pc_flat = PC[:].rearrange("p a b t -> p (a b t)")
        wqn_sb = pa_flat[0:NOPE, 0:H * C].rearrange("d (h c) -> d h c", h=H)
        wo2_sb = pa_flat[0:NOPE, H * C:2 * H * C].rearrange("d (h c) -> d h c", h=H)
        masks_sb = pc_flat[:, 0:2 * P].rearrange("p (a b) -> p a b", a=2)
        erow_sb = pc_flat[:, 2 * T:3 * T].rearrange("p (a b) -> p a b", a=4)
        wkvb_sb = pc_flat[0:NOPE, 3 * T:3 * T + H * LAT].rearrange("d (h r) -> d h r", h=H)
        wco_t = pc_flat[:, 3 * T + H * LAT:3 * T + 2 * H * LAT].rearrange("p (a b) -> p a b", a=2)
        q_flat = QS1[:].rearrange("p a t -> p (a t)").bitcast(F32)
        HH = q_flat[:, 0:5 * T].rearrange("p (n t) -> p n t", t=T)
        sg = q_flat[:, 5 * T:7 * T].rearrange("p (n t) -> p n t", t=T)
        xT3 = q_flat[:, 7 * T:8 * T]
        k_flat = KS1[:].rearrange("p a t -> p (a t)").bitcast(F32)
        y_c = k_flat[:, 0:T].rearrange("p (t c) -> p t c", t=NT)
        gs = k_flat[:, 2 * T:3 * T]
        wgu_sb = k_flat[:, 4 * T:6 * T].rearrange("p (k a i) -> p k a i", k=4, a=2)
        wd_sb = k_flat[:, 6 * T:7 * T].rearrange("p (k c) -> p k c", k=4)
        wgus_sb = k_flat[:, 7 * T:7 * T + 2 * I].rearrange("p (a i) -> p a i", a=2)
        wds_sb = k_flat[0:I, 7 * T + 2 * I:7 * T + 2 * I + C]
        gates = k_flat[:, 7 * T + 2 * I + C:7 * T + 2 * I + C + 7 * NT * E].rearrange("p (k t e) -> p k t e", k=7, t=NT)
        lg, probs, eq, key, s1, s2, comb = (gates[:, k] for k in range(7))
        room1 = sb("room1", [P, 4 * T])
        qp = room1[:, 0:3 * T // 2].bitcast(BF16).rearrange("p (a t) -> p a t", a=3)
        kp = room1[:, 3 * T // 2:3 * T].bitcast(BF16).rearrange("p (a t) -> p a t", a=3)
        xT1 = room1[:, 3 * T:4 * T]
        ON2 = room1[:, 0:2 * T].rearrange("p (t c) -> p t c", t=NT)
        hres = [sb("hres0", [P, NT, C])[:], room1[:, 3 * T:4 * T].rearrange("p (t c) -> p t c", t=NT),
                room1[:, 2 * T:3 * T].rearrange("p (t c) -> p t c", t=NT),
                k_flat[:, T:2 * T].rearrange("p (t c) -> p t c", t=NT)]

        scr_q = nc.dram_tensor("scr_q", [B, 3, P, T], BF16, kind="Internal")
        scr_k = nc.dram_tensor("scr_k", [B, 5, P, T], BF16, kind="Internal")
        scr_2 = nc.dram_tensor("scr_2", [B, 6, 2, P, T], F32, kind="Internal")

        ps = ctx.enter_context(nc.psum_tensor("ps", [P, 8, T], F32))
        ST0, BK_O, SIDE = 2, 5, 6

        loaded_first, loaded, x_loaded = sem("loaded_first"), sem("loaded"), sem("x_loaded")
        loaded_late = sem("loaded_late")
        consts_ready, cleared = sem("consts_ready"), sem("cleared")
        dve_step = sem("dve_step")
        score_fill, fill_read = sem("score_fill"), sem("fill_read")
        m_step, m_copied = sem("m_step"), sem("m_copied")
        m_stacked = [sem(f"m_stacked{g}") for g in range(G)]
        st_ready, exp_done = sem("st_ready"), sem("exp_done")
        pv, ot_ready, o_turned, on_ready = sem("pv"), sem("ot_ready"), sem("o_turned"), sem("on_ready")
        bank_full = sem("bank_full")
        bank_read = [sem("bank_read0"), sem("bank_read1")]
        var_ready, rstd_ready = sem("var_ready"), sem("rstd_ready")
        xn_ready = sem("xn_ready")
        xT1_ready, xT2_ready, xT3_ready = sem("xT1_ready"), sem("xT2_ready"), sem("xT3_ready")
        terms_ready, whole_ready = sem("terms_ready"), sem("whole_ready")
        job_done = [sem("job_done0"), sem("job_done1")]
        high1, middle1, rest1, low1 = sem("high1"), sem("middle1"), sem("rest1"), sem("low1")
        stored1 = sem("stored1")
        stack1_in = [sem(f"stack1_in{g}") for g in range(G)]
        vc_ready, v1_ready, v2_ready = sem("vc_ready"), sem("v1_ready"), sem("v2_ready")
        k_high, k_low = sem("k_high"), sem("k_low")
        ont_ready, y_ready = sem("ont_ready"), sem("y_ready")
        q_high, q_low = sem("q_high"), sem("q_low")
        q_stored = [sem("q_stored0"), sem("q_stored1")]
        stack2_in = [sem(f"stack2_in{g}") for g in range(G)]
        gate_in, gate_exp, comb_ready, ct_high, ct_low = (sem("gate_in"), sem("gate_exp"), sem("comb_ready"),
                                                          sem("ct_high"), sem("ct_low"))
        tanh_ready, gated, h_ready = sem("tanh_ready"), sem("gated"), sem("h_ready")
        out_ready, out_sent = sem("out_ready"), sem("out_sent")

        FIRST_LOADS = ((ident_sb[:], ident[:]), (wqkv_sb[:], wqkv[:]), (rope1_sb[:], rope1[:]), (masks_sb, masks[:]))
        LOADS = ((wqn_sb, wq_nope[:]), (wo2_sb, wo2[:]), (wkvb_sb, wkvb[:]), (erow_sb, expert_rows[:]),
                 (wo1_sb[:], wo1[:]), (ln1w_sb[:], ln1w[:]), (wkva_sb[:], wkva[:]), (wqr_sb[:], wq_rope[:]),
                 (ropek_sb[:], ropek[:]), (ropeq_sb[:], ropeq[:]), (ln2w_sb[:], ln2w[:]),
                 (wgate_sb[:], wgate[:]), (gbias_sb[:], gbias[:]), (rank_sb[:], rank[:]))
        LATE_LOADS = ((wgu_sb, wgu[:]), (wgus_sb, wgu_s[:]), (wd_sb, wd[:]), (wds_sb, wd_s[:]))
        ALL_FIRST, ALL_LOADED = 16 * len(FIRST_LOADS), 16 * len(LOADS)

        def stream(engine_main, stages):
            for n in range(-3, LAST + 1):
                for hh in range(HG):
                    if n >= -2:
                        engine_main(n, hh)
                    for m, h, stage, b, part in BESIDE:
                        if (m, h) == (n, hh) and stage in stages:
                            stages[stage](b, part)

        block = ctx.enter_context(nc.Block())

        @block.sync
        def _(sp):
            x_seq = x.rearrange("(b n p) c -> b p n c", b=B, p=P)
            out_seq = out.rearrange("(b n p) c -> b p n c", b=B, p=P)
            sp.dma_start(xs[0][:], x_seq[0]).then_inc(x_loaded, 16)
            for dst, src in FIRST_LOADS:
                sp.dma_start(dst, src).then_inc(loaded_first, 16)
            for dst, src in LOADS:
                sp.dma_start(dst, src).then_inc(loaded, 16)

            def main(n, hh):
                m = n + 1
                if hh == 0 and 0 <= m < NG:
                    g = m % G
                    sp.wait_ge(m_copied, m + 1)
                    if LAYER[m] == 1:
                        sp.dma_start(QS1[MROW:MROW + 3, HG * g:HG * g + HG, :],
                                     MP[:, m % 2, 0:T // 2].bitcast(BF16)).then_inc(m_stacked[g], 16)
                    else:
                        sp.dma_start(QS2[MROW:MROW + 2, HG * g:HG * g + HG, :].bitcast(F32),
                                     MP[0:2 * HG, m % 2, :]).then_inc(m_stacked[g], 16)

            def ln1(b, _):
                if b == 0:
                    for k in range(1, B):
                        sp.dma_start(xs[k][:], x_seq[k]).then_inc(x_loaded, 16)

            def store1(b, _):
                sp.wait_ge(low1, 2 * (b + 1))
                sp.dma_start(scr_q[b].rearrange("a p t -> p a t"), qp).then_inc(stored1, 16)
                sp.dma_start(scr_k[b, 0:3].rearrange("a p t -> p a t"), kp).then_inc(stored1, 16)
                sp.dma_start(scr_k[b, 3:5].rearrange("a p t -> p a t"), kp[:, 0:2, :]).then_inc(stored1, 16)

            def load1(b, g):
                sp.wait_ge(stored1, 48 * (b + 1))
                if b == 0:
                    sp.wait_ge(consts_ready, 3)
                else:
                    sp.wait_ge(st_ready, UNITS * (first_group(1, b - 1) + g + 1))
                heads = slice(HG * g, HG * g + HG)
                for a in range(3):
                    sp.dma_start(QS1[24 * a:24 * a + 24, heads, :],
                                 scr_q[b].rearrange("a (d h) t -> (a d) h t", h=H)[:, heads, :]).then_inc(stack1_in[g], 16)
                    sp.dma_start(KS1[24 * a:24 * a + 24, heads, :],
                                 scr_k[b, a:a + 3].rearrange("a (d h) t -> (a d) h t", h=H)[:, heads, :])\
                      .then_inc(stack1_in[g], 16)

            def store2(stage):
                def _(b, part):
                    c = QTILE[stage, b, part]
                    sp.wait_ge(q_low, c + 1)
                    tile = part if stage == "qabs" else 2 + part
                    sp.dma_start(scr_2[b, tile].rearrange("a p t -> p a t"), QC[:, c % 2, :, :].bitcast(F32))\
                      .then_inc(q_stored[c % 2], 16)
                return _

            def load2(b, g):
                tiles = [QTILE["qabs", b, 0], QTILE["qabs", b, 1], QTILE["ropeB", b, g]]
                for k in range(2):
                    sp.wait_ge(q_stored[k], 16 * max([c // 2 + 1 for c in tiles if c % 2 == k] + [1]))
                if b == 0:
                    sp.wait_ge(cleared, 1)
                else:
                    sp.wait_ge(st_ready, UNITS * (first_group(2, b - 1) + g + 1))
                heads = slice(HG * g, HG * g + HG)
                for a in range(2):
                    for t in range(2):
                        sp.dma_start(QS2[DK2 * a + 8 * t:DK2 * a + 8 * t + 8, heads, :].bitcast(F32),
                                     scr_2[b, t, a].rearrange("(r h) t -> r h t", h=H)[:, heads, :])\
                          .then_inc(stack2_in[g], 16)
                    sp.dma_start(QS2[DK2 * a + LAT:DK2 * a + DK2, heads, :].bitcast(F32),
                                 scr_2[b, 2 + g, a].rearrange("(h d) t -> d h t", h=HG)).then_inc(stack2_in[g], 16)

            def experts_in(b, _):
                sp.wait_ge(st_ready, UNITS * (first_group(1, B - 1) + G))
                for dst, src in LATE_LOADS:
                    sp.dma_start(dst, src).then_inc(loaded_late, 16)

            def fin(b, _):
                sp.wait_ge(out_ready, b + 1)
                sp.dma_start(out_seq[b], xs[b][:]).then_inc(out_sent, 16)

            stream(main, dict(ln1=ln1, store1=store1, load1=load1, qabs=store2("qabs"), ropeB=store2("ropeB"),
                              load2=load2, experts_in=experts_in, fin=fin))
            sp.wait_ge(out_sent, 16 * B)

        @block.tensor
        def _(pe):
            def products(dst, n, h, i, k):
                if LAYER[n] == 1:
                    pe.matmul(dst, QS1[0:MROW, h, P * i:P * i + P], KS1[0:MROW, h, 0:P * k], start=True, stop=False)
                else:
                    pe.matmul(dst, QS2[0:MROW, h, P * i:P * i + P], K1[0:MROW, SEQ[n] % 2, 0:P * k], start=True,
                              stop=False)
                return pe.matmul(dst[:, P * (k - 1):P * k], identb[:], maskb[:, 0, :], start=False, stop=True)

            def fill(n, k):
                if k == 1 and n:
                    pe.wait_ge(m_copied, n)
                elif k >= 2 or n:
                    pe.wait_ge(fill_read, n * (FILLS - 1) + k - 1)
                return ps[:, (n * FILLS + k) % 2, :]

            def scores_for_max(n, hh):
                h = HG * (n % G) + hh
                k = 2 * hh + hh // 2
                products(fill(n, k), n, h, 3, 4).then_inc(score_fill, 1)
                products(fill(n, k + 1)[:, 0:3 * P], n, h, 2, 3).then_inc(score_fill, 1)
                if hh % 2:
                    bank = fill(n, k + 2)
                    for j in range(2):
                        mm = products(bank[:, 256 * j:256 * j + 256], n, h - 1 + j, 1, 2)
                    mm.then_inc(score_fill, 1)
                if hh == HG - 1:
                    bank = fill(n, k + 3)
                    for j in range(HG):
                        mm = products(bank[:, P * j:P * j + P], n, h - hh + j, 0, 1)
                    mm.then_inc(score_fill, 1)

            def turn_max(n):
                pe.wait_ge(m_step, MSTEPS[n + 1])
                pe.wait_ge(fill_read, n * (FILLS - 1) + FILLS - 2)
                bank = ps[:, (n * FILLS + FILLS - 1) % 2, :]
                for t in range(NT):
                    if LAYER[n] == 1:
                        mm = pe.transpose(bank[0:3 * HG, :].bitcast(BF16)[:, P * t:P * t + P],
                                          MB[:, t, :, :].rearrange("p a h -> p (a h)"), identb[:])
                    else:
                        mm = pe.transpose(bank[0:2 * HG, P * t:P * t + P],
                                          MF[:, t, :, :].bitcast(F32).rearrange("p a h -> p (a h)"), ident_sb[:])
                mm.then_inc(score_fill, 1)

            def scores_t(dst, n, h, j):
                q0 = P * j
                if LAYER[n] == 1:
                    pe.matmul(dst, KS1[:, h, q0:q0 + P], QS1[:, h, q0:T], start=True, stop=False)
                else:
                    for keys in (K1, K2):
                        pe.matmul(dst, keys[:, SEQ[n] % 2, q0:q0 + P], QS2[:, h, q0:T], start=(keys is K1), stop=False)
                return pe.matmul(dst[:, 0:P], identb[:], maskb[:, 1, :], start=False, stop=True)

            def scores_for_exp(n, hh):
                h = HG * (n % G) + hh
                u = n * UNITS + 5 * (hh // 2) + 2 * (hh % 2)
                if hh == 0:
                    pe.wait_ge(m_stacked[n % G], 16 * (n // G + 1))

                def unit(u):
                    if u >= 3:
                        pe.wait_ge(exp_done, u - 2)
                    return ps[:, ST0 + u % 3, :]

                scores_t(unit(u), n, h, 0).then_inc(st_ready, 1)
                bank = unit(u + 1)
                scores_t(bank[:, 0:3 * P], n, h, 1)
                scores_t(bank[:, 3 * P:T], n, h, 3).then_inc(st_ready, 1)
                if hh % 2:
                    bank = unit(u + 2)
                    scores_t(bank[:, 0:256], n, h - 1, 2)
                    scores_t(bank[:, 256:T], n, h, 2).then_inc(st_ready, 1)

            def values(n):
                pe.wait_ge(exp_done, UNITS * (n + 1))
                if n:
                    pe.wait_ge(on_ready, n)
                if n % G == 0:
                    pe.wait_ge(v1_ready if LAYER[n] == 1 else v2_ready, SEQ[n] + 1)
                for j in range(NT):
                    for hh in range(HG):
                        h = HG * (n % G) + hh
                        slot = h % 8
                        p = (PA[:, slot, 0:T], PA[:, slot, T:T + 3 * P], PC[:, slot // 2, hh % 2, :],
                             PA[:, slot, T + 3 * P:2 * T])[j]
                        v = V1[:, j, h, :] if LAYER[n] == 1 else V2[:, SEQ[n] % 2, j, :]
                        mm = pe.matmul(ps[32 * hh:32 * hh + 32, BK_O, P * j:T], v, p, start=(j == 0), stop=(j == NT - 1),
                                       skip_group_check=True)
                mm.then_inc(pv, 1)

            def turn_out(n):
                pe.wait_ge(ot_ready, n + 1)
                for t in range(NT):
                    mm = pe.transpose(ps[:, BK_O, P * t:P * t + P], OT[:, P * t:P * t + P], ident_sb[:])
                mm.then_inc(o_turned, 1)

            def main(n, hh):
                if 0 <= n < NG:
                    scores_for_exp(n, hh)
                if hh == 0 and 0 <= n + 1 < NG:
                    turn_max(n + 1)
                if n + 2 < NG:
                    m = n + 2
                    if hh == 0:
                        if LAYER[m] == 1:
                            pe.wait_ge(stack1_in[m % G], 96 * (SEQ[m] + 1))
                        else:
                            pe.wait_ge(stack2_in[m % G], 96 * (SEQ[m] + 1))
                            pe.wait_ge(k_low, SEQ[m] + 1)
                    scores_for_max(m, hh)
                if hh == 1 and 1 <= n <= NG:
                    values(n - 1)
                if hh == 3 and 1 <= n <= NG:
                    turn_out(n - 1)

            def bank(u):
                if u >= 2:
                    pe.wait_ge(bank_read[u % 2], u // 2)
                return ps[:, SIDE + u % 2, :]

            def turn_tile(stage):
                def _(b, part):
                    u = BANK0[stage, b, part]
                    pe.wait_ge(xn_ready, TURN_OF.index(u) + 1)
                    dst = bank(u)
                    for t in range(NT):
                        mm = pe.transpose(dst[:, P * t:P * t + P], xn[:, t, :], ident_sb[:])
                    mm.then_inc(bank_full, 1)
                return _

            def project(u, w, xT, rows=P):
                pe.matmul(bank(u)[0:rows, :], w, xT, start=True, stop=True).then_inc(bank_full, 1)

            def q1(b, _):
                pe.wait_ge(xT1_ready, b + 1)
                for k in range(2):
                    project(BANK0["q1", b, 0] + k, wqkv_sb[:, k, :], xT1)

            def k1(b, _):
                for k in range(2):
                    project(BANK0["k1", b, 0] + k, wqkv_sb[:, 2 + k, :], xT1)

            def v1(b, _):
                dst = bank(BANK0["v1", b, 0])
                for t in range(NT):
                    mm = pe.matmul(dst[:, P * t:P * t + P], xT1[:, P * t:P * t + P], wqkv_sb[:, 4, :], start=True, stop=True)
                mm.then_inc(bank_full, 1)

            def wprod(b, _):
                u = BANK0["wprod", 0, 0]
                pe.wait_ge(loaded, ALL_LOADED)
                for k, w in enumerate((wqn_sb, wo2_sb)):
                    dst = bank(u + k)
                    for h in range(H):
                        mm = pe.matmul(dst[:, LAT * h:LAT * h + LAT], w[:, h, :], wkvb_sb[:, h, :], start=True, stop=True)
                    mm.then_inc(bank_full, 1)

            def wturn(b, _):
                u = BANK0["wturn", 0, 0]
                pe.wait_ge(bank_read[(u - 1) % 2], (u - 1) // 2 + 1)
                dst = bank(u)
                for a in range(2):
                    mm = pe.transpose(dst[:, P * a:P * a + P], wco_t[:, a, :], ident_sb[:])
                mm.then_inc(bank_full, 1)

            def o1T(b, _):
                pe.wait_ge(on_ready, first_group(1, b) + G)
                dst = bank(BANK0["o1T", b, 0])
                for t in range(NT):
                    mm = pe.transpose(dst[:, P * t:P * t + P], ON1[:, t, :], ident_sb[:])
                mm.then_inc(bank_full, 1)

            def outputs(stage, ready, weights):
                def _(b, part):
                    pe.wait_ge(ont_ready, ready(b))
                    dst = bank(BANK0[stage, b, 0])
                    for t in range(NT):
                        for a, w in enumerate(weights):
                            mm = pe.matmul(dst[:, P * t:P * t + P], ONT[:, a, P * t:P * t + P], w, start=(a == 0),
                                           stop=(a == len(weights) - 1))
                    mm.then_inc(bank_full, 1)
                return _

            def kst(b, _):
                pe.wait_ge(xT2_ready, b + 1)
                for k in range(2):
                    project(BANK0["kst", b, 0] + k, wkva_sb[:, k, :], xT2[:])

            def latv(b, _):
                pe.wait_ge(xT2_ready, b + 1)
                dst = bank(BANK0["latv", b, 0])
                for t in range(NT):
                    mm = pe.matmul(dst[:, LAT * t:LAT * t + LAT], xT2[:, P * t:P * t + P], wkva_sb[:, 0, 0:LAT], start=True,
                                   stop=True)
                mm.then_inc(bank_full, 1)

            def qabs(b, part):
                pe.wait_ge(xT2_ready, b + 1)
                project(BANK0["qabs", b, part], wabs_sb[:, part, :], xT2[:])

            def ropeA(b, part):
                pe.wait_ge(xT2_ready, b + 1)
                for k in range(2):
                    project(BANK0["ropeA", b, part] + k, wqr_sb[:, k, part, :], xT2[:])

            def o2T(b, _):
                pe.wait_ge(on_ready, first_group(2, b) + G)
                for a in range(2):
                    dst = bank(BANK0["o2T", b, 0] + a)
                    for t in range(NT):
                        mm = pe.transpose(dst[:, P * t:P * t + P], ON2[:, t, P * a:P * a + P], ident_sb[:])
                    mm.then_inc(bank_full, 1)

            def logit(b, _):
                pe.wait_ge(xT3_ready, b + 1)
                dst = bank(BANK0["logit", b, 0])
                for t in range(NT):
                    mm = pe.matmul(dst[:, E * t:E * t + E], xT3[:, P * t:P * t + P], wgate_sb[:], start=True, stop=True)
                mm.then_inc(bank_full, 1)

            def shared(b, _):
                pe.wait_ge(loaded_late, 16 * len(LATE_LOADS))
                for k in range(2):
                    project(BANK0["shared", b, 0] + k, wgus_sb[:, k, :], xT3, rows=I)

            def pairA(b, part):
                for k in range(2):
                    project(BANK0["pairA", b, part] + k, wgu_sb[:, part, k, :], xT3)

            def combT(b, _):
                pe.wait_ge(comb_ready, b + 1)
                dst = bank(BANK0["combT", b, 0])
                for t in range(NT):
                    mm = pe.transpose(dst[0:E, P * t:P * t + P], comb[:, t, :], ident_sb[:])
                mm.then_inc(bank_full, 1)

            def pairB(b, part):
                pe.wait_ge(ct_low, b + 1)
                project(BANK0["pairB", b, part], erow[:, part, :], CT)

            def y3(b, _):
                pe.wait_ge(h_ready, 5 * (b + 1))
                dst = bank(BANK0["y3", b, 0])
                for t in range(NT):
                    pe.matmul(dst[:, P * t:P * t + P], HH[0:I, 4, P * t:P * t + P], wds_sb, start=True, stop=False)
                    for k in range(4):
                        mm = pe.matmul(dst[:, P * t:P * t + P], HH[:, k, P * t:P * t + P], wd_sb[:, k, :], start=False,
                                       stop=(k == 3))
                mm.then_inc(bank_full, 1)

            pe.wait_ge(loaded_first, ALL_FIRST)
            pe.wait_ge(consts_ready, 3)
            stream(main, dict(
                x1T=turn_tile("x1T"), q1=q1, k1=k1, v1=v1, wprod=wprod, wturn=wturn, o1T=o1T,
                o1y=outputs("o1y", lambda b: ONT_AFTER["o1T", b], [wo1_sb[:]]), x2T=turn_tile("x2T"), kst=kst, latv=latv,
                qabs=qabs, ropeA=ropeA, o2T=o2T,
                o2y=outputs("o2y", lambda b: ONT_AFTER["o2T", b], [wco_sb[:, 0, :], wco_sb[:, 1, :]]),
                x3T=turn_tile("x3T"), logit=logit, shared=shared, pairA=pairA, combT=combT, pairB=pairB, y3=y3))

        @block.scalar
        def _(act):
            def main(n, hh):
                m = n + 1
                if 0 <= n < NG:
                    h = HG * (n % G) + hh
                    u = n * UNITS + 5 * (hh // 2) + 2 * (hh % 2)
                    scale = (D1 if LAYER[n] == 1 else D2) ** -0.5
                    if hh == 0 and n >= 2:
                        act.wait_ge(pv, n - 1)
                    if n <= 1 and hh == 0:
                        act.wait_ge(consts_ready, 5 if n else 1)
                    for k in range(2):
                        act.wait_ge(st_ready, u + k + 1)
                        act.activation(PA[:, h % 8, T * k:T * k + T], ps[:, ST0 + (u + k) % 3, :], ACT.Exp, scale=scale)\
                           .then_inc(exp_done, 1)
                    if hh % 2:
                        act.wait_ge(st_ready, u + 3)
                        act.activation(PC[:, (h % 8) // 2, :, :].rearrange("p a t -> p (a t)"), ps[:, ST0 + (u + 2) % 3, :],
                                       ACT.Exp, scale=scale).then_inc(exp_done, 1)
                if hh == 0 and 0 <= m < NG:
                    act.wait_ge(score_fill, FILLS * (m + 1))
                    if m >= 2:
                        act.wait_ge(m_stacked[(m - 2) % G], 16 * ((m - 2) // G + 1))
                    bank = ps[:, (m * FILLS + FILLS - 1) % 2, :]
                    if LAYER[m] == 1:
                        act.activation(MP[:, m % 2, 0:T // 2].bitcast(BF16), bank[0:3 * HG, :].bitcast(BF16)[:, 0:T],
                                       ACT.Copy).then_inc(m_copied, 1)
                    else:
                        act.activation(MP[0:2 * HG, m % 2, :], bank[0:2 * HG, :], ACT.Copy).then_inc(m_copied, 1)
                if hh == 2 and 1 <= n <= NG:
                    act.wait_ge(pv, n)
                    if n >= 2:
                        act.wait_ge(o_turned, n - 1)
                    act.activation(OT[:], ps[:, BK_O, :], ACT.Copy).then_inc(ot_ready, 1)

            def full(u):
                act.wait_ge(bank_full, u + 1)
                return ps[:, SIDE + u % 2, :]

            def take(stage, dst, ready, scale=1.0):
                def _(b, part):
                    src = full(BANK0[stage, b, part])
                    act.activation(dst, src, ACT.Copy, scale=scale).then_inc(ready, 1)
                    act.wait_ge(ready, b + 1)
                    act.sem_inc(bank_read[BANK0[stage, b, part] % 2], 1)
                return _

            def parts1(b, _):
                for k, (stage, parts) in enumerate((("q1", qp), ("k1", kp))):
                    j = JOB0[stage, b, 0]
                    act.wait_ge(whole_ready, j + 1)
                    if b and k == 0:
                        act.wait_ge(stored1, 48 * b)
                    act.activation(parts[:, 0, :], whole[:, j % 2, :], ACT.Copy).then_inc(high1, 1)
                for k, (stage, parts) in enumerate((("q1", qp), ("k1", kp))):
                    j = JOB0[stage, b, 0]
                    act.wait_ge(rest1, 2 * b + k + 1)
                    act.activation(parts[:, 1, :], terms[:, j % 2, 0, :], ACT.Copy).then_inc(middle1, 1)

            def v1(b, _):
                src = full(BANK0["v1", b, 0])
                if b:
                    act.wait_ge(v1_ready, b)
                act.activation(vc[:].rearrange("p t c -> p (t c)"), src, ACT.Copy).then_inc(vc_ready, 1)
                act.wait_ge(vc_ready, b + 1)
                act.sem_inc(bank_read[BANK0["v1", b, 0] % 2], 1)

            def turned(stage):
                def _(b, part):
                    for a in range(TAKES[stage][0]):
                        u = BANK0[stage, b, 0] + a
                        src = full(u)
                        act.activation(ONT[:, a, :], src, ACT.Copy).then_inc(ont_ready, 1)
                        act.wait_ge(ont_ready, ONT_AFTER[stage, b] - TAKES[stage][0] + a + 1)
                        act.sem_inc(bank_read[u % 2], 1)
                return _

            def kst2(b, _):
                j = JOB0["kst", b, 0]
                act.wait_ge(whole_ready, j + 1)
                if b >= 2:
                    act.wait_ge(st_ready, UNITS * (first_group(2, b - 2) + G))
                if b == 0:
                    act.wait_ge(consts_ready, 3)
                act.activation(K1[0:2 * DK2, b % 2, :], whole[0:2 * DK2, j % 2, :], ACT.Copy).then_inc(k_high, 1)

            def latv(b, _):
                src = full(BANK0["latv", b, 0])
                if b >= 2:
                    act.wait_ge(pv, first_group(2, b - 2) + G)
                if b == 0:
                    act.wait_ge(cleared, 2)
                act.activation(V2[:, b % 2, :, 0:LAT], src[:, 0:NT * LAT].rearrange("p (t r) -> p t r", t=NT), ACT.Copy)\
                   .then_inc(v2_ready, 1)
                act.wait_ge(v2_ready, b + 1)
                act.sem_inc(bank_read[BANK0["latv", b, 0] % 2], 1)

            def slot_sent(c):
                if c >= 2:
                    act.wait_ge(q_stored[c % 2], 16 * (c // 2))

            def qabs(b, part):
                c = QTILE["qabs", b, part]
                src = full(BANK0["qabs", b, part])
                slot_sent(c)
                act.activation(QC[:, c % 2, 0, :], src, ACT.Copy).then_inc(q_high, 1)

            def ropeB(b, part):
                c, j = QTILE["ropeB", b, part], JOB0["ropeA", b, part]
                act.wait_ge(whole_ready, j + 1)
                slot_sent(c)
                act.activation(QC[:, c % 2, 0, :], whole[:, j % 2, :], ACT.Copy).then_inc(q_high, 1)

            def logit(b, _):
                act.wait_ge(gate_in, b + 1)
                act.activation(probs, key, ACT.Exp).then_inc(gate_exp, 1)

            def combT(b, _):
                src = full(BANK0["combT", b, 0])
                act.activation(CT[0:E, :], src[0:E, :], ACT.Copy).then_inc(ct_high, 1)

            def tanh(stage):
                def _(b, part):
                    k = 5 * b + (0 if stage == "shared" else part + 1)
                    rows = I if stage == "shared" else P
                    src = full(BANK0[stage, b, part])
                    if k >= 2:
                        act.wait_ge(gated, k - 1)
                    act.activation(sg[0:rows, k % 2, :], src[0:rows, :], ACT.Tanh, scale=0.5).then_inc(tanh_ready, 1)
                return _

            act.wait_ge(loaded_first, ALL_FIRST)
            stream(main, dict(
                x1T=take("x1T", xT1, xT1_ready), v1=v1, parts1=parts1, o1T=turned("o1T"),
                x2T=take("x2T", xT2[:], xT2_ready, ln1w_sb[:]), kst2=kst2, latv=latv, qabs=qabs, ropeB=ropeB,
                o2T=turned("o2T"), x3T=take("x3T", xT3, xT3_ready, ln2w_sb[:]), logit=logit, combT=combT,
                shared=tanh("shared"), pairA=tanh("pairA")))

        @block.gpsimd
        def _(pool):
            def power(stage, chain):
                def _(b, part):
                    k = NORM0[stage, b]
                    pool.wait_ge(var_ready, k + 1)
                    pool.tensor_tensor(rstd[chain][:], ve[chain][:], half[:], ALU.pow).then_inc(rstd_ready, 1)
                return _

            def add_terms(stage):
                def _(b, part):
                    j = JOB0[stage, b, part]
                    pool.wait_ge(terms_ready, j + 1)
                    pool.tensor_tensor(whole[:, j % 2, :], terms[:, j % 2, 0, :], terms[:, j % 2, 1, :], ALU.add)\
                        .then_inc(whole_ready, 1)
                return _

            def parts1(b, _):
                for k, (stage, parts) in enumerate((("q1", qp), ("k1", kp))):
                    j = JOB0[stage, b, 0] % 2
                    pool.wait_ge(high1, 2 * b + k + 1)
                    pool.tensor_tensor(terms[:, j, 0, :], whole[:, j, :], parts[:, 0, :], ALU.subtract).then_inc(rest1, 1)
                for k, (stage, parts) in enumerate((("q1", qp), ("k1", kp))):
                    j = JOB0[stage, b, 0] % 2
                    pool.wait_ge(middle1, 2 * b + k + 1)
                    pool.tensor_tensor(parts[:, 2, :], terms[:, j, 0, :], parts[:, 1, :], ALU.subtract).then_inc(low1, 1)
                    pool.wait_ge(low1, 2 * b + k + 1)
                    pool.sem_inc(job_done[j], 1)

            def v1c(b, _):
                pool.wait_ge(vc_ready, b + 1)
                if b:
                    pool.wait_ge(pv, first_group(1, b - 1) + G)
                pool.tensor_copy(V1[:, :, :, 0:D1], vc[:].rearrange("p t (h d) -> p t h d", h=H)).then_inc(v1_ready, 1)

            def ropeB(b, part):
                c, j = QTILE["ropeB", b, part], JOB0["ropeA", b, part] % 2
                pool.wait_ge(q_high, c + 1)
                if c:
                    pool.wait_ge(q_low, c)
                pool.tensor_tensor(QC[:, c % 2, 1, :], whole[:, j, :], QC[:, c % 2, 0, :].bitcast(F32), ALU.subtract)\
                    .then_inc(q_low, 1)
                pool.wait_ge(q_low, c + 1)
                pool.sem_inc(job_done[j], 1)

            pool.memset(V1[:], 1.0)
            pool.memset(V2[:], 1.0)
            pool.memset(half[:], -0.5).then_inc(cleared, 1)
            pool.wait_ge(cleared, 1)
            pool.memset(QS2[64:P].bitcast(F32), 0.0).then_inc(cleared, 1)
            pool.wait_ge(cleared, 2)
            stream(lambda n, hh: None, dict(
                ln1=power("ln1", 0), q1=add_terms("q1"), k1=add_terms("k1"), parts1=parts1, v1c=v1c,
                o1y=power("o1y", 1), lna=power("lna", 1), lnb=power("lnb", 1), kst=add_terms("kst"),
                ropeA=add_terms("ropeA"), ropeB=ropeB, o2y=power("o2y", 2), y3=power("y3", 2)))

        @block.vector
        def _(dve):
            steps = [0]

            def step(ins):
                steps[0] += 1
                ins.then_inc(dve_step, 1)
                dve.wait_ge(dve_step, steps[0])

            def moments(src, chain):
                for t in range(NT):
                    last = dve.bn_stats(stats[chain][:, t, :], src[:, t, :])
                step(last)
                for t in range(NT):
                    last = dve.bn_aggr(mv[chain][:, t, :], stats[chain][:, t, :])
                step(last)

            def layer_var(chain):
                dve.tensor_scalar(ve[chain][:], mv[chain][:, :, 1], EPS, None, ALU.add).then_inc(var_ready, 1)

            def normalise(dst, src, chain):
                for t in range(NT):
                    last = dve.tensor_scalar(dst[:, t, :], src[:, t, :], mv[chain][:, t, 0:1], rstd[chain][:, t:t + 1],
                                             ALU.subtract, ALU.mult)
                return last

            def rescale(dst, src, chain):
                for t in range(NT):
                    last = dve.tensor_scalar(dst[:, t, :], src[:, t, :], rstd[chain][:, t:t + 1], None, ALU.mult)
                return last

            def full(u):
                dve.wait_ge(bank_full, u + 1)
                return ps[:, SIDE + u % 2, :]

            def reduce_fill(n, k, src, dst):
                dve.wait_ge(score_fill, n * FILLS + k + 1)
                dve.tensor_reduce(dst, src, AX.X, ALU.max, negate=True).then_inc(fill_read, 1)

            def maxima(n, hh):
                h = HG * (n % G) + hh
                k = 2 * hh + hh // 2
                bank = [ps[:, (n * FILLS + k + j) % 2, :] for j in range(4)]
                reduce_fill(n, k, bank[0], NM[:, 3, h:h + 1])
                reduce_fill(n, k + 1, bank[1][:, 0:3 * P], NM[:, 2, h:h + 1])
                if hh % 2:
                    reduce_fill(n, k + 2, bank[2].rearrange("p (a k) -> p a k", a=2), NM[:, 1, h - 1:h + 1])
                if hh == HG - 1:
                    reduce_fill(n, k + 3, bank[3].rearrange("p (a k) -> p a k", a=4), NM[:, 0, h - hh:h + 1])

            def split_max(n):
                m = NM[:, :, HG * (n % G):HG * (n % G) + HG]
                dve.wait_ge(fill_read, (n + 1) * (FILLS - 1))
                if n:
                    dve.wait_ge(score_fill, n * FILLS)
                k = MSTEPS[n]
                if LAYER[n] == 1:
                    dve.tensor_copy(MB[:, :, 0, :], m).then_inc(m_step, 1)
                    dve.wait_ge(m_step, k + 1)
                    dve.tensor_tensor(MRest[:], m, MB[:, :, 0, :], ALU.subtract).then_inc(m_step, 1)
                    dve.wait_ge(m_step, k + 2)
                    dve.tensor_copy(MB[:, :, 1, :], MRest[:]).then_inc(m_step, 1)
                    dve.wait_ge(m_step, k + 3)
                    dve.tensor_tensor(MB[:, :, 2, :], MRest[:], MB[:, :, 1, :], ALU.subtract).then_inc(m_step, 1)
                else:
                    dve.tensor_copy(MF[:, :, 0, :], m).then_inc(m_step, 1)
                    dve.wait_ge(m_step, k + 1)
                    dve.tensor_tensor(MF[:, :, 1, :], m, MF[:, :, 0, :].bitcast(F32), ALU.subtract).then_inc(m_step, 1)

            def divide(n):
                w, on = (D1, ON1) if LAYER[n] == 1 else (LAT, ON2)
                bank = ps[:, BK_O, :].rearrange("p (t h d) -> p t h d", t=NT, h=HG)
                dve.wait_ge(o_turned, n + 1)
                if n % G == 0 and SEQ[n]:
                    stage = "o1T" if LAYER[n] == 1 else "o2T"
                    dve.wait_ge(bank_full, BANK0[stage, SEQ[n] - 1, 0] + TAKES[stage][0])
                if n == first_group(2, 0):
                    dve.wait_ge(stored1, 48 * B)
                step(dve.reciprocal(rec[:], bank[:, :, :, w]))
                dve.tensor_tensor(on[:].rearrange("p t (h d) -> p t h d", h=H)[:, :, HG * (n % G):HG * (n % G) + HG, :],
                                  bank[:, :, :, 0:w], rec[:].unsqueeze(3).to_broadcast([P, NT, HG, w]), ALU.mult)\
                   .then_inc(on_ready, 1)

            def main(n, hh):
                if hh == 0 and 2 <= n <= NG + 1:
                    divide(n - 2)
                if n + 2 < NG:
                    maxima(n + 2, hh)
                    if hh == 3:
                        split_max(n + 2)

            def ln1(b, _):
                dve.wait_ge(x_loaded, 16 if b == 0 else 16 * B)
                moments(xs[b], 0)
                layer_var(0)

            def tile_free(stage, b):
                j = TILE0[stage, b]
                if j:
                    dve.wait_ge(bank_full, TURN_OF[j - 1] + 1)

            def ln1n(b, _):
                dve.wait_ge(rstd_ready, NORM0["ln1", b] + 1)
                tile_free("ln1n", b)
                normalise(xn, xs[b], 0).then_inc(xn_ready, 1)

            def rotation(stage, table):
                def _(b, part):
                    u, j = BANK0[stage, b, part], JOB0[stage, b, part]
                    if j >= 2:
                        dve.wait_ge(job_done[j % 2], j // 2)
                    for k in range(2):
                        src = full(u + k)
                        last = dve.tensor_tensor(terms[:, j % 2, k, :], src, table[:, k, :], ALU.mult)
                        last.then_inc(bank_read[(u + k) % 2], 1)
                    dve.wait_ge(bank_read[(u + 1) % 2], (u + 1) // 2 + 1)
                    dve.sem_inc(terms_ready, 1)
                return _

            def wprod(b, _):
                dve.wait_ge(loaded, ALL_LOADED)
                dve.tensor_copy(erow[:], erow_sb).then_inc(consts_ready, 1)
                u = BANK0["wprod", 0, 0]
                dve.tensor_copy(wabs_sb[:].rearrange("p a b -> p (a b)").rearrange("p (r h) -> p r h", h=H),
                                full(u)[:, 0:H * LAT].rearrange("p (h r) -> p r h", h=H)).then_inc(bank_read[u % 2], 1)
                dve.tensor_copy(wco_t.rearrange("p a b -> p (a b)"), full(u + 1)[:, 0:H * LAT])\
                   .then_inc(bank_read[(u + 1) % 2], 1)

            def wturn(b, _):
                u = BANK0["wturn", 0, 0]
                dve.tensor_copy(wco_sb[:].rearrange("p a b -> p (a b)"), full(u)[:, 0:2 * P]).then_inc(bank_read[u % 2], 1)
                dve.wait_ge(bank_read[u % 2], u // 2 + 1)
                dve.sem_inc(consts_ready, 1)

            def o1y(b, _):
                u = BANK0["o1y", b, 0]
                dve.tensor_copy(y_b[:].rearrange("p t c -> p (t c)"), full(u)).then_inc(bank_read[u % 2], 1)
                dve.wait_ge(bank_read[u % 2], u // 2 + 1)
                moments(y_b, 1)
                layer_var(1)

            def lna(b, _):
                dve.wait_ge(rstd_ready, NORM0["o1y", b] + 1)
                step(normalise(y_b, y_b, 1))
                step(dve.tensor_tensor(xs[b][:], xs[b][:], y_b[:], ALU.add))
                moments(xs[b], 1)
                layer_var(1)

            def lnb(b, _):
                dve.wait_ge(rstd_ready, NORM0["lna", b] + 1)
                if b == 2:
                    dve.wait_ge(stored1, 48 * B)
                normalise(hres[b], xs[b], 1)
                step(dve.tensor_tensor(sq[1][:], mv[1][:, :, 1], rstd[1][:], ALU.mult))
                step(dve.tensor_tensor(sq[1][:], sq[1][:], rstd[1][:], ALU.mult))
                dve.tensor_scalar(ve[1][:], sq[1][:], EPS, None, ALU.add).then_inc(var_ready, 1)

            def rms(b, _):
                dve.wait_ge(rstd_ready, NORM0["lnb", b] + 1)
                tile_free("rms", b)
                rescale(xn, hres[b], 1).then_inc(xn_ready, 1)

            def kst2(b, _):
                j = JOB0["kst", b, 0]
                dve.wait_ge(k_high, b + 1)
                dve.tensor_tensor(K2[0:2 * DK2, b % 2, :], whole[0:2 * DK2, j % 2, :],
                                  K1[0:2 * DK2, b % 2, :].bitcast(F32), ALU.subtract).then_inc(k_low, 1)
                dve.wait_ge(k_low, b + 1)
                dve.sem_inc(job_done[j % 2], 1)

            def qabs(b, part):
                u, c = BANK0["qabs", b, part], QTILE["qabs", b, part]
                dve.wait_ge(q_high, c + 1)
                if c:
                    dve.wait_ge(q_low, c)
                dve.tensor_tensor(QC[:, c % 2, 1, :], full(u), QC[:, c % 2, 0, :].bitcast(F32), ALU.subtract)\
                   .then_inc(q_low, 1)
                dve.wait_ge(q_low, c + 1)
                dve.sem_inc(bank_read[u % 2], 1)

            def o2y(b, _):
                u = BANK0["o2y", b, 0]
                dve.tensor_tensor(hres[b], hres[b], full(u).rearrange("p (t c) -> p t c", t=NT), ALU.add)\
                   .then_inc(bank_read[u % 2], 1)
                dve.wait_ge(bank_read[u % 2], u // 2 + 1)
                moments(hres[b], 2)
                step(dve.tensor_tensor(sq[2][:], mv[2][:, :, 0], mv[2][:, :, 0], ALU.mult))
                dve.scalar_tensor_tensor(out=ve[2][:], in0=sq[2][:], scalar=EPS, in1=mv[2][:, :, 1], op0=ALU.add,
                                         op1=ALU.add).then_inc(var_ready, 1)

            def rms2(b, _):
                dve.wait_ge(rstd_ready, NORM0["o2y", b] + 1)
                tile_free("rms2", b)
                rescale(xn, hres[b], 2).then_inc(xn_ready, 1)

            def wide(v):
                return v[:].unsqueeze(2).to_broadcast([P, NT, E])

            def logit(b, _):
                u = BANK0["logit", b, 0]
                dve.tensor_tensor(lg, full(u)[:, 0:NT * E].rearrange("p (t e) -> p t e", t=NT),
                                  gbias_sb[:].unsqueeze(1).to_broadcast([P, NT, E]), ALU.add).then_inc(bank_read[u % 2], 1)
                dve.wait_ge(bank_read[u % 2], u // 2 + 1)
                step(dve.tensor_reduce(mx[:], lg, AX.X, ALU.max))
                dve.tensor_tensor(key, lg, wide(mx), ALU.subtract).then_inc(gate_in, 1)

            def route(b, _):
                dve.wait_ge(gate_exp, b + 1)
                for prob, chosen in ((probs, s1), (lg, s2)):
                    step(dve.tensor_reduce(mx[:], prob, AX.X, ALU.max))
                    step(dve.tensor_tensor(eq, prob, wide(mx), ALU.is_ge))
                    step(dve.tensor_tensor(key, eq, rank_sb[:], ALU.mult))
                    step(dve.tensor_reduce(mx[:], key, AX.X, ALU.max))
                    step(dve.tensor_tensor(chosen[:], key, wide(mx), ALU.is_equal))
                    if chosen is s1:
                        step(dve.scalar_tensor_tensor(out=lg, in0=s1, scalar=-2.0, in1=probs, op0=ALU.mult,
                                                      op1=ALU.add))
                step(dve.tensor_tensor(s1, s1, s2, ALU.add))
                step(dve.tensor_tensor(s2, probs, s1, ALU.mult))
                step(dve.tensor_reduce(mx[:], s2, AX.X, ALU.add))
                step(dve.reciprocal(sq[2][:], mx[:]))
                dve.tensor_tensor(comb, s2, wide(sq[2]), ALU.mult).then_inc(comb_ready, 1)

            def combT(b, _):
                u = BANK0["combT", b, 0]
                dve.wait_ge(ct_high, b + 1)
                dve.tensor_tensor(CT[32:32 + E, :], full(u)[0:E, :], CT[0:E, :].bitcast(F32), ALU.subtract)\
                   .then_inc(ct_low, 1)
                dve.wait_ge(ct_low, b + 1)
                dve.sem_inc(bank_read[u % 2], 1)

            def gate(stage):
                def _(b, part):
                    u = BANK0[stage, b, part]
                    k = 5 * b + (0 if stage == "shared" else part + 1)
                    rows, row = (I, 4) if stage == "shared" else (P, part)
                    dve.wait_ge(tanh_ready, k + 1)
                    dve.scalar_tensor_tensor(out=gs[0:rows, :], in0=sg[0:rows, k % 2, :], scalar=1.0,
                                             in1=full(u)[0:rows, :], op0=ALU.add, op1=ALU.mult).then_inc(gated, 1)
                    dve.wait_ge(gated, k + 1)
                    dve.sem_inc(bank_read[u % 2], 1)
                    last = dve.scalar_tensor_tensor(out=HH[0:rows, row, :], in0=gs[0:rows, :], scalar=0.5,
                                                    in1=full(u + 1)[0:rows, :], op0=ALU.mult, op1=ALU.mult)
                    last.then_inc(bank_read[(u + 1) % 2], 1)
                    if stage == "shared":
                        dve.wait_ge(bank_read[(u + 1) % 2], (u + 1) // 2 + 1)
                        dve.sem_inc(h_ready, 1)
                return _

            def pairB(b, part):
                u = BANK0["pairB", b, part]
                v = BANK0["pairA", b, part] + 1
                dve.wait_ge(bank_read[v % 2], v // 2 + 1)
                dve.tensor_tensor(HH[:, part, :], HH[:, part, :], full(u), ALU.mult).then_inc(h_ready, 1)
                dve.wait_ge(h_ready, 5 * b + part + 2)
                dve.sem_inc(bank_read[u % 2], 1)

            def y3(b, _):
                u = BANK0["y3", b, 0]
                dve.tensor_tensor(y_c, hres[b], full(u).rearrange("p (t c) -> p t c", t=NT), ALU.add)\
                   .then_inc(bank_read[u % 2], 1)
                dve.wait_ge(bank_read[u % 2], u // 2 + 1)
                moments(y_c, 2)
                layer_var(2)

            def fin(b, _):
                dve.wait_ge(rstd_ready, NORM0["y3", b] + 1)
                step(normalise(y_c, y_c, 2))
                dve.tensor_tensor(xs[b][:], xs[b][:], y_c, ALU.add).then_inc(out_ready, 1)

            dve.wait_ge(loaded_first, ALL_FIRST)
            dve.tensor_copy(identb[:], ident_sb[:])
            dve.tensor_copy(maskb[:], masks_sb)
            dve.memset(QS1[64:P].bitcast(F32), 0.0)
            dve.memset(KS1[64:P].bitcast(F32), 0.0)
            dve.memset(K1[:].bitcast(F32), 0.0)
            dve.memset(K2[:].bitcast(F32), 0.0)
            dve.memset(CT.bitcast(F32), 0.0).then_inc(consts_ready, 1)
            dve.wait_ge(consts_ready, 1)
            dve.memset(KS1[MROW:P], 1.0).then_inc(consts_ready, 1)
            dve.memset(K1[MROW:P].bitcast(F32), 1.0).then_inc(consts_ready, 1)
            stream(main, dict(
                ln1=ln1, ln1n=ln1n, q1=rotation("q1", rope1_sb), k1=rotation("k1", rope1_sb), wprod=wprod, wturn=wturn,
                o1y=o1y, lna=lna, lnb=lnb, rms=rms, kst=rotation("kst", ropek_sb), kst2=kst2, qabs=qabs,
                ropeA=rotation("ropeA", ropeq_sb), o2y=o2y, rms2=rms2, logit=logit, route=route, combT=combT,
                shared=gate("shared"), pairA=gate("pairA"), pairB=pairB, y3=y3, fin=fin))


def _constants(np):
    ident = np.eye(P, dtype=np.float32)
    k_above_q = np.triu(np.full((P, P), NEG, np.float32), 1)
    masks = np.stack([k_above_q, k_above_q.T], axis=1)
    t = np.arange(T, dtype=np.float32)[:, None]

    def table(freqs):
        ang = (t * freqs[None, :].astype(np.float32)).astype(np.float32).astype(np.float64)
        return np.cos(ang).astype(np.float32).T, np.sin(ang).astype(np.float32).T

    half1 = D1 // 2
    cos1, sin1 = table(1.0 / np.float32(10000.0) ** (np.arange(half1, dtype=np.float32) / np.float32(half1)))
    d = np.arange(D1)
    rope1 = np.stack([cos1[d % half1], np.where(d < half1, -1, 1)[:, None].astype(np.float32) * sin1[d % half1]], axis=1)
    rope1 = np.repeat(rope1, H, axis=0)
    cos2, sin2 = table(1.0 / np.float32(100000.0) ** (np.arange(0, ROPE, 2, dtype=np.float32) / np.float32(ROPE)))
    d = np.arange(ROPE)
    rope2 = np.stack([cos2[d // 2], np.where(d % 2 == 0, -1, 1)[:, None].astype(np.float32) * sin2[d // 2]], axis=1)
    ropeq = np.tile(rope2, (HG, 1, 1))
    plain = np.zeros((LAT, 2, T), np.float32)
    plain[:, 0] = 1
    ropek = np.concatenate([plain, rope2, plain, rope2, np.zeros((P - 2 * DK2, 2, T), np.float32)])
    rank = np.broadcast_to(np.arange(E, 0, -1, dtype=np.float32), (P, NT, E))
    rows = np.zeros((P, E // 2, P), np.float32)
    for e in range(E):
        for r in (e, 32 + e):
            rows[r, e // 2, I * (e % 2):I * (e % 2) + I] = 1
    return dict(ident=ident, masks=masks, rope1=rope1, ropek=ropek, ropeq=ropeq, rank=rank, expert_rows=rows)


def _layouts(np, w):
    a = {k: np.asarray(v) for k, v in w.items()}
    d, h = np.meshgrid(np.arange(D1), np.arange(H), indexing="ij")
    plain1, turned1 = (h * D1 + d).ravel(), (h * D1 + (d + D1 // 2) % D1).ravel()
    wq, wk = a["L0_attn_Wq"], a["L0_attn_Wk"]
    wqkv = np.stack([wq[plain1].T, wq[turned1].T, wk[plain1].T, wk[turned1].T, a["L0_attn_Wv"].T], axis=1)
    kva = a["L0_ffn_Wkva"]
    zeros = np.zeros((C, P - 2 * DK2), kva.dtype)
    turned = np.arange(ROPE) ^ 1
    kturned = np.concatenate([np.zeros((C, LAT), kva.dtype), kva[:, LAT:][:, turned]], axis=1)
    wkva = np.stack([np.concatenate([kva, kva, zeros], axis=1), np.concatenate([kturned, kturned, zeros], axis=1)], axis=1)
    wq2 = a["L0_ffn_Wq"].reshape(C, H, D2)
    rope = wq2[:, :, NOPE:]
    wq_rope = np.stack([rope.reshape(C, G, P), rope[:, :, turned].reshape(C, G, P)], axis=1)
    wkvb = a["L0_ffn_Wkvb"].reshape(LAT, H, NOPE).transpose(2, 1, 0)
    wo2 = a["L0_ffn_Wo"].reshape(H, D2, C)[:, :NOPE].transpose(1, 0, 2)
    wg, wu = (a[k].reshape(E // 2, 2, C, I).transpose(2, 0, 1, 3).reshape(C, E // 2, P) for k in ("L0_ffn_Wg", "L0_ffn_Wu"))
    return dict(
        x=a["L0_attn_x"].reshape(B * T, C), wqkv=wqkv, wo1=a["L0_attn_Wo"].T, wkva=wkva,
        wq_nope=wq2[:, :, :NOPE].transpose(2, 1, 0), wq_rope=wq_rope, wkvb=wkvb, wo2=wo2,
        ln1w=a["L0_ffn_w_ln1"].reshape(C, 1), ln2w=a["L0_ffn_w_ln2"].reshape(C, 1), wgate=a["L0_ffn_Wgate"],
        gbias=np.broadcast_to(a["L0_ffn_expert_bias"], (P, E)), wgu=np.stack([wg, wu], axis=2),
        wgu_s=np.stack([a["L0_ffn_sWg"][0], a["L0_ffn_sWu"][0]], axis=1),
        wd=a["L0_ffn_Wd"].reshape(E // 2, P, C).transpose(1, 0, 2), wd_s=a["L0_ffn_sWd"][0])


def kernel(**inputs):
    import numpy as np
    from concourse import bacc
    from concourse.bass_utils import run_bass_kernel_spmd

    nc = bacc.Bacc("TRN2", target_bir_lowering=False, num_devices=1)
    arrays = {k: np.ascontiguousarray(v) for k, v in {**_layouts(np, inputs), **_constants(np)}.items()}
    aps = {k: nc.dram_tensor(f"in_{k}", v.shape, F32, kind="ExternalInput").ap() for k, v in arrays.items()}
    out = nc.dram_tensor("out_x", (B * T, C), F32, kind="ExternalOutput").ap()
    block_program(nc, out=out, **aps)
    r = run_bass_kernel_spmd(nc, [{f"in_{k}": v for k, v in arrays.items()}], core_ids=[0])
    return r.results[0]["out_x"].reshape(B, T, C)
```

```python
from contextlib import ExitStack

import concourse.bass as bass
from concourse import mybir

F32 = mybir.dt.float32
F32R = mybir.dt.float32r
BF16 = mybir.dt.bfloat16
ALU = mybir.AluOpType
ACT = mybir.ActivationFunctionType
AX = mybir.AxisListType

P = 128
B, T, C = 4, 512, 128
NT = T // P
H = 16
G, HG = 4, 4
D1 = C // H
NOPE, ROPE, LAT = 32, 32, 16
D2 = NOPE + ROPE
DK2 = LAT + ROPE
E, I = 8, 64
EPS = 1e-5
MROW = 96
TWO_ONES = 1.0 + 0x3F80 / 2.0 ** 23
NEG = -1e30
FILLS = 11
VALUES_AT = ((1, 0), (1, 1), (1, 2), (2, 0))
UNITS = 10

PHASES = ((1, 0), (1, 1), (1, 2), (2, 0), (1, 3), (2, 1), (2, 2), (2, 3))
NG = G * len(PHASES)
LAYER = [PHASES[n // G][0] for n in range(NG)]
SEQ = [PHASES[n // G][1] for n in range(NG)]
MSTEPS = [sum(4 if LAYER[m] == 1 else 2 for m in range(n)) for n in range(NG + 1)]


def first_group(layer, b):
    return G * PHASES.index((layer, b))


def beside():
    def prep1(b, at):
        names = ("ln1", "ln1n", "x1T", "q1", "k1", "parts1", "parts1b", "store1")
        return [(*slot, name, b, 0) for slot, name in zip((*at, at[-1]), names)]

    def row(b, *stages):
        out = []
        for (n, h), name, part in stages:
            out.append((n, h, name, b, part))
            if name in ("o1y", "lnb", "route"):
                out.append((*divmod(HG * n + h + 1, HG), name + "2", b, part))
        return out

    def experts(b, n, tight):
        k = 4 * n
        order = [("o2T", 0), ("o2y", 0), ("rms2", 0), ("x3T", 0), ("logit", 0), ("route", 0), ("shared", 0), ("pairA", 0),
                 ("pairA", 1), ("combT", 0), ("pairB", 0), ("pairA", 2), ("pairB", 1), ("pairA", 3), ("pairB", 2),
                 ("pairB", 3), ("y3", 0), ("fin", 0)]
        slots = ((1, 2, 4, 5, 6, 7, 7, 8, 9, 10, 11, 11, 12, 12, 13, 14, 14, 15) if tight else
                 (1, 2, 4, 5, 6, 7, 7, 8, 9, 10, 11, 12, 12, 13, 14, 14, 15, 17))
        return row(b, *((divmod(k + s, HG), name, part) for s, (name, part) in zip(slots, order)))

    plan = [(n - 1, 1, "turnmax", n, 0) for n in range(NG)]
    pre = -3
    plan += [(pre, 0, name, 0, 0) for name in ("ln1", "ln1n", "consts", "x1T", "q1", "k1", "parts1", "parts1b", "v1",
                                                 "v1c", "store1")]
    plan += [(pre, 0, "load1", 0, g) for g in range(G)]
    plan += row(1, ((pre, 0), "ln1", 0), ((pre, 0), "ln1n", 0)) + row(0, ((pre, 0), "wprod", 0), ((pre, 0), "wturn", 0))
    plan += [(pre, 0, name, 1, 0) for name in ("x1T", "q1", "k1")]
    plan += row(1, ((-2, 0), "v1", 0), ((-2, 0), "parts1", 0), ((-2, 2), "parts1b", 0), ((-2, 3), "store1", 0),
                ((4, 2), "v1c", 0))
    plan += [(1 + g, 0, "load1", 1, g) for g in range(G)]
    plan += [(part // HG, part % HG, "clear2", 0, part) for part in range(G + 1)]
    plan += prep1(2, ((1, 1), (1, 2), (1, 3), (2, 1), (2, 2), (2, 3), (3, 1)))
    plan += row(2, ((4, 3), "v1", 0), ((8, 2), "v1c", 0))
    plan += [(5 + g, 0, "load1", 2, g) for g in range(G)]
    plan += row(0, ((5, 0), "o1T", 0), ((5, 1), "o1y", 0), ((6, 0), "lna", 0), ((6, 2), "lna2", 0), ((7, 0), "lnb", 0),
                ((7, 1), "x2T", 0), ((7, 2), "kst", 0), ((7, 2), "latv", 0), ((7, 3), "qabs", 0), ((7, 3), "kst2", 0),
                ((8, 0), "qabs", 1), ((8, 0), "ropeA", 0), ((8, 1), "ropeB", 0), ((8, 1), "ropeA", 1),
                ((8, 2), "ropeB", 1), ((8, 2), "ropeA", 2), ((8, 3), "ropeB", 2), ((8, 3), "ropeA", 3),
                ((9, 0), "ropeB", 3), ((9, 1), "load2", 0), ((9, 3), "load2", 1), ((10, 2), "load2", 2),
                ((11, 2), "load2", 3))
    plan += prep1(3, ((9, 1), (9, 2), (9, 3), (10, 0), (10, 1), (10, 3), (11, 0)))
    plan += row(3, ((10, 2), "v1", 0), ((12, 2), "v1c", 0))
    plan += [(12, g, "load1", 3, g) for g in range(G)]
    plan += row(1, ((9, 1), "o1T", 0), ((9, 3), "o1y", 0), ((10, 2), "lna", 0), ((11, 0), "lna2", 0), ((11, 2), "lnb", 0),
                ((12, 0), "x2T", 0), ((12, 1), "kst", 0), ((12, 1), "latv", 0), ((12, 2), "qabs", 0),
                ((12, 3), "qabs", 1), ((12, 3), "kst2", 0), ((13, 0), "ropeA", 0), ((13, 1), "ropeB", 0),
                ((13, 1), "ropeA", 1), ((13, 2), "ropeB", 1), ((13, 2), "ropeA", 2), ((13, 3), "ropeB", 2),
                ((13, 3), "ropeA", 3), ((14, 0), "ropeB", 3), ((16, 3), "load2", 0), ((17, 0), "load2", 1),
                ((17, 1), "load2", 2), ((17, 2), "load2", 3))
    plan += row(2, ((13, 0), "o1T", 0), ((13, 1), "o1y", 0), ((14, 0), "lna", 0), ((14, 2), "lna2", 0), ((15, 0), "lnb", 0),
                ((15, 2), "x2T", 0), ((15, 3), "qabs", 0), ((16, 0), "qabs", 1), ((16, 1), "kst", 0),
                ((16, 2), "latv", 0), ((16, 2), "kst2", 0), ((17, 0), "ropeA", 0), ((17, 1), "ropeB", 0),
                ((17, 1), "ropeA", 1), ((17, 2), "ropeB", 1), ((17, 2), "ropeA", 2), ((17, 3), "ropeB", 2),
                ((17, 3), "ropeA", 3), ((18, 0), "ropeB", 3), ((21, 0), "load2", 0), ((22, 0), "load2", 1),
                ((23, 0), "load2", 2), ((24, 0), "load2", 3))
    plan += row(0, ((20, 0), "experts_in", 0))
    plan += row(0, ((18, 1), "o2T", 0), ((18, 2), "o2y", 0), ((19, 0), "rms2", 0), ((20, 1), "x3T", 0), ((20, 2), "logit", 0),
                ((20, 3), "route", 0), ((20, 3), "shared", 0), ((21, 1), "pairA", 0), ((21, 3), "combT", 0),
                ((22, 0), "pairB", 0), ((22, 2), "pairA", 1), ((22, 3), "pairB", 1), ((23, 1), "pairA", 2),
                ((23, 2), "pairB", 2), ((24, 3), "pairA", 3), ((25, 0), "pairB", 3), ((25, 1), "y3", 0), ((25, 3), "fin", 0))
    plan += row(3, ((21, 0), "o1T", 0), ((21, 1), "o1y", 0), ((21, 3), "lna", 0), ((22, 1), "lna2", 0), ((22, 3), "lnb", 0),
                ((23, 0), "x2T", 0), ((23, 1), "qabs", 0), ((23, 2), "qabs", 1), ((23, 2), "ropeA", 0),
                ((23, 3), "ropeB", 0), ((23, 3), "ropeA", 1), ((24, 0), "ropeB", 1), ((24, 0), "ropeA", 2),
                ((24, 1), "ropeB", 2), ((24, 1), "kst", 0), ((24, 2), "latv", 0), ((24, 2), "kst2", 0),
                ((24, 2), "ropeA", 3), ((24, 3), "ropeB", 3), ((25, 0), "load2", 0), ((26, 0), "load2", 1),
                ((27, 0), "load2", 2), ((28, 0), "load2", 3))
    plan += experts(1, 25, False)
    two = experts(2, 29, True)
    plan += [e for e in two if e[2] not in ("y3", "fin")]
    plan += row(3, ((33, 1), "o2T", 0), ((33, 1), "o2y", 0)) + row(2, ((33, 1), "y3", 0))
    plan += row(3, ((33, 1), "rms2", 0), ((33, 1), "x3T", 0), ((33, 1), "logit", 0)) + row(2, ((33, 1), "fin", 0))
    plan += [(33, 2, name, 3, part) for name, part in (
        ("route", 0), ("shared", 0), ("route2", 0), ("pairA", 0), ("pairA", 1), ("combT", 0), ("pairA", 2), ("y3part", 0),
        ("pairB", 0), ("y3part", 1), ("pairB", 1), ("pairA", 3), ("y3part", 2), ("pairB", 2), ("y3part", 3), ("pairB", 3),
        ("y3part", 4), ("y3", 0), ("fin", 0))]
    return sorted(plan, key=lambda e: (e[0], e[1]))


BESIDE = beside()
LAST = max(e[0] for e in BESIDE)

TAKES = {"turnmax": (1, 0, 0, 0), "x1T": (1, 0, 0, 0), "q1": (2, 0, 1, 0), "k1": (2, 0, 1, 0), "v1": (1, 0, 0, 0), "wprod": (2, 0, 0, 0),
         "wturn": (1, 0, 0, 0), "ln1": (0, 1, 0, 0), "ln1n": (0, 0, 0, 1), "o1T": (1, 0, 0, 0), "o1y": (1, 0, 0, 0), "o1y2": (0, 1, 0, 0),
         "lna2": (0, 1, 0, 0), "lnb": (0, 0, 0, 1), "x2T": (1, 0, 0, 0), "kst": (2, 0, 1, 0),
         "latv": (1, 0, 0, 0), "qabs": (1, 0, 0, 0), "ropeA": (2, 0, 1, 0), "o2T": (2, 0, 0, 0), "o2y": (1, 1, 0, 0),
         "rms2": (0, 0, 0, 1), "x3T": (1, 0, 0, 0), "logit": (1, 0, 0, 0), "combT": (1, 0, 0, 0), "shared": (2, 0, 0, 0),
         "pairA": (2, 0, 0, 0), "pairB": (1, 0, 0, 0), "y3": (1, 1, 0, 0)}
BANK0, NORM0, JOB0, TILE0, TURN_OF = {}, {}, {}, {}, []
_n = [0, 0, 0, 0]
for _, _, _stage, _b, _part in BESIDE:
    BANK0[_stage, _b, _part], NORM0[_stage, _b], JOB0[_stage, _b, _part], TILE0[_stage, _b] = _n
    if _stage in ("x1T", "x2T", "x3T"):
        TURN_OF.append(_n[0])
    _n = [a + t for a, t in zip(_n, TAKES.get(_stage, (0, 0, 0, 0)))]
BANK = []
for _u in range(_n[0]):
    _k = _u - BANK0["o2T", B - 1, 0]
    BANK.append(4 if _u == BANK0["y3", B - 1, 0] else 6 + _u % 2 if _k < 0 else (6, 7, 0, 1, 2, 3)[_k % 6])
USE = [BANK[:_u].count(BANK[_u]) for _u in range(_n[0])]


def bank_of(u):
    return BANK[u]


GATED_BEFORE, _u = {}, None
for _, _, _stage, _b, _part in BESIDE:
    if _stage in ("shared", "pairA"):
        GATED_BEFORE[_stage, _b, _part] = _u
        _u = BANK0[_stage, _b, _part] + 1


QTILE = {}
for _, _, _stage, _b, _part in BESIDE:
    if _stage in ("qabs", "ropeB"):
        QTILE[_stage, _b, _part] = len(QTILE)


SCALE_OF, TURN_ORDER, _k = {}, {}, 0
for _, _, _stage, _b, _ in BESIDE:
    if _stage in ("ln1", "o1y2", "lna2", "o2y", "y3"):
        _k += 1
        SCALE_OF[{"ln1": "ln1n", "o1y2": "lna", "lna2": "lnb", "o2y": "rms2", "y3": "fin"}[_stage], _b] = _k
        _k += _stage == "lna2"
    if _stage in ("ln1n", "lnb", "rms2"):
        TURN_ORDER[_stage, _b] = len(TURN_ORDER)

ONT_AFTER, _k = {}, 0
for _, _, _stage, _b, _ in BESIDE:
    if _stage in ("o1T", "o2T"):
        _k += TAKES[_stage][0]
        ONT_AFTER[_stage, _b] = _k


def block_program(nc, x, wqkv, wo1, wkva, wq_nope, wq_rope, wkvb, wo2, ln1w, ln2w, wgate, gbias, wgu, wgu_s, wd,
                  wd_s, ident, masks, rope1, ropek, ropeq, rank, expert_rows, out):
    with ExitStack() as ctx:
        def sb(name, shape, dt=F32):
            return ctx.enter_context(nc.sbuf_tensor(name, shape, dt))

        def sem(name):
            return ctx.enter_context(nc.semaphore(name))

        wqkv_sb = sb("wqkv_sb", [P, 5, C])
        wo1_sb = sb("wo1_sb", [P, C])
        wkva_sb = sb("wkva_sb", [P, 2, P])
        wqr_sb = sb("wqr_sb", [P, 2, 4, P])
        wabs_sb = sb("wabs_sb", [P, 2, P])
        wco_sb = sb("wco_sb", [P, 2, C])
        ln1w_sb = sb("ln1w_sb", [P, 1])
        ln2w_sb = sb("ln2w_sb", [P, 1])
        wgate_sb = sb("wgate_sb", [P, E])
        gbias_sb = sb("gbias_sb", [P, E])
        ident_sb = sb("ident_sb", [P, P])
        identb = sb("identb", [P, P], BF16)
        maskb = sb("maskb", [P, 2, P], BF16)
        rope1_sb = sb("rope1_sb", [P, 2, T])
        ropek_sb = sb("ropek_sb", [P, 2, T])
        ropeq_sb = sb("ropeq_sb", [P, 2, T])
        rank_sb = sb("rank_sb", [P, NT, E])
        erow = sb("erow", [P, 4, P], F32R)
        half = sb("half", [P, NT])

        xs = [sb(f"x{b}", [P, NT, C]) for b in range(B)]
        xn = sb("xn", [P, NT, C])
        y_b = sb("y_b", [P, NT, C])
        stats = sb("stats", [P, NT, 6])
        mv = [sb(f"mv{k}", [P, NT, 2]) for k in range(4)]
        ve = [sb(f"ve{k}", [P, NT]) for k in range(4)]
        rstd = [sb(f"rstd{k}", [P, NT]) for k in range(4)]
        nmean = [sb(f"nmean{k}", [P, NT]) if k != 2 else None for k in range(4)]
        sq = sb("sq", [P, NT])
        rstd_xn, nmean_xn = sb("rstd_xn", [P, NT]), sb("nmean_xn", [P, NT])
        sums = sb("sums", [P, NT])
        xT2 = sb("xT2", [P, T])
        terms = sb("terms", [P, 2, 2, T])
        whole = sb("whole", [P, 2, T])
        vc = sb("vc", [P, NT, C])
        QS1 = sb("QS1", [P, H, T], BF16)
        KS1 = sb("KS1", [P, H, T], BF16)
        V1 = sb("V1", [P, NT, H, 32])
        QC = sb("QC", [P, 2, 2, T], F32R)
        QS2 = sb("QS2", [P, H, T], F32R)
        K1 = sb("K1", [P, 2, T], F32R)
        K2 = sb("K2", [P, 2, T], F32R)
        V2 = sb("V2", [P, 2, NT, 32])
        NM = sb("NM", [P, NT, H])
        MB = sb("MB", [P, NT, 3, HG], BF16)
        MRest = sb("MRest", [P, NT, HG])
        MF = sb("MF", [P, NT, 2, HG], F32R)
        MP = sb("MP", [3 * HG, 2, T])
        PA = sb("PA", [P, 8, 2 * T])
        PC = sb("PC", [P, 4, 2, 256])
        OT = sb("OT", [P, T])
        rec = sb("rec", [P, NT, HG])
        ON1 = sb("ON1", [P, NT, H * D1])
        ONT = sb("ONT", [P, 2, T])
        CT = sb("CT", [P, T], F32R)[:]

        pa_flat = PA[:].rearrange("p a t -> p (a t)")[:, 8 * T:16 * T]
        pc_flat = PC[:].rearrange("p a b t -> p (a b t)")
        wqn_sb = pa_flat[0:NOPE, 0:H * C].rearrange("d (h c) -> d h c", h=H)
        wo2_sb = pa_flat[0:NOPE, H * C:2 * H * C].rearrange("d (h c) -> d h c", h=H)
        masks_sb = pc_flat[:, 0:2 * P].rearrange("p (a b) -> p a b", a=2)
        erow_sb = pc_flat[:, 2 * T:3 * T].rearrange("p (a b) -> p a b", a=4)
        wkvb_sb = pc_flat[0:NOPE, 3 * T:3 * T + H * LAT].rearrange("d (h r) -> d h r", h=H)
        wco_t = pc_flat[:, 3 * T + H * LAT:3 * T + 2 * H * LAT].rearrange("p (a b) -> p a b", a=2)
        q_flat = QS1[:].rearrange("p a t -> p (a t)").bitcast(F32)
        HH = q_flat[:, 0:5 * T].rearrange("p (n t) -> p n t", t=T)
        sg = q_flat[:, 5 * T:7 * T].rearrange("p (n t) -> p n t", t=T)
        xT3 = q_flat[:, 7 * T:8 * T]
        k_flat = KS1[:].rearrange("p a t -> p (a t)").bitcast(F32)
        y_c = k_flat[:, 0:T].rearrange("p (t c) -> p t c", t=NT)
        gs = k_flat[:, 2 * T:3 * T]
        wgu_sb = k_flat[:, 4 * T:6 * T].rearrange("p (k a i) -> p k a i", k=4, a=2)
        wd_sb = k_flat[:, 6 * T:7 * T].rearrange("p (k c) -> p k c", k=4)
        wgus_sb = k_flat[:, 7 * T:7 * T + 2 * I].rearrange("p (a i) -> p a i", a=2)
        wds_sb = k_flat[0:I, 7 * T + 2 * I:7 * T + 2 * I + C]
        gates = k_flat[:, 7 * T + 2 * I + C:7 * T + 2 * I + C + 7 * NT * E].rearrange("p (k t e) -> p k t e", k=7, t=NT)
        lg, probs, eq, key, s1, s2, comb = (gates[:, k] for k in range(7))
        mx = k_flat[:, 8 * T - NT:8 * T]
        room1 = sb("room1", [P, 4 * T])
        qp = room1[:, 0:3 * T // 2].bitcast(BF16).rearrange("p (a t) -> p a t", a=3)
        kp = room1[:, 3 * T // 2:3 * T].bitcast(BF16).rearrange("p (a t) -> p a t", a=3)
        xT1 = room1[:, 3 * T:4 * T]
        ON2 = room1[:, 0:2 * T].rearrange("p (t c) -> p t c", t=NT)
        hres = [sb("hres0", [P, NT, C])[:], room1[:, 3 * T:4 * T].rearrange("p (t c) -> p t c", t=NT),
                room1[:, 2 * T:3 * T].rearrange("p (t c) -> p t c", t=NT),
                k_flat[:, T:2 * T].rearrange("p (t c) -> p t c", t=NT)]

        scr_q = nc.dram_tensor("scr_q", [B, 3, P, T], BF16, kind="Internal")
        scr_k = nc.dram_tensor("scr_k", [B, 5, P, T], BF16, kind="Internal")
        scr_2 = nc.dram_tensor("scr_2", [B, 6, 2, P, T], F32, kind="Internal")

        ps = ctx.enter_context(nc.psum_tensor("ps", [P, 8, T], F32))
        ST0, BK_O = 2, 5

        loaded_first, loaded_qkv, loaded, x_loaded = sem("loaded_first"), sem("loaded_qkv"), sem("loaded"), sem("x_loaded")
        x0_loaded = sem("x0_loaded")
        loaded_late = sem("loaded_late")
        consts_ready, cleared = sem("consts_ready"), sem("cleared")
        dve_step, pool_step = sem("dve_step"), sem("pool_step")
        score_fill, fill_read = sem("score_fill"), sem("fill_read")
        rec_ready = sem("rec_ready")
        m_step, m_copied = sem("m_step"), sem("m_copied")
        m_stacked = [sem(f"m_stacked{g}") for g in range(G)]
        st_ready, exp_done = sem("st_ready"), sem("exp_done")
        pv, ot_ready, o_turned, on_ready = sem("pv"), sem("ot_ready"), sem("o_turned"), sem("on_ready")
        bank_full = sem("bank_full")
        bank_read = [sem(f"bank_read{k}") for k in range(8)]
        y_normed, yc_normed, hres_ready, scale_ready = sem("y_normed"), sem("yc_normed"), sem("hres_ready"), sem("scale_ready")
        var_ready, xn_ready, x1_ready = sem("var_ready"), sem("xn_ready"), sem("x1_ready")
        xT1_ready, xT2_ready, xT3_ready = sem("xT1_ready"), sem("xT2_ready"), sem("xT3_ready")
        terms_ready, whole_ready = sem("terms_ready"), sem("whole_ready")
        job_done = [sem("job_done0"), sem("job_done1")]
        high1, middle1, rest1, low1 = sem("high1"), sem("middle1"), sem("rest1"), sem("low1")
        stored1 = sem("stored1")
        stack1_in = [sem(f"stack1_in{g}") for g in range(G)]
        vc_ready, v1_ready, v2_ready = sem("vc_ready"), sem("v1_ready"), sem("v2_ready")
        k_high, k_low = sem("k_high"), sem("k_low")
        ont_ready, y_ready = sem("ont_ready"), sem("y_ready")
        q_high, q_low = sem("q_high"), sem("q_low")
        q_stored = [sem("q_stored0"), sem("q_stored1")]
        stack2_in = [sem(f"stack2_in{g}") for g in range(G)]
        gate_in, gate_exp, comb_ready, ct_high, ct_low = (sem("gate_in"), sem("gate_exp"), sem("comb_ready"),
                                                          sem("ct_high"), sem("ct_low"))
        tanh_ready, gated, h_ready = sem("tanh_ready"), sem("gated"), sem("h_ready")
        out_ready, out_sent = sem("out_ready"), sem("out_sent")

        FIRST_LOADS = ((ident_sb[:], ident[:]), (masks_sb, masks[:]))
        QKV_LOADS = ((wqkv_sb[:], wqkv[:]), (rope1_sb[:], rope1[:]))
        LOADS = ((wqn_sb, wq_nope[:]), (wo2_sb, wo2[:]), (wkvb_sb, wkvb[:]), (erow_sb, expert_rows[:]),
                 (wo1_sb[:], wo1[:]), (ln1w_sb[:], ln1w[:]), (wkva_sb[:], wkva[:]), (wqr_sb[:], wq_rope[:]),
                 (ropek_sb[:], ropek[:]), (ropeq_sb[:], ropeq[:]), (ln2w_sb[:], ln2w[:]),
                 (wgate_sb[:], wgate[:]), (gbias_sb[:], gbias[:]), (rank_sb[:], rank[:]))
        LATE_LOADS = ((wgu_sb, wgu[:]), (wgus_sb, wgu_s[:]), (wd_sb, wd[:]), (wds_sb, wd_s[:]))
        STORED1 = 16 * 8
        ALL_FIRST, ALL_QKV, ALL_LOADED = 16 * len(FIRST_LOADS), 16 * len(QKV_LOADS), 16 * len(LOADS)
        STACK_ZEROS, CONSTS, EROW, WCO = 1, 2, 3, 4
        HALF, QUERY_ZEROS, V1_ONES, LAYER2 = 1, 2, 3, 3 + G + 5

        def was_read(u):
            return bank_read[BANK[u]], USE[u] + 1

        def stream(engine_main, stages):
            for n in range(-3, LAST + 1):
                for hh in range(HG):
                    if n >= -2:
                        engine_main(n, hh)
                    for m, h, stage, b, part in BESIDE:
                        if (m, h) == (n, hh) and stage in stages:
                            stages[stage](b, part)

        block = ctx.enter_context(nc.Block())

        @block.sync
        def _(sp):
            x_seq = x.rearrange("(b n p) c -> b p n c", b=B, p=P)
            out_seq = out.rearrange("(b n p) c -> b p n c", b=B, p=P)
            sp.dma_start(xs[0][:], x_seq[0]).then_inc(x0_loaded, 16)
            for dst, src in FIRST_LOADS:
                sp.dma_start(dst, src).then_inc(loaded_first, 16)
            for dst, src in QKV_LOADS:
                sp.dma_start(dst, src).then_inc(loaded_qkv, 16)
            for dst, src in LOADS:
                sp.dma_start(dst, src).then_inc(loaded, 16)

            def turnmax(m, _):
                g = m % G
                sp.wait_ge(m_copied, m + 1)
                if LAYER[m] == 1:
                    sp.dma_start(QS1[MROW:MROW + 3, HG * g:HG * g + HG, :],
                                 MP[:, m % 2, 0:T // 2].bitcast(BF16)).then_inc(m_stacked[g], 16)
                else:
                    sp.dma_start(QS2[MROW:MROW + 2, HG * g:HG * g + HG, :].bitcast(F32),
                                 MP[0:2 * HG, m % 2, :]).then_inc(m_stacked[g], 16)

            def ln1(b, _):
                if b == 0:
                    for k in range(1, B):
                        sp.dma_start(xs[k][:], x_seq[k]).then_inc(x_loaded, 16)

            def store1(b, _):
                for a, ready in enumerate((high1, middle1, low1)):
                    sp.wait_ge(ready, 2 * (b + 1))
                    sp.dma_start(scr_q[b, a], qp[:, a, :]).then_inc(stored1, 16)
                    sp.dma_start(scr_k[b, a], kp[:, a, :]).then_inc(stored1, 16)
                    if a < 2:
                        sp.dma_start(scr_k[b, 3 + a], kp[:, a, :]).then_inc(stored1, 16)

            def load1(b, g):
                sp.wait_ge(stored1, STORED1 * (b + 1))
                if b == 0:
                    sp.wait_ge(consts_ready, CONSTS)
                    sp.wait_ge(cleared, QUERY_ZEROS)
                else:
                    sp.wait_ge(st_ready, UNITS * (first_group(1, b - 1) + g + 1))
                heads = slice(HG * g, HG * g + HG)
                q_parts = scr_q[b].rearrange("a (d h) t -> (a d) h t", h=H)[:, heads, :]
                k_parts = scr_k[b, 0:3].rearrange("a (d h) t -> (a d) h t", h=H)[:, heads, :]
                sp.dma_start(QS1[0:72, heads, :], bass.AP(q_parts.tensor, q_parts.offset, [[0, 3], *q_parts.ap]))\
                  .then_inc(stack1_in[g], 16)
                sp.dma_start(KS1[0:72, heads, :], bass.AP(k_parts.tensor, k_parts.offset, [[P * T, 3], *k_parts.ap]))\
                  .then_inc(stack1_in[g], 16)

            def store2(stage):
                def _(b, part):
                    c = QTILE[stage, b, part]
                    sp.wait_ge(q_low, c + 1)
                    tile = part if stage == "qabs" else 2 + part
                    sp.dma_start(scr_2[b, tile].rearrange("a p t -> p a t"), QC[:, c % 2, :, :].bitcast(F32))\
                      .then_inc(q_stored[c % 2], 16)
                return _

            def load2(b, g):
                tiles = [QTILE["qabs", b, 0], QTILE["qabs", b, 1], QTILE["ropeB", b, g]]
                for k in range(2):
                    sp.wait_ge(q_stored[k], 16 * max([c // 2 + 1 for c in tiles if c % 2 == k] + [1]))
                if b == 0:
                    sp.wait_ge(cleared, LAYER2)
                else:
                    sp.wait_ge(st_ready, UNITS * (first_group(2, b - 1) + g + 1))
                heads = slice(HG * g, HG * g + HG)
                for a in range(2):
                    for t in range(2):
                        sp.dma_start(QS2[DK2 * a + 8 * t:DK2 * a + 8 * t + 8, heads, :].bitcast(F32),
                                     scr_2[b, t, a].rearrange("(r h) t -> r h t", h=H)[:, heads, :])\
                          .then_inc(stack2_in[g], 16)
                    sp.dma_start(QS2[DK2 * a + LAT:DK2 * a + DK2, heads, :].bitcast(F32),
                                 scr_2[b, 2 + g, a].rearrange("(h d) t -> d h t", h=HG)).then_inc(stack2_in[g], 16)

            def experts_in(b, _):
                sp.wait_ge(st_ready, UNITS * (first_group(1, B - 1) + G))
                for dst, src in LATE_LOADS:
                    sp.dma_start(dst, src).then_inc(loaded_late, 16)

            def fin(b, _):
                sp.wait_ge(out_ready, b + 1)
                sp.dma_start(out_seq[b], xs[b][:]).then_inc(out_sent, 16)

            stream(lambda n, hh: None, dict(turnmax=turnmax, ln1=ln1, store1=store1, load1=load1, qabs=store2("qabs"), ropeB=store2("ropeB"),
                              load2=load2, experts_in=experts_in, fin=fin))
            sp.wait_ge(out_sent, 16 * B)

        @block.tensor
        def _(pe):
            def products(dst, n, h, i, k):
                if LAYER[n] == 1:
                    pe.matmul(dst, QS1[0:MROW, h, P * i:P * i + P], KS1[0:MROW, h, 0:P * k], start=True, stop=False)
                else:
                    pe.matmul(dst, QS2[0:MROW, h, P * i:P * i + P], K1[0:MROW, SEQ[n] % 2, 0:P * k], start=True,
                              stop=False)
                return pe.matmul(dst[:, P * (k - 1):P * k], identb[:], maskb[:, 0, :], start=False, stop=True)

            def fills_of(hh):
                return 2 * hh + hh // 2, 2 + hh % 2 + hh // 3

            def scores_for_max(n, hh, i):
                h = HG * (n % G) + hh
                f = n * FILLS + fills_of(hh)[0] + i
                if f >= 2:
                    pe.wait_ge(fill_read, f - 1)
                bank = ps[:, f % 2, :]
                heads = (1, 1, 2, 4)[i]
                for j in range(heads):
                    w = P * (4 - i)
                    mm = products(bank[:, w * j:w * j + w], n, h - heads + 1 + j, 3 - i, 4 - i)
                mm.then_inc(score_fill, 1)

            def scores_t(dst, n, h, j):
                q0 = P * j
                if LAYER[n] == 1:
                    pe.matmul(dst, KS1[:, h, q0:q0 + P], QS1[:, h, q0:T], start=True, stop=False)
                else:
                    for keys in (K1, K2):
                        pe.matmul(dst, keys[:, SEQ[n] % 2, q0:q0 + P], QS2[:, h, q0:T], start=(keys is K1), stop=False)
                return pe.matmul(dst[:, 0:P], identb[:], maskb[:, 1, :], start=False, stop=True)

            def scores_for_exp(n, hh, i):
                h = HG * (n % G) + hh
                u = n * UNITS + 5 * (hh // 2) + 2 * (hh % 2) + i
                if hh == 0 and i == 0:
                    pe.wait_ge(m_stacked[n % G], 16 * (n // G + 1))
                if u >= 3:
                    pe.wait_ge(exp_done, u - 2)
                bank = ps[:, ST0 + u % 3, :]
                tiles = (((0, T, h, 0),), ((0, 3 * P, h, 1), (3 * P, T, h, 3)), ((0, 256, h - 1, 2), (256, T, h, 2)))[i]
                for lo, hi, head, j in tiles:
                    mm = scores_t(bank[:, lo:hi], n, head, j)
                mm.then_inc(st_ready, 1)

            def values(n, j):
                if j == 0:
                    pe.wait_ge(exp_done, UNITS * (n + 1))
                    if n:
                        pe.wait_ge(on_ready, n)
                    if n % G == 0:
                        pe.wait_ge(v1_ready if LAYER[n] == 1 else v2_ready, SEQ[n] + 1)
                for hh in range(HG):
                    h = HG * (n % G) + hh
                    slot = h % 8
                    p = (PA[:, slot, 0:T], PA[:, slot, T:T + 3 * P], PC[:, slot // 2, hh % 2, :],
                         PA[:, slot, T + 3 * P:2 * T])[j]
                    v = V1[:, j, h, :] if LAYER[n] == 1 else V2[:, SEQ[n] % 2, j, :]
                    mm = pe.matmul(ps[32 * hh:32 * hh + 32, BK_O, P * j:T], v, p, start=(j == 0), stop=(j == NT - 1),
                                   skip_group_check=True)
                if j == NT - 1:
                    mm.then_inc(pv, 1)

            def turn_out(n):
                pe.wait_ge(ot_ready, n + 1)
                for t in range(NT):
                    mm = pe.transpose(ps[:, BK_O, P * t:P * t + P], OT[:, P * t:P * t + P], ident_sb[:])
                mm.then_inc(o_turned, 1)

            def main(n, hh):
                if hh == 0 and n + 2 < NG:
                    m = n + 2
                    if m == 0:
                        pe.wait_ge(consts_ready, CONSTS)
                    if LAYER[m] == 1:
                        pe.wait_ge(stack1_in[m % G], 32 * (SEQ[m] + 1))
                    else:
                        pe.wait_ge(stack2_in[m % G], 96 * (SEQ[m] + 1))
                        pe.wait_ge(k_low, SEQ[m] + 1)
                for i in range(4):
                    if 0 <= n < NG and i < 2 + hh % 2:
                        scores_for_exp(n, hh, i)
                    if n + 2 < NG and i < fills_of(hh)[1]:
                        scores_for_max(n + 2, hh, i)
                    if 1 <= n <= NG and (hh, i) in VALUES_AT:
                        values(n - 1, VALUES_AT.index((hh, i)))
                if hh == 3 and 1 <= n <= NG:
                    turn_out(n - 1)

            def bank(u):
                if USE[u]:
                    pe.wait_ge(bank_read[BANK[u]], USE[u])
                return ps[:, bank_of(u), :]

            def turnmax(n, _):
                pe.wait_ge(m_step, MSTEPS[n + 1])
                dst = bank(BANK0["turnmax", n, 0])
                for t in range(NT):
                    if LAYER[n] == 1:
                        mm = pe.transpose(dst[0:3 * HG, :].bitcast(BF16)[:, P * t:P * t + P],
                                          MB[:, t, :, :].rearrange("p a h -> p (a h)"), identb[:])
                    else:
                        mm = pe.transpose(dst[0:2 * HG, P * t:P * t + P],
                                          MF[:, t, :, :].bitcast(F32).rearrange("p a h -> p (a h)"), ident_sb[:])
                mm.then_inc(bank_full, 1)

            def turn_tile(stage):
                def _(b, part):
                    u = BANK0[stage, b, part]
                    if u == 0:
                        pe.wait_ge(loaded_first, ALL_FIRST)
                    pe.wait_ge(xn_ready, TURN_OF.index(u) + 1)
                    dst = bank(u)
                    for t in range(NT):
                        mm = pe.transpose(dst[:, P * t:P * t + P], xn[:, t, :], ident_sb[:])
                    mm.then_inc(bank_full, 1)
                return _

            def project(u, w, xT, rows=P):
                pe.matmul(bank(u)[0:rows, :], w, xT, start=True, stop=True).then_inc(bank_full, 1)

            def q1(b, _):
                if b == 0:
                    pe.wait_ge(loaded_qkv, ALL_QKV)
                pe.wait_ge(xT1_ready, b + 1)
                for k in range(2):
                    project(BANK0["q1", b, 0] + k, wqkv_sb[:, k, :], xT1)

            def k1(b, _):
                for k in range(2):
                    project(BANK0["k1", b, 0] + k, wqkv_sb[:, 2 + k, :], xT1)

            def v1(b, _):
                dst = bank(BANK0["v1", b, 0])
                for t in range(NT):
                    mm = pe.matmul(dst[:, P * t:P * t + P], xT1[:, P * t:P * t + P], wqkv_sb[:, 4, :], start=True, stop=True)
                mm.then_inc(bank_full, 1)

            def wprod(b, _):
                u = BANK0["wprod", 0, 0]
                pe.wait_ge(loaded, ALL_LOADED)
                for k, w in enumerate((wqn_sb, wo2_sb)):
                    dst = bank(u + k)
                    for h in range(H):
                        mm = pe.matmul(dst[:, LAT * h:LAT * h + LAT], w[:, h, :], wkvb_sb[:, h, :], start=True, stop=True)
                    mm.then_inc(bank_full, 1)

            def wturn(b, _):
                u = BANK0["wturn", 0, 0]
                pe.wait_ge(*was_read(u - 1))
                dst = bank(u)
                for a in range(2):
                    mm = pe.transpose(dst[:, P * a:P * a + P], wco_t[:, a, :], ident_sb[:])
                mm.then_inc(bank_full, 1)

            def o1T(b, _):
                pe.wait_ge(on_ready, first_group(1, b) + G)
                dst = bank(BANK0["o1T", b, 0])
                for t in range(NT):
                    mm = pe.transpose(dst[:, P * t:P * t + P], ON1[:, t, :], ident_sb[:])
                mm.then_inc(bank_full, 1)

            def outputs(stage, ready, weights):
                def _(b, part):
                    pe.wait_ge(ont_ready, ready(b))
                    dst = bank(BANK0[stage, b, 0])
                    for t in range(NT):
                        for a, w in enumerate(weights):
                            mm = pe.matmul(dst[:, P * t:P * t + P], ONT[:, a, P * t:P * t + P], w, start=(a == 0),
                                           stop=(a == len(weights) - 1))
                    mm.then_inc(bank_full, 1)
                return _

            def kst(b, _):
                pe.wait_ge(xT2_ready, b + 1)
                for k in range(2):
                    project(BANK0["kst", b, 0] + k, wkva_sb[:, k, :], xT2[:])

            def latv(b, _):
                pe.wait_ge(xT2_ready, b + 1)
                dst = bank(BANK0["latv", b, 0])
                for t in range(NT):
                    mm = pe.matmul(dst[:, LAT * t:LAT * t + LAT], xT2[:, P * t:P * t + P], wkva_sb[:, 0, 0:LAT], start=True,
                                   stop=True)
                mm.then_inc(bank_full, 1)

            def qabs(b, part):
                pe.wait_ge(xT2_ready, b + 1)
                project(BANK0["qabs", b, part], wabs_sb[:, part, :], xT2[:])

            def ropeA(b, part):
                pe.wait_ge(xT2_ready, b + 1)
                for k in range(2):
                    project(BANK0["ropeA", b, part] + k, wqr_sb[:, k, part, :], xT2[:])

            def o2T(b, _):
                pe.wait_ge(on_ready, first_group(2, b) + G)
                for a in range(2):
                    dst = bank(BANK0["o2T", b, 0] + a)
                    for t in range(NT):
                        mm = pe.transpose(dst[:, P * t:P * t + P], ON2[:, t, P * a:P * a + P], ident_sb[:])
                    mm.then_inc(bank_full, 1)

            def logit(b, _):
                pe.wait_ge(xT3_ready, b + 1)
                dst = bank(BANK0["logit", b, 0])
                for t in range(NT):
                    mm = pe.matmul(dst[:, E * t:E * t + E], xT3[:, P * t:P * t + P], wgate_sb[:], start=True, stop=True)
                mm.then_inc(bank_full, 1)

            def shared(b, _):
                pe.wait_ge(loaded_late, 16 * len(LATE_LOADS))
                for k in range(2):
                    project(BANK0["shared", b, 0] + k, wgus_sb[:, k, :], xT3, rows=I)

            def pairA(b, part):
                for k in range(2):
                    project(BANK0["pairA", b, part] + k, wgu_sb[:, part, k, :], xT3)

            def combT(b, _):
                pe.wait_ge(comb_ready, b + 1)
                dst = bank(BANK0["combT", b, 0])
                for t in range(NT):
                    mm = pe.transpose(dst[0:E, P * t:P * t + P], comb[:, t, :], ident_sb[:])
                mm.then_inc(bank_full, 1)

            def pairB(b, part):
                pe.wait_ge(ct_low, b + 1)
                project(BANK0["pairB", b, part], erow[:, part, :], CT)

            def y3(b, _):
                if b == B - 1:
                    return
                pe.wait_ge(h_ready, 5 * (b + 1))
                dst = bank(BANK0["y3", b, 0])
                for t in range(NT):
                    pe.matmul(dst[:, P * t:P * t + P], HH[0:I, 4, P * t:P * t + P], wds_sb, start=True, stop=False)
                    for k in range(4):
                        mm = pe.matmul(dst[:, P * t:P * t + P], HH[:, k, P * t:P * t + P], wd_sb[:, k, :], start=False,
                                       stop=(k == 3))
                mm.then_inc(bank_full, 1)

            def y3part(b, part):
                pe.wait_ge(h_ready, 5 * b + part + 1)
                dst = ps[:, BANK[BANK0["y3", b, 0]], :]
                for t in range(NT):
                    h, w = (HH[0:I, 4, P * t:P * t + P], wds_sb) if part == 0 else (HH[:, part - 1, P * t:P * t + P],
                                                                                   wd_sb[:, part - 1, :])
                    mm = pe.matmul(dst[:, P * t:P * t + P], h, w, start=(part == 0 and t == 0), stop=(part == 4),
                                   skip_group_check=True)
                if part == 4:
                    mm.then_inc(bank_full, 1)

            stream(main, dict(
                y3part=y3part, turnmax=turnmax, x1T=turn_tile("x1T"), q1=q1, k1=k1, v1=v1, wprod=wprod, wturn=wturn, o1T=o1T,
                o1y=outputs("o1y", lambda b: ONT_AFTER["o1T", b], [wo1_sb[:]]), x2T=turn_tile("x2T"), kst=kst, latv=latv,
                qabs=qabs, ropeA=ropeA, o2T=o2T,
                o2y=outputs("o2y", lambda b: ONT_AFTER["o2T", b], [wco_sb[:, 0, :], wco_sb[:, 1, :]]),
                x3T=turn_tile("x3T"), logit=logit, shared=shared, pairA=pairA, combT=combT, pairB=pairB, y3=y3))

        @block.scalar
        def _(act):
            def main(n, hh):
                if 0 <= n < NG:
                    h = HG * (n % G) + hh
                    u = n * UNITS + 5 * (hh // 2) + 2 * (hh % 2)
                    scale = (D1 if LAYER[n] == 1 else D2) ** -0.5
                    if hh == 0 and n >= 2:
                        act.wait_ge(pv, n - 1)
                    if n <= 1 and hh == 0:
                        act.wait_ge(consts_ready, WCO if n else CONSTS)
                    for k in range(2):
                        act.wait_ge(st_ready, u + k + 1)
                        act.activation(PA[:, h % 8, T * k:T * k + T], ps[:, ST0 + (u + k) % 3, :], ACT.Exp, scale=scale)\
                           .then_inc(exp_done, 1)
                    if hh % 2:
                        act.wait_ge(st_ready, u + 3)
                        act.activation(PC[:, (h % 8) // 2, :, :].rearrange("p a t -> p (a t)"), ps[:, ST0 + (u + 2) % 3, :],
                                       ACT.Exp, scale=scale).then_inc(exp_done, 1)
                if hh == 2 and 1 <= n <= NG:
                    act.wait_ge(pv, n)
                    if n >= 2:
                        act.wait_ge(o_turned, n - 1)
                    act.activation(OT[:], ps[:, BK_O, :], ACT.Copy).then_inc(ot_ready, 1)

            def full(u):
                act.wait_ge(bank_full, u + 1)
                return ps[:, bank_of(u), :]

            def turnmax(m, _):
                if m >= 2:
                    act.wait_ge(m_stacked[(m - 2) % G], 16 * ((m - 2) // G + 1))
                src = full(BANK0["turnmax", m, 0])
                if LAYER[m] == 1:
                    act.activation(MP[:, m % 2, 0:T // 2].bitcast(BF16), src[0:3 * HG, :].bitcast(BF16)[:, 0:T],
                                   ACT.Copy).then_inc(m_copied, 1)
                else:
                    act.activation(MP[0:2 * HG, m % 2, :], src[0:2 * HG, :], ACT.Copy).then_inc(m_copied, 1)
                act.wait_ge(m_copied, m + 1)
                act.sem_inc(bank_read[bank_of(BANK0["turnmax", m, 0])], 1)

            def take(stage, dst, ready, scale=1.0):
                def _(b, part):
                    src = full(BANK0[stage, b, part])
                    act.activation(dst, src, ACT.Copy, scale=scale).then_inc(ready, 1)
                    act.wait_ge(ready, b + 1)
                    act.sem_inc(bank_read[bank_of(BANK0[stage, b, part])], 1)
                return _

            def parts1(b, _):
                for k, (stage, parts) in enumerate((("q1", qp), ("k1", kp))):
                    j = JOB0[stage, b, 0]
                    act.wait_ge(whole_ready, j + 1)
                    if b and k == 0:
                        act.wait_ge(stored1, STORED1 * b)
                    act.activation(parts[:, 0, :], whole[:, j % 2, :], ACT.Copy).then_inc(high1, 1)

            def parts1b(b, _):
                for k, (stage, parts) in enumerate((("q1", qp), ("k1", kp))):
                    j = JOB0[stage, b, 0]
                    act.wait_ge(rest1, 2 * b + k + 1)
                    act.activation(parts[:, 1, :], terms[:, j % 2, 0, :], ACT.Copy).then_inc(middle1, 1)

            def v1(b, _):
                src = full(BANK0["v1", b, 0])
                if b:
                    act.wait_ge(v1_ready, b)
                act.activation(vc[:].rearrange("p t c -> p (t c)"), src, ACT.Copy).then_inc(vc_ready, 1)
                act.wait_ge(vc_ready, b + 1)
                act.sem_inc(bank_read[bank_of(BANK0["v1", b, 0])], 1)

            def turned(stage):
                def _(b, part):
                    for a in range(TAKES[stage][0]):
                        u = BANK0[stage, b, 0] + a
                        src = full(u)
                        act.activation(ONT[:, a, :], src, ACT.Copy).then_inc(ont_ready, 1)
                        act.wait_ge(ont_ready, ONT_AFTER[stage, b] - TAKES[stage][0] + a + 1)
                        act.sem_inc(bank_read[bank_of(u)], 1)
                return _

            def kst2(b, _):
                j = JOB0["kst", b, 0]
                act.wait_ge(whole_ready, j + 1)
                if b >= 2:
                    act.wait_ge(st_ready, UNITS * (first_group(2, b - 2) + G))
                if b == 0:
                    act.wait_ge(cleared, LAYER2)
                act.activation(K1[0:2 * DK2, b % 2, :], whole[0:2 * DK2, j % 2, :], ACT.Copy).then_inc(k_high, 1)

            def latv(b, _):
                src = full(BANK0["latv", b, 0])
                if b >= 2:
                    act.wait_ge(pv, first_group(2, b - 2) + G)
                if b == 0:
                    act.wait_ge(cleared, LAYER2)
                act.activation(V2[:, b % 2, :, 0:LAT], src[:, 0:NT * LAT].rearrange("p (t r) -> p t r", t=NT), ACT.Copy)\
                   .then_inc(v2_ready, 1)
                act.wait_ge(v2_ready, b + 1)
                act.sem_inc(bank_read[bank_of(BANK0["latv", b, 0])], 1)

            def slot_sent(c):
                if c >= 2:
                    act.wait_ge(q_stored[c % 2], 16 * (c // 2))

            def qabs(b, part):
                c = QTILE["qabs", b, part]
                src = full(BANK0["qabs", b, part])
                slot_sent(c)
                act.activation(QC[:, c % 2, 0, :], src, ACT.Copy).then_inc(q_high, 1)

            def ropeB(b, part):
                c, j = QTILE["ropeB", b, part], JOB0["ropeA", b, part]
                act.wait_ge(whole_ready, j + 1)
                slot_sent(c)
                act.activation(QC[:, c % 2, 0, :], whole[:, j % 2, :], ACT.Copy).then_inc(q_high, 1)

            def logit(b, _):
                act.wait_ge(gate_in, b + 1)
                act.activation(probs, key, ACT.Exp).then_inc(gate_exp, 1)

            def o1y(b, _):
                u = BANK0["o1y", b, 0]
                src = full(u)
                if b:
                    act.wait_ge(x1_ready, b)
                act.activation(y_b[:].rearrange("p t c -> p (t c)"), src, ACT.Copy).then_inc(y_ready, 1)
                act.wait_ge(y_ready, b + 1)
                act.sem_inc(bank_read[bank_of(u)], 1)

            def affine(dst, src, scales, adds):
                for t in range(NT):
                    last = act.activation(dst[:, t, :], src[:, t, :], ACT.Identity, scale=scales[:, t:t + 1],
                                          bias=adds[:, t:t + 1] if adds else 0.0)
                return last

            def tile_free(stage, b):
                j = TILE0[stage, b]
                if j:
                    act.wait_ge(bank_full, TURN_OF[j - 1] + 1)

            def ln1n(b, _):
                act.wait_ge(scale_ready, SCALE_OF["ln1n", b])
                tile_free("ln1n", b)
                affine(xn, xs[b], rstd[0], nmean[0]).then_inc(xn_ready, 1)

            def lna(b, _):
                act.wait_ge(scale_ready, SCALE_OF["lna", b])
                affine(y_b, y_b, rstd[1], nmean[1]).then_inc(y_normed, 1)

            def lnb(b, _):
                act.wait_ge(scale_ready, SCALE_OF["lnb", b] + 1)
                tile_free("lnb", b)
                affine(xn, xs[b], rstd_xn, nmean_xn).then_inc(xn_ready, 1)

            def lnb2(b, _):
                if b == 2:
                    act.wait_ge(stored1, STORED1 * B)
                affine(hres[b], xs[b], rstd[1], nmean[1]).then_inc(hres_ready, 1)

            def rms2(b, _):
                act.wait_ge(scale_ready, SCALE_OF["rms2", b])
                tile_free("rms2", b)
                affine(xn, hres[b], rstd[2], None).then_inc(xn_ready, 1)

            def fin(b, _):
                act.wait_ge(scale_ready, SCALE_OF["fin", b])
                affine(y_c, y_c, rstd[3], nmean[3]).then_inc(yc_normed, 1)

            def combT(b, _):
                src = full(BANK0["combT", b, 0])
                act.activation(CT[0:E, :], src[0:E, :], ACT.Copy).then_inc(ct_high, 1)

            def tanh(stage):
                def _(b, part):
                    k = 5 * b + (0 if stage == "shared" else part + 1)
                    rows = I if stage == "shared" else P
                    src = full(BANK0[stage, b, part])
                    if k >= 2:
                        act.wait_ge(gated, k - 1)
                    act.activation(sg[0:rows, k % 2, :], src[0:rows, :], ACT.Tanh, scale=0.5).then_inc(tanh_ready, 1)
                return _

            stream(main, dict(
                turnmax=turnmax, x1T=take("x1T", xT1, xT1_ready), v1=v1, parts1=parts1, parts1b=parts1b,
                o1T=turned("o1T"), o1y=o1y, ln1n=ln1n, lna=lna, lnb=lnb, lnb2=lnb2, rms2=rms2, fin=fin,
                x2T=take("x2T", xT2[:], xT2_ready, ln1w_sb[:]), kst2=kst2, latv=latv, qabs=qabs, ropeB=ropeB,
                o2T=turned("o2T"), x3T=take("x3T", xT3, xT3_ready, ln2w_sb[:]), logit=logit, combT=combT,
                shared=tanh("shared"), pairA=tanh("pairA")))

        @block.gpsimd
        def _(pool):
            steps = [0]

            def step(ins):
                steps[0] += 1
                ins.then_inc(pool_step, 1)
                pool.wait_ge(pool_step, steps[0])

            def power(chain):
                step(pool.tensor_tensor(rstd[chain][:], ve[chain][:], half[:], ALU.pow))

            def scale(stage, chain):
                def _(b, part):
                    pool.wait_ge(var_ready, NORM0[stage, b] + 1)
                    power(chain)
                    if stage == "o2y":
                        pool.sem_inc(scale_ready, 1)
                    else:
                        pool.tensor_tensor(nmean[chain][:], nmean[chain][:], rstd[chain][:], ALU.mult)\
                            .then_inc(scale_ready, 1)
                return _

            def lna(b, _):
                pool.wait_ge(y_normed, b + 1)
                pool.tensor_tensor(xs[b][:], xs[b][:], y_b[:], ALU.add).then_inc(x1_ready, 1)

            def lna2(b, _):
                scale("lna2", 1)(b, 0)
                k = SCALE_OF["lnb", b]
                pool.wait_ge(scale_ready, k)
                step(pool.tensor_tensor(sq[:], mv[1][:, :, 1], rstd[1][:], ALU.mult))
                step(pool.tensor_tensor(sq[:], sq[:], rstd[1][:], ALU.mult))
                step(pool.tensor_scalar(sq[:], sq[:], EPS, None, ALU.add))
                step(pool.tensor_tensor(sq[:], sq[:], half[:], ALU.pow))
                if b:
                    pool.wait_ge(xn_ready, TURN_ORDER["lnb", b - 1] + 1)
                pool.tensor_tensor(rstd_xn[:], rstd[1][:], sq[:], ALU.mult)
                pool.tensor_tensor(nmean_xn[:], nmean[1][:], sq[:], ALU.mult).then_inc(scale_ready, 1)

            def fin(b, _):
                pool.wait_ge(yc_normed, b + 1)
                pool.tensor_tensor(xs[b][:], xs[b][:], y_c, ALU.add).then_inc(out_ready, 1)

            def clear(ins, count):
                ins.then_inc(cleared, 1)
                pool.wait_ge(cleared, count)

            def clear2(_, part):
                if part < G:
                    clear(pool.memset(QS2[64:P, HG * part:HG * part + HG].bitcast(F32), 0.0), V1_ONES + 1 + part)
                else:
                    n = V1_ONES + G
                    clear(pool.memset(V2[:], 1.0), n + 1)
                    clear(pool.memset(K1[:].bitcast(F32), 0.0), n + 2)
                    clear(pool.memset(K2[:].bitcast(F32), 0.0), n + 3)
                    clear(pool.memset(CT.bitcast(F32), 0.0), n + 4)
                    clear(pool.memset(K1[MROW:P].bitcast(F32), 1.0), n + 5)

            def add_terms(stage):
                def _(b, part):
                    j = JOB0[stage, b, part]
                    pool.wait_ge(terms_ready, j + 1)
                    pool.tensor_tensor(whole[:, j % 2, :], terms[:, j % 2, 0, :], terms[:, j % 2, 1, :], ALU.add)\
                        .then_inc(whole_ready, 1)
                return _

            def parts1(b, _):
                for k, (stage, parts) in enumerate((("q1", qp), ("k1", kp))):
                    j = JOB0[stage, b, 0] % 2
                    pool.wait_ge(high1, 2 * b + k + 1)
                    pool.tensor_tensor(terms[:, j, 0, :], whole[:, j, :], parts[:, 0, :], ALU.subtract).then_inc(rest1, 1)

            def parts1b(b, _):
                for k, (stage, parts) in enumerate((("q1", qp), ("k1", kp))):
                    j = JOB0[stage, b, 0] % 2
                    pool.wait_ge(middle1, 2 * b + k + 1)
                    pool.tensor_tensor(parts[:, 2, :], terms[:, j, 0, :], parts[:, 1, :], ALU.subtract).then_inc(low1, 1)
                    pool.wait_ge(low1, 2 * b + k + 1)
                    pool.sem_inc(job_done[j], 1)

            def v1c(b, _):
                pool.wait_ge(vc_ready, b + 1)
                if b:
                    pool.wait_ge(pv, first_group(1, b - 1) + G)
                pool.tensor_copy(V1[:, :, :, 0:D1], vc[:].rearrange("p t (h d) -> p t h d", h=H)).then_inc(v1_ready, 1)

            def ropeB(b, part):
                c, j = QTILE["ropeB", b, part], JOB0["ropeA", b, part] % 2
                pool.wait_ge(q_high, c + 1)
                if c:
                    pool.wait_ge(q_low, c)
                pool.tensor_tensor(QC[:, c % 2, 1, :], whole[:, j, :], QC[:, c % 2, 0, :].bitcast(F32), ALU.subtract)\
                    .then_inc(q_low, 1)
                pool.wait_ge(q_low, c + 1)
                pool.sem_inc(job_done[j], 1)

            clear(pool.memset(half[:], -0.5), HALF)
            clear(pool.memset(QS1[64:P].bitcast(F32), 0.0), QUERY_ZEROS)
            clear(pool.memset(V1[:], 1.0), V1_ONES)
            stream(lambda n, hh: None, dict(
                clear2=clear2, ln1=scale("ln1", 0), q1=add_terms("q1"), k1=add_terms("k1"), parts1=parts1, parts1b=parts1b, v1c=v1c,
                o1y2=scale("o1y2", 1), lna=lna, lna2=lna2, kst=add_terms("kst"), ropeA=add_terms("ropeA"), ropeB=ropeB,
                o2y=scale("o2y", 2), y3=scale("y3", 3), fin=fin))

        @block.vector
        def _(dve):
            steps = [0]

            def step(ins):
                steps[0] += 1
                ins.then_inc(dve_step, 1)
                dve.wait_ge(dve_step, steps[0])

            def moments(src, chain):
                for t in range(NT):
                    last = dve.bn_stats(stats[:, t, :], src[:, t, :])
                step(last)
                for t in range(NT):
                    last = dve.bn_aggr(mv[chain][:, t, :], stats[:, t, :])
                step(last)

            def layer_var(chain):
                dve.tensor_scalar(nmean[chain][:], mv[chain][:, :, 0], -1.0, None, ALU.mult)
                dve.tensor_scalar(ve[chain][:], mv[chain][:, :, 1], EPS, None, ALU.add).then_inc(var_ready, 1)

            def full(u):
                dve.wait_ge(bank_full, u + 1)
                return ps[:, bank_of(u), :]

            def reduce_fill(n, k, src, dst):
                dve.wait_ge(score_fill, n * FILLS + k + 1)
                dve.tensor_reduce(dst, src, AX.X, ALU.max, negate=True).then_inc(fill_read, 1)

            def maximum(n, hh, i):
                h = HG * (n % G) + hh
                k = 2 * hh + hh // 2 + i
                bank = ps[:, (n * FILLS + k) % 2, :]
                src, dst = ((bank, NM[:, 3, h:h + 1]), (bank[:, 0:3 * P], NM[:, 2, h:h + 1]),
                            (bank.rearrange("p (a k) -> p a k", a=2), NM[:, 1, h - 1:h + 1]),
                            (bank.rearrange("p (a k) -> p a k", a=4), NM[:, 0, h - hh:h + 1]))[i]
                reduce_fill(n, k, src, dst)

            def split_max(n, i):
                m = NM[:, :, HG * (n % G):HG * (n % G) + HG]
                if i == 0:
                    dve.wait_ge(fill_read, (n + 1) * FILLS)
                    if n:
                        dve.wait_ge(bank_full, BANK0["turnmax", n - 1, 0] + 1)
                elif MSTEPS[n] + i < MSTEPS[n + 1]:
                    dve.wait_ge(m_step, MSTEPS[n] + i)
                if LAYER[n] == 1:
                    if i == 0:
                        dve.tensor_copy(MB[:, :, 0, :], m).then_inc(m_step, 1)
                    elif i == 1:
                        dve.tensor_tensor(MRest[:], m, MB[:, :, 0, :], ALU.subtract).then_inc(m_step, 1)
                    elif i == 2:
                        dve.tensor_copy(MB[:, :, 1, :], MRest[:]).then_inc(m_step, 1)
                    else:
                        dve.tensor_tensor(MB[:, :, 2, :], MRest[:], MB[:, :, 1, :], ALU.subtract).then_inc(m_step, 1)
                elif i == 0:
                    dve.tensor_copy(MF[:, :, 0, :], m).then_inc(m_step, 1)
                elif i == 1:
                    dve.tensor_tensor(MF[:, :, 1, :], m, MF[:, :, 0, :].bitcast(F32), ALU.subtract).then_inc(m_step, 1)

            def divide(n, i):
                w, on = (D1, ON1) if LAYER[n] == 1 else (LAT, ON2)
                bank = ps[:, BK_O, :].rearrange("p (t h d) -> p t h d", t=NT, h=HG)
                if i == 0:
                    dve.wait_ge(o_turned, n + 1)
                    dve.reciprocal(rec[:], bank[:, :, :, w]).then_inc(rec_ready, 1)
                    return
                dve.wait_ge(rec_ready, n + 1)
                if n % G == 0 and SEQ[n]:
                    stage = "o1T" if LAYER[n] == 1 else "o2T"
                    dve.wait_ge(bank_full, BANK0[stage, SEQ[n] - 1, 0] + TAKES[stage][0])
                if n == first_group(2, 0):
                    dve.wait_ge(stored1, STORED1 * B)
                dve.tensor_tensor(on[:].rearrange("p t (h d) -> p t h d", h=H)[:, :, HG * (n % G):HG * (n % G) + HG, :],
                                  bank[:, :, :, 0:w], rec[:].unsqueeze(3).to_broadcast([P, NT, HG, w]), ALU.mult)\
                   .then_inc(on_ready, 1)

            def main(n, hh):
                split, out = hh == 0 and 0 <= n + 1 < NG, hh == 0 and 2 <= n <= NG + 1
                for i in range(4):
                    if split:
                        split_max(n + 1, i)
                    if out and i < 2:
                        divide(n - 2, i)
                    if n + 2 < NG and i < 2 + hh % 2 + hh // 3:
                        maximum(n + 2, hh, i)

            def ln1(b, _):
                if b == 0:
                    dve.wait_ge(x0_loaded, 16)
                else:
                    dve.wait_ge(x_loaded, 16 * (B - 1))
                moments(xs[b], 0)
                layer_var(0)

            def consts(b, _):
                dve.wait_ge(loaded_first, ALL_FIRST)
                dve.tensor_copy(identb[:], ident_sb[:])
                dve.tensor_copy(maskb[:], masks_sb)
                dve.wait_ge(consts_ready, STACK_ZEROS)
                dve.memset(KS1[MROW:P].bitcast(F32), TWO_ONES).then_inc(consts_ready, 1)

            def rotation(stage, table):
                def _(b, part):
                    u, j = BANK0[stage, b, part], JOB0[stage, b, part]
                    if j >= 2:
                        dve.wait_ge(job_done[j % 2], j // 2)
                    for k in range(2):
                        src = full(u + k)
                        if u == BANK0["q1", 0, 0] and k == 0:
                            dve.wait_ge(loaded_qkv, ALL_QKV)
                        last = dve.tensor_tensor(terms[:, j % 2, k, :], src, table[:, k, :], ALU.mult)
                        last.then_inc(bank_read[bank_of(u + k)], 1)
                    dve.wait_ge(*was_read(u + 1))
                    dve.sem_inc(terms_ready, 1)
                return _

            def wprod(b, _):
                dve.wait_ge(loaded, ALL_LOADED)
                dve.tensor_copy(erow[:], erow_sb).then_inc(consts_ready, 1)
                u = BANK0["wprod", 0, 0]
                dve.tensor_copy(wabs_sb[:].rearrange("p a b -> p (a b)").rearrange("p (r h) -> p r h", h=H),
                                full(u)[:, 0:H * LAT].rearrange("p (h r) -> p r h", h=H)).then_inc(bank_read[bank_of(u)], 1)
                dve.tensor_copy(wco_t.rearrange("p a b -> p (a b)"), full(u + 1)[:, 0:H * LAT])\
                   .then_inc(bank_read[bank_of(u + 1)], 1)

            def wturn(b, _):
                u = BANK0["wturn", 0, 0]
                dve.tensor_copy(wco_sb[:].rearrange("p a b -> p (a b)"), full(u)[:, 0:2 * P]).then_inc(bank_read[bank_of(u)], 1)
                dve.wait_ge(*was_read(u))
                dve.sem_inc(consts_ready, 1)

            def o1y2(b, _):
                dve.wait_ge(y_ready, b + 1)
                if b:
                    dve.wait_ge(hres_ready, b)
                moments(y_b, 1)
                layer_var(1)

            def lna2(b, _):
                dve.wait_ge(x1_ready, b + 1)
                moments(xs[b], 1)
                layer_var(1)

            def kst2(b, _):
                j = JOB0["kst", b, 0]
                dve.wait_ge(k_high, b + 1)
                dve.tensor_tensor(K2[0:2 * DK2, b % 2, :], whole[0:2 * DK2, j % 2, :],
                                  K1[0:2 * DK2, b % 2, :].bitcast(F32), ALU.subtract).then_inc(k_low, 1)
                dve.wait_ge(k_low, b + 1)
                dve.sem_inc(job_done[j % 2], 1)

            def qabs(b, part):
                u, c = BANK0["qabs", b, part], QTILE["qabs", b, part]
                dve.wait_ge(q_high, c + 1)
                if c:
                    dve.wait_ge(q_low, c)
                dve.tensor_tensor(QC[:, c % 2, 1, :], full(u), QC[:, c % 2, 0, :].bitcast(F32), ALU.subtract)\
                   .then_inc(q_low, 1)
                dve.wait_ge(q_low, c + 1)
                dve.sem_inc(bank_read[bank_of(u)], 1)

            def o2y(b, _):
                u = BANK0["o2y", b, 0]
                dve.wait_ge(hres_ready, b + 1)
                dve.tensor_tensor(hres[b], hres[b], full(u).rearrange("p (t c) -> p t c", t=NT), ALU.add)\
                   .then_inc(bank_read[bank_of(u)], 1)
                dve.wait_ge(*was_read(u))
                moments(hres[b], 2)
                step(dve.tensor_tensor(sums[:], mv[2][:, :, 0], mv[2][:, :, 0], ALU.mult))
                dve.scalar_tensor_tensor(out=ve[2][:], in0=sums[:], scalar=EPS, in1=mv[2][:, :, 1], op0=ALU.add,
                                         op1=ALU.add).then_inc(var_ready, 1)

            def wide(v):
                return v.unsqueeze(2).to_broadcast([P, NT, E])

            def logit(b, _):
                u = BANK0["logit", b, 0]
                dve.tensor_tensor(lg, full(u)[:, 0:NT * E].rearrange("p (t e) -> p t e", t=NT),
                                  gbias_sb[:].unsqueeze(1).to_broadcast([P, NT, E]), ALU.add).then_inc(bank_read[bank_of(u)], 1)
                dve.wait_ge(*was_read(u))
                step(dve.tensor_reduce(mx, lg, AX.X, ALU.max))
                dve.tensor_tensor(key, lg, wide(mx), ALU.subtract).then_inc(gate_in, 1)

            def choose(prob, chosen):
                step(dve.tensor_reduce(mx, prob, AX.X, ALU.max))
                step(dve.tensor_tensor(eq, prob, wide(mx), ALU.is_ge))
                step(dve.tensor_tensor(key, eq, rank_sb[:], ALU.mult))
                step(dve.tensor_reduce(mx, key, AX.X, ALU.max))
                step(dve.tensor_tensor(chosen, key, wide(mx), ALU.is_equal))

            def route(b, _):
                dve.wait_ge(gate_exp, b + 1)
                choose(probs, s1)
                step(dve.scalar_tensor_tensor(out=lg, in0=s1, scalar=-2.0, in1=probs, op0=ALU.mult, op1=ALU.add))

            def route2(b, _):
                choose(lg, s2)
                step(dve.tensor_tensor(s1, s1, s2, ALU.add))
                step(dve.tensor_tensor(s2, probs, s1, ALU.mult))
                step(dve.tensor_reduce(mx, s2, AX.X, ALU.add))
                step(dve.reciprocal(sums[:], mx))
                dve.tensor_tensor(comb, s2, wide(sums[:]), ALU.mult).then_inc(comb_ready, 1)

            def combT(b, _):
                u = BANK0["combT", b, 0]
                dve.wait_ge(ct_high, b + 1)
                dve.tensor_tensor(CT[32:32 + E, :], full(u)[0:E, :], CT[0:E, :].bitcast(F32), ALU.subtract)\
                   .then_inc(ct_low, 1)
                dve.wait_ge(ct_low, b + 1)
                dve.sem_inc(bank_read[bank_of(u)], 1)

            def gate(stage):
                def _(b, part):
                    u = BANK0[stage, b, part]
                    k = 5 * b + (0 if stage == "shared" else part + 1)
                    rows, row = (I, 4) if stage == "shared" else (P, part)
                    dve.wait_ge(tanh_ready, k + 1)
                    if GATED_BEFORE[stage, b, part] is not None:
                        dve.wait_ge(*was_read(GATED_BEFORE[stage, b, part]))
                    dve.scalar_tensor_tensor(out=gs[0:rows, :], in0=sg[0:rows, k % 2, :], scalar=1.0,
                                             in1=full(u)[0:rows, :], op0=ALU.add, op1=ALU.mult).then_inc(gated, 1)
                    dve.wait_ge(gated, k + 1)
                    dve.sem_inc(bank_read[bank_of(u)], 1)
                    last = dve.scalar_tensor_tensor(out=HH[0:rows, row, :], in0=gs[0:rows, :], scalar=0.5,
                                                    in1=full(u + 1)[0:rows, :], op0=ALU.mult, op1=ALU.mult)
                    last.then_inc(bank_read[bank_of(u + 1)], 1)
                    if stage == "shared":
                        dve.wait_ge(*was_read(u + 1))
                        dve.sem_inc(h_ready, 1)
                return _

            def pairB(b, part):
                u = BANK0["pairB", b, part]
                v = BANK0["pairA", b, part] + 1
                dve.wait_ge(*was_read(v))
                dve.tensor_tensor(HH[:, part, :], HH[:, part, :], full(u), ALU.mult).then_inc(h_ready, 1)
                dve.wait_ge(h_ready, 5 * b + part + 2)
                dve.sem_inc(bank_read[bank_of(u)], 1)

            def y3(b, _):
                u = BANK0["y3", b, 0]
                if b:
                    dve.wait_ge(out_ready, b)
                dve.tensor_tensor(y_c, hres[b], full(u).rearrange("p (t c) -> p t c", t=NT), ALU.add)\
                   .then_inc(bank_read[bank_of(u)], 1)
                dve.wait_ge(*was_read(u))
                moments(y_c, 3)
                layer_var(3)

            dve.memset(KS1[64:P].bitcast(F32), 0.0).then_inc(consts_ready, 1)
            stream(main, dict(
                ln1=ln1, consts=consts, q1=rotation("q1", rope1_sb), k1=rotation("k1", rope1_sb), wprod=wprod, wturn=wturn,
                o1y2=o1y2, lna2=lna2, kst=rotation("kst", ropek_sb), kst2=kst2, qabs=qabs,
                ropeA=rotation("ropeA", ropeq_sb), o2y=o2y, logit=logit, route=route, route2=route2, combT=combT,
                shared=gate("shared"), pairA=gate("pairA"), pairB=pairB, y3=y3))


def _constants(np):
    ident = np.eye(P, dtype=np.float32)
    k_above_q = np.triu(np.full((P, P), NEG, np.float32), 1)
    masks = np.stack([k_above_q, k_above_q.T], axis=1)
    t = np.arange(T, dtype=np.float32)[:, None]

    def table(freqs):
        ang = (t * freqs[None, :].astype(np.float32)).astype(np.float32).astype(np.float64)
        return np.cos(ang).astype(np.float32).T, np.sin(ang).astype(np.float32).T

    half1 = D1 // 2
    cos1, sin1 = table(1.0 / np.float32(10000.0) ** (np.arange(half1, dtype=np.float32) / np.float32(half1)))
    d = np.arange(D1)
    rope1 = np.stack([cos1[d % half1], np.where(d < half1, -1, 1)[:, None].astype(np.float32) * sin1[d % half1]], axis=1)
    rope1 = np.repeat(rope1, H, axis=0)
    cos2, sin2 = table(1.0 / np.float32(100000.0) ** (np.arange(0, ROPE, 2, dtype=np.float32) / np.float32(ROPE)))
    d = np.arange(ROPE)
    rope2 = np.stack([cos2[d // 2], np.where(d % 2 == 0, -1, 1)[:, None].astype(np.float32) * sin2[d // 2]], axis=1)
    ropeq = np.tile(rope2, (HG, 1, 1))
    plain = np.zeros((LAT, 2, T), np.float32)
    plain[:, 0] = 1
    ropek = np.concatenate([plain, rope2, plain, rope2, np.zeros((P - 2 * DK2, 2, T), np.float32)])
    rank = np.broadcast_to(np.arange(E, 0, -1, dtype=np.float32), (P, NT, E))
    rows = np.zeros((P, E // 2, P), np.float32)
    for e in range(E):
        for r in (e, 32 + e):
            rows[r, e // 2, I * (e % 2):I * (e % 2) + I] = 1
    return dict(ident=ident, masks=masks, rope1=rope1, ropek=ropek, ropeq=ropeq, rank=rank, expert_rows=rows)


def _layouts(np, w):
    a = {k: np.asarray(v) for k, v in w.items()}
    d, h = np.meshgrid(np.arange(D1), np.arange(H), indexing="ij")
    plain1, turned1 = (h * D1 + d).ravel(), (h * D1 + (d + D1 // 2) % D1).ravel()
    wq, wk = a["L0_attn_Wq"], a["L0_attn_Wk"]
    wqkv = np.stack([wq[plain1].T, wq[turned1].T, wk[plain1].T, wk[turned1].T, a["L0_attn_Wv"].T], axis=1)
    kva = a["L0_ffn_Wkva"]
    zeros = np.zeros((C, P - 2 * DK2), kva.dtype)
    turned = np.arange(ROPE) ^ 1
    kturned = np.concatenate([np.zeros((C, LAT), kva.dtype), kva[:, LAT:][:, turned]], axis=1)
    wkva = np.stack([np.concatenate([kva, kva, zeros], axis=1), np.concatenate([kturned, kturned, zeros], axis=1)], axis=1)
    wq2 = a["L0_ffn_Wq"].reshape(C, H, D2)
    rope = wq2[:, :, NOPE:]
    wq_rope = np.stack([rope.reshape(C, G, P), rope[:, :, turned].reshape(C, G, P)], axis=1)
    wkvb = a["L0_ffn_Wkvb"].reshape(LAT, H, NOPE).transpose(2, 1, 0)
    wo2 = a["L0_ffn_Wo"].reshape(H, D2, C)[:, :NOPE].transpose(1, 0, 2)
    wg, wu = (a[k].reshape(E // 2, 2, C, I).transpose(2, 0, 1, 3).reshape(C, E // 2, P) for k in ("L0_ffn_Wg", "L0_ffn_Wu"))
    return dict(
        x=a["L0_attn_x"].reshape(B * T, C), wqkv=wqkv, wo1=a["L0_attn_Wo"].T, wkva=wkva,
        wq_nope=wq2[:, :, :NOPE].transpose(2, 1, 0), wq_rope=wq_rope, wkvb=wkvb, wo2=wo2,
        ln1w=a["L0_ffn_w_ln1"].reshape(C, 1), ln2w=a["L0_ffn_w_ln2"].reshape(C, 1), wgate=a["L0_ffn_Wgate"],
        gbias=np.broadcast_to(a["L0_ffn_expert_bias"], (P, E)), wgu=np.stack([wg, wu], axis=2),
        wgu_s=np.stack([a["L0_ffn_sWg"][0], a["L0_ffn_sWu"][0]], axis=1),
        wd=a["L0_ffn_Wd"].reshape(E // 2, P, C).transpose(1, 0, 2), wd_s=a["L0_ffn_sWd"][0])


def kernel(**inputs):
    import numpy as np
    from concourse import bacc
    from concourse.bass_utils import run_bass_kernel_spmd

    nc = bacc.Bacc("TRN2", target_bir_lowering=False, num_devices=1)
    arrays = {k: np.ascontiguousarray(v) for k, v in {**_layouts(np, inputs), **_constants(np)}.items()}
    aps = {k: nc.dram_tensor(f"in_{k}", v.shape, F32, kind="ExternalInput").ap() for k, v in arrays.items()}
    out = nc.dram_tensor("out_x", (B * T, C), F32, kind="ExternalOutput").ap()
    block_program(nc, out=out, **aps)
    r = run_bass_kernel_spmd(nc, [{f"in_{k}": v for k, v in arrays.items()}], core_ids=[0])
    return r.results[0]["out_x"].reshape(B, T, C)
```
